# Optimizing a Trainium2 kernel written in Bass

```python
import numpy as np
import jax
import jax.numpy as jnp

def _softmax(x, axis=-1):
    return jax.nn.softmax(x, axis=axis)

def _gelu(x):
    return jax.nn.gelu(x, approximate=True)

def _silu(x):
    return jax.nn.silu(x)

def _sigmoid(x):
    return jax.nn.sigmoid(x)

def _layernorm(x, axis=-1, eps=1e-05):
    m = jnp.mean(x, axis=axis, keepdims=True)
    v = jnp.var(x, axis=axis, keepdims=True)
    return (x - m) / jnp.sqrt(v + eps)

def _scatter_add(tgt, idx, src, axis=0):
    return tgt.at[idx].add(src)

def _segment_sum(src, seg, n):
    return jax.ops.segment_sum(src, seg, n)
kernel_name = 'mk_lm_tower_d1_tok_ids256_r4_82b792'

def setup_inputs(seed: int=0):
    np.random.seed(seed)
    _w = jnp.asarray

    def _rec_inputs():
        import jax
        import jax.numpy as jnp
        _rk = jax.random.key(seed)
        x = jax.random.randint(jax.random.fold_in(_rk, 1), (32, 512), 0, 50257, jnp.int32)
        return x
    x = _rec_inputs()

    def _L0_tok_setup():
        import jax, jax.numpy as jnp
        import numpy as np
        VOCAB = 50257
        DIM = 64

        def _positional_table(seq_len, dim, dtype=jnp.float32):
            pos = jnp.arange(seq_len, dtype=dtype)[:, None]
            d = jnp.arange(dim)
            exponent = (d - d % 2).astype(dtype) / dim
            inv_freq = jnp.power(jnp.asarray(10000.0, dtype), -exponent)
            angle = pos * inv_freq
            return jnp.where(d % 2 == 0, jnp.sin(angle), jnp.cos(angle))
        key = jax.random.key(seed)
        k1, k2 = jax.random.split(key)
        x = jax.random.randint(k1, (32, 1024), 0, VOCAB)
        W = jax.random.normal(k2, (VOCAB, DIM), dtype=jnp.float32)
        return {'x': x, 'W': W}
    _L0_tok_all = _L0_tok_setup()
    _L0_tok_in = {k: v for k, v in _L0_tok_all.items() if k in ('W',)}
    del _L0_tok_all

    def _L0_attn_setup():
        import jax, jax.numpy as jnp
        import numpy as np
        B, L, DIM = (8, 4096, 64)
        WINDOW, SHIFT, HEADS = (128, 64, 8)
        key = jax.random.key(seed)
        k0, k1, k2, k3 = jax.random.split(key, 4)
        x = jax.random.normal(k0, (B, L, DIM), dtype=jnp.float32)
        qkv_weight = jax.random.normal(k1, (3 * DIM, DIM), dtype=jnp.float32) * 0.02
        qkv_bias = jnp.zeros((3 * DIM,), dtype=jnp.float32)
        proj_weight = jax.random.normal(k2, (DIM, DIM), dtype=jnp.float32) * 0.02
        proj_bias = jnp.zeros((DIM,), dtype=jnp.float32)
        bias_table = jax.random.normal(k3, (2 * WINDOW - 1, HEADS), dtype=jnp.float32) * 0.02
        return {'x': x, 'qkv_weight': qkv_weight, 'qkv_bias': qkv_bias, 'proj_weight': proj_weight, 'proj_bias': proj_bias, 'bias_table': bias_table}
    _L0_attn_all = _L0_attn_setup()
    _L0_attn_in = {k: v for k, v in _L0_attn_all.items() if k in ('qkv_weight', 'qkv_bias', 'proj_weight', 'proj_bias', 'bias_table')}
    del _L0_attn_all

    def _L0_ffn_setup():
        import jax, jax.numpy as jnp
        import numpy as np
        B, N, D = (16, 1024, 64)
        NUM_EXPERTS, TOP_K, HEADS = (4, 2, 4)
        N_EDGES = 262144
        LN_EPS = 1e-05

        def _layernorm(x, g, b):
            mu = x.mean(-1, keepdims=True)
            var = ((x - mu) ** 2).mean(-1, keepdims=True)
            return (x - mu) * jax.lax.rsqrt(var + LN_EPS) * g + b

        def _forward(x, edge_index, W_gat, att_src, att_dst, b_gat, ln_gamma, ln_beta, W1, b1, W2, b2):
            Bc, Nc, Dc = x.shape
            M = Bc * Nc
            x_flat = x.reshape(M, Dc)
            h = (x_flat @ W_gat).reshape(M, HEADS, NUM_EXPERTS)
            loops = jnp.arange(M, dtype=edge_index.dtype)
            src = jnp.concatenate([edge_index[0], loops])
            dst = jnp.concatenate([edge_index[1], loops])
            a_src = (h * att_src).sum(-1)
            a_dst = (h * att_dst).sum(-1)
            e = jax.nn.leaky_relu(a_src[src] + a_dst[dst], negative_slope=0.2)
            e_max = jax.ops.segment_max(e, dst, num_segments=M)
            ee = jnp.exp(e - e_max[dst])
            denom = jax.ops.segment_sum(ee, dst, num_segments=M)
            alpha = ee / (denom[dst] + 1e-16)
            msg = h[src] * alpha[:, :, None]
            agg = jax.ops.segment_sum(msg, dst, num_segments=M).reshape(M, HEADS * NUM_EXPERTS) + b_gat
            scores = _layernorm(agg, ln_gamma, ln_beta).reshape(M, HEADS, NUM_EXPERTS).mean(1)
            scores = scores.reshape(Bc, Nc, NUM_EXPERTS)
            topk_s, topk_i = jax.lax.top_k(scores, TOP_K)
            w = jax.nn.softmax(topk_s, axis=-1)
            out = jnp.zeros_like(x)
            for ei in range(NUM_EXPERTS):
                g = jnp.where(topk_i == ei, w, 0.0).sum(-1)
                hh = jax.nn.gelu(x @ W1[ei] + b1[ei], approximate=False)
                out = out + g[..., None] * (hh @ W2[ei] + b2[ei])
            return out
        key = jax.random.key(seed)
        ks = jax.random.split(key, 8)
        s = 0.05
        return {'x': jax.random.normal(ks[0], (B, N, D), jnp.float32), 'W_gat': jax.random.normal(ks[1], (D, HEADS * NUM_EXPERTS), jnp.float32) * s, 'att_src': jax.random.normal(ks[2], (HEADS, NUM_EXPERTS), jnp.float32) * s, 'att_dst': jax.random.normal(ks[3], (HEADS, NUM_EXPERTS), jnp.float32) * s, 'b_gat': jnp.zeros((HEADS * NUM_EXPERTS,), jnp.float32), 'ln_gamma': jnp.ones((HEADS * NUM_EXPERTS,), jnp.float32), 'ln_beta': jnp.zeros((HEADS * NUM_EXPERTS,), jnp.float32), 'W1': jax.random.normal(ks[4], (NUM_EXPERTS, D, 2 * D), jnp.float32) * s, 'b1': jnp.zeros((NUM_EXPERTS, 2 * D), jnp.float32), 'W2': jax.random.normal(ks[5], (NUM_EXPERTS, 2 * D, D), jnp.float32) * s, 'b2': jnp.zeros((NUM_EXPERTS, D), jnp.float32), 'edge_index': jax.random.randint(ks[6], (2, N_EDGES), 0, B * N, jnp.int32)}
    _L0_ffn_all = _L0_ffn_setup()
    _L0_ffn_in = {k: v for k, v in _L0_ffn_all.items() if k in ('W_gat', 'att_src', 'att_dst', 'b_gat', 'ln_gamma', 'ln_beta', 'W1', 'b1', 'W2', 'b2', 'edge_index')}
    del _L0_ffn_all
    return {'x': x, 'L0_tok_W': _L0_tok_in['W'], 'L0_attn_qkv_weight': _L0_attn_in['qkv_weight'], 'L0_attn_qkv_bias': _L0_attn_in['qkv_bias'], 'L0_attn_proj_weight': _L0_attn_in['proj_weight'], 'L0_attn_proj_bias': _L0_attn_in['proj_bias'], 'L0_attn_bias_table': _L0_attn_in['bias_table'], 'L0_ffn_W_gat': _L0_ffn_in['W_gat'], 'L0_ffn_att_src': _L0_ffn_in['att_src'], 'L0_ffn_att_dst': _L0_ffn_in['att_dst'], 'L0_ffn_b_gat': _L0_ffn_in['b_gat'], 'L0_ffn_ln_gamma': _L0_ffn_in['ln_gamma'], 'L0_ffn_ln_beta': _L0_ffn_in['ln_beta'], 'L0_ffn_W1': _L0_ffn_in['W1'], 'L0_ffn_b1': _L0_ffn_in['b1'], 'L0_ffn_W2': _L0_ffn_in['W2'], 'L0_ffn_b2': _L0_ffn_in['b2'], 'L0_ffn_edge_index': _L0_ffn_in['edge_index']}

def reference(x, L0_tok_W, L0_attn_qkv_weight, L0_attn_qkv_bias, L0_attn_proj_weight, L0_attn_proj_bias, L0_attn_bias_table, L0_ffn_W_gat, L0_ffn_att_src, L0_ffn_att_dst, L0_ffn_b_gat, L0_ffn_ln_gamma, L0_ffn_ln_beta, L0_ffn_W1, L0_ffn_b1, L0_ffn_W2, L0_ffn_b2, L0_ffn_edge_index):
    import jax
    import jax.numpy as jnp

    def _L0_tok_ref(x, W):
        import jax, jax.numpy as jnp
        import numpy as np
        VOCAB = 50257
        DIM = 64

        def _positional_table(seq_len, dim, dtype=jnp.float32):
            pos = jnp.arange(seq_len, dtype=dtype)[:, None]
            d = jnp.arange(dim)
            exponent = (d - d % 2).astype(dtype) / dim
            inv_freq = jnp.power(jnp.asarray(10000.0, dtype), -exponent)
            angle = pos * inv_freq
            return jnp.where(d % 2 == 0, jnp.sin(angle), jnp.cos(angle))
        seq_len = x.shape[1]
        pe = _positional_table(seq_len, W.shape[1], W.dtype)
        return W[x] + pe[None, :, :]

    def _L0_attn_ref(x, qkv_weight, qkv_bias, proj_weight, proj_bias, bias_table):
        import jax, jax.numpy as jnp
        import numpy as np
        B, L, DIM = (8, 4096, 64)
        WINDOW, SHIFT, HEADS = (128, 64, 8)
        Bb, Ll, C = x.shape
        hd = C // HEADS
        pad = (WINDOW - Ll % WINDOW) % WINDOW
        xp = jnp.pad(x, ((0, 0), (0, pad), (0, 0)))
        pad_L = Ll + pad
        shift = 0 if WINDOW >= pad_L else SHIFT
        if shift > 0:
            xp = jnp.roll(xp, -shift, axis=1)
        nW = pad_L // WINDOW
        xw = xp.reshape(Bb * nW, WINDOW, C)
        qkv = xw @ qkv_weight.T + qkv_bias
        qkv = qkv.reshape(Bb * nW, WINDOW, 3, HEADS, hd).transpose(2, 0, 3, 1, 4)
        q, k, v = (qkv[0], qkv[1], qkv[2])
        scale = hd ** (-0.5)
        attn = jnp.einsum('whqd,whkd->whqk', q * scale, k)
        coords = jnp.arange(WINDOW)
        rel_idx = coords[:, None] - coords[None, :] + WINDOW - 1
        rpb = bias_table[rel_idx]
        attn = attn + jnp.transpose(rpb, (2, 0, 1))[None]
        if shift > 0:
            region = jnp.zeros((pad_L,), dtype=x.dtype)
            region = region.at[pad_L - WINDOW:pad_L - shift].set(1.0)
            region = region.at[pad_L - shift:].set(2.0)
            region = region.reshape(nW, WINDOW)
            mask = jnp.where(region[:, None, :] != region[:, :, None], -100.0, 0.0).astype(x.dtype)
            attn = attn.reshape(Bb, nW, HEADS, WINDOW, WINDOW) + mask[None, :, None]
            attn = attn.reshape(Bb * nW, HEADS, WINDOW, WINDOW)
        attn = jax.nn.softmax(attn, axis=-1)
        out = jnp.einsum('whqk,whkd->wqhd', attn, v).reshape(Bb * nW, WINDOW, C)
        out = out @ proj_weight.T + proj_bias
        out = out.reshape(Bb, pad_L, C)
        if shift > 0:
            out = jnp.roll(out, shift, axis=1)
        return out[:, :Ll, :]

    def _L0_ffn_ref(x, W_gat, att_src, att_dst, b_gat, ln_gamma, ln_beta, W1, b1, W2, b2, edge_index):
        import jax, jax.numpy as jnp
        import numpy as np
        B, N, D = (16, 1024, 64)
        NUM_EXPERTS, TOP_K, HEADS = (4, 2, 4)
        N_EDGES = 262144
        LN_EPS = 1e-05

        def _layernorm(x, g, b):
            mu = x.mean(-1, keepdims=True)
            var = ((x - mu) ** 2).mean(-1, keepdims=True)
            return (x - mu) * jax.lax.rsqrt(var + LN_EPS) * g + b

        def _forward(x, edge_index, W_gat, att_src, att_dst, b_gat, ln_gamma, ln_beta, W1, b1, W2, b2):
            Bc, Nc, Dc = x.shape
            M = Bc * Nc
            x_flat = x.reshape(M, Dc)
            h = (x_flat @ W_gat).reshape(M, HEADS, NUM_EXPERTS)
            loops = jnp.arange(M, dtype=edge_index.dtype)
            src = jnp.concatenate([edge_index[0], loops])
            dst = jnp.concatenate([edge_index[1], loops])
            a_src = (h * att_src).sum(-1)
            a_dst = (h * att_dst).sum(-1)
            e = jax.nn.leaky_relu(a_src[src] + a_dst[dst], negative_slope=0.2)
            e_max = jax.ops.segment_max(e, dst, num_segments=M)
            ee = jnp.exp(e - e_max[dst])
            denom = jax.ops.segment_sum(ee, dst, num_segments=M)
            alpha = ee / (denom[dst] + 1e-16)
            msg = h[src] * alpha[:, :, None]
            agg = jax.ops.segment_sum(msg, dst, num_segments=M).reshape(M, HEADS * NUM_EXPERTS) + b_gat
            scores = _layernorm(agg, ln_gamma, ln_beta).reshape(M, HEADS, NUM_EXPERTS).mean(1)
            scores = scores.reshape(Bc, Nc, NUM_EXPERTS)
            topk_s, topk_i = jax.lax.top_k(scores, TOP_K)
            w = jax.nn.softmax(topk_s, axis=-1)
            out = jnp.zeros_like(x)
            for ei in range(NUM_EXPERTS):
                g = jnp.where(topk_i == ei, w, 0.0).sum(-1)
                hh = jax.nn.gelu(x @ W1[ei] + b1[ei], approximate=False)
                out = out + g[..., None] * (hh @ W2[ei] + b2[ei])
            return out
        return _forward(x, edge_index, W_gat, att_src, att_dst, b_gat, ln_gamma, ln_beta, W1, b1, W2, b2)
    h = _L0_tok_ref(x, L0_tok_W)
    h = h + _L0_attn_ref(_layernorm(h, axis=-1), L0_attn_qkv_weight, L0_attn_qkv_bias, L0_attn_proj_weight, L0_attn_proj_bias, L0_attn_bias_table)
    h = h + _L0_ffn_ref(_layernorm(h, axis=-1), L0_ffn_W_gat, L0_ffn_att_src, L0_ffn_att_dst, L0_ffn_b_gat, L0_ffn_ln_gamma, L0_ffn_ln_beta, L0_ffn_W1, L0_ffn_b1, L0_ffn_W2, L0_ffn_b2, L0_ffn_edge_index)
    return h

_drawn_inputs = setup_inputs


def setup_inputs(seed=0):
    import zlib

    import numpy as np

    out = dict(_drawn_inputs(seed))
    spreads = {'L0_attn_qkv_bias': (0.0, 0.395),
     'L0_attn_proj_bias': (0.0, 0.1),
     'L0_ffn_b_gat': (0.0, 0.403),
     'L0_ffn_ln_gamma': (1.0, 0.6),
     'L0_ffn_ln_beta': (0.0, 2.0),
     'L0_ffn_b1': (0.0, 0.449),
     'L0_ffn_b2': (0.0, 0.1)}
    factors = {'L0_attn_qkv_weight': 6.0,
     'L0_attn_proj_weight': 2.739,
     'L0_attn_bias_table': 64.0,
     'L0_ffn_att_src': 119.502,
     'L0_ffn_att_dst': 200.0,
     'L0_ffn_W_gat': 2.821}
    for name, (base, spread) in spreads.items():
        noise = np.random.default_rng([zlib.crc32(name.encode()), seed]).standard_normal(out[name].shape)
        drawn = base * np.exp(spread * noise) if base else spread * noise
        out[name] = jnp.asarray(drawn.astype(out[name].dtype))
    for name, factor in factors.items():
        out[name] = (out[name] * factor).astype(out[name].dtype)
    return out
```

```python
import concourse.bass as bass
from concourse import mybir
from contextlib import ExitStack
import numpy as np


def lm_tower_kernel(nc, x, emb, qkv_w, proj_w, bias_rev, att, w_gat, gat_rows, w1, w2, b2_rows, edges, pos_enc, consts, out):
    f32, bf16, i32 = mybir.dt.float32, mybir.dt.bfloat16, mybir.dt.int32
    ALU, ACT, AX = mybir.AluOpType, mybir.ActivationFunctionType, mybir.AxisListType
    P = 128
    SEQS, SEQ = x.shape
    D = emb.shape[1]
    WIN = SEQ // P
    SHIFT = P // 2
    NH, HD = 8, 8
    NB = SEQS * WIN
    NE = edges.shape[1]
    NT = NE // P
    NX = 4
    HID = 2 * D
    CH = 4
    CE = CH * P
    NCH = NE // CE + NB
    LC = (NCH + 4) * CH
    NS = 8
    TW = NT // NB
    FW = 32
    BIG = float(2 ** 20)
    EMPTY = P << 14
    EPS = 1e-5

    ctx = ExitStack()
    with ctx:
        def sb(name, shape, dt=f32):
            return ctx.enter_context(nc.sbuf_tensor(name, shape, dt))

        def sem(name):
            return ctx.enter_context(nc.semaphore(name))

        edge_list = nc.dram_tensor("edge_list", [P * LC, 1], i32, kind="Internal").ap()
        node_rows = nc.dram_tensor("node_rows", [NB * P, FW], f32, kind="Internal").ap()
        expert_out = nc.dram_tensor("expert_out", [NB * P, NX * D], f32, kind="Internal").ap()

        h_sb = sb("h_sb", [P, NB, D])
        rows_sb = sb("rows_sb", [P, NB, FW])
        big_i = sb("big_i", [P, LC], i32)
        pay_i = sb("pay_i", [P, LC], i32)
        big_f = sb("big_f", [P, LC])
        iota_b = sb("iota_b", [P, P], bf16)
        cst = sb("cst", [P, 5 * P + LC // CH])
        ident, iota_f, upper, ones, flip = (cst[:, k * P:(k + 1) * P] for k in range(5))
        chunk_iota = cst[:, 5 * P:]
        before_b = sb("before_b", [P, P], bf16)
        notbefore_b = sb("notbefore_b", [P, P], bf16)
        ones_b = sb("ones_b", [P, P], bf16)
        zeros_b = sb("zeros_b", [P, CE], bf16)
        bigi_b = sb("bigi_b", [P, P], bf16)
        sel_b = sb("sel_b", [8, NX, P], bf16)
        pe_sb = sb("pe_sb", [P, WIN, D])
        rb_sb = sb("rb_sb", [P, 2, NH, P])
        hmask = sb("hmask", [D, NH])
        qkvw_sb = sb("qkvw_sb", [D + 1, 3 * D])
        projw_sb = sb("projw_sb", [D + 1, D])
        w1_sb = sb("w1_sb", [D + 1, NX, HID])
        w2_sb = sb("w2_sb", [HID, NX, D])
        b2_sb = sb("b2_sb", [P, NX, D])
        wg_sb = sb("wg_sb", [D, 16])
        att_sb = sb("att_sb", [P, 2, 16])
        gr_sb = sb("gr_sb", [P, 3, 16])
        xi = sb("xi", [SEQS, SEQ], i32)
        xf = sb("xf", [SEQS, SEQ])
        tok_i = sb("tok_i", [P, WIN, SEQS], i32)
        tok_now = sb("tok_now", [P, WIN], i32)
        emb_now = sb("emb_now", [P, WIN, D])
        oh = sb("oh", [P, 2, CH, P], bf16)
        junk = sb("junk", [P, CH, P])
        pos_f = sb("pos_f", [P, 2, NS])
        pos_i = sb("pos_i", [P, 2, NS], i32)
        lo_i = sb("lo_i", [P, 2, NS], i32)
        addr_i = sb("addr_i", [P, 2, NS], i32)
        pay_now = sb("pay_now", [P, 2, NS], i32)
        hist = sb("hist", [P, NS, P])
        rowa = sb("rowa", [P, P])
        rowi = sb("rowi", [P, P], i32)
        rowb = sb("rowb", [P, P])
        colv = sb("colv", [P, 4])
        cmp_b = sb("cmp_b", [P, LC // CH], bf16)
        block_of = sb("block_of", [P, LC // CH], i32)
        stat = sb("stat", [P, 6])
        mv = sb("mv", [P, 2])
        rstd = sb("rstd", [P, 1])
        xn = sb("xn", [P, D])
        xT = sb("xT", [D + 1, P])
        kT = sb("kT", [D, P])
        qm = sb("qm", [D, NH, P])
        v1 = sb("v1", [P, NH, HD + 1])
        nmax = sb("nmax", [P, NH])
        pr = sb("pr", [P, NH, P])
        prT = sb("prT", [P, NH, P])
        rden = sb("rden", [P, NH])
        on = sb("on", [P, D])
        oT = sb("oT", [D + 1, P])
        xn2 = sb("xn2", [P, D])
        xT2 = sb("xT2", [D + 1, WIN, P])
        hh = sb("hh", [HID, NX, SEQ])
        eo = sb("eo", [P, WIN, NX, D])
        gt = sb("gt", [P, WIN, 16])
        ab16 = sb("ab16", [P, WIN, NX], bf16)

        state = sb("state", [P, NB + 1, 12])
        acc = sb("acc", [P, NB + 1, NX, NX + 1])
        src_now = sb("src_now", [P, 4, CH], i32)
        nodes = sb("nodes", [P, 4, CH, FW])
        hot = sb("hot", [P, 2, CH, P])
        hotT = sb("hotT", [P, 2, CH, P])
        hotT_b = sb("hotT_b", [P, 2, CH, P], bf16)
        halves_b = sb("halves_b", [8, 2, CE], bf16)
        top = sb("top", [P, NX])
        dst_in = sb("dst_in", [P, 2, 8])
        fade = sb("fade", [P, 2, NX])
        lg = sb("lg", [P, 2, CH, NX])
        msg = sb("msg", [P, 2, CH, NX, NX + 1])
        ag = sb("ag", [P, NB, 16])
        ag2 = sb("ag2", [P, NB, 16])
        g1 = sb("g1", [P, NB])
        g2 = sb("g2", [P, NB])
        g3 = sb("g3", [P, NB])
        sc = sb("sc", [P, NB, NX])
        wins = sb("wins", [P, NB, NX])
        gate = sb("gate", [P, NB, NX])
        GB = 8
        eb = rows_sb[:, :, :].rearrange("p b f -> p (b f)").rearrange("p (k b e d) -> p k b e d", k=2, b=GB, e=NX)

        psum = [ctx.enter_context(nc.psum_tensor(f"bank{k}", [P, 512], f32)) for k in range(8)]
        count_ps = psum[0:2]
        bank_x, bank_y = psum[6], psum[7]

        names = """apart dve_late dve_chunk dve_end dve_mix const_loaded const_ready ids_loaded edges_loaded eo_free dve_step
            tok_T tok_ready tok_now_ready emb_gathered emb_used hist_oh hist_added hist_done base_mm base_row base_set
            chunk_cmp chunk_sum oh_ready ranked ranks_read counted addr_a addr_b scat_a scat_b edges_sorted
            var_ready log_ready rstd_ready xn_ready xT_mm xT_ready qk_mm v_mm kT_ready q_v_ready s_mm shifted probs pT_mm pT_ready o_mm o_ready oT_mm oT_ready
            proj_mm xn2_ready xT2_mm xT2_ready gat_mm rows_ready rows_out hid_mm hid_ready eo_mm eo_ready eo_out
            sorted_read list_loaded list_ready state_ready src_ready gath_0 gath_1 gath_2 gath_3 hot_ready hotT_mm halves_mm hotT_ready halves_ready
            top_mm top_read dst_ready edge_mm fade_in fade_ready lg_ready weights msg_ready sums_mm
            gvar_ready glog grstd gate_in gate_exp eb_a eb_b eb_used out_ready
            out_done""".split()
        NCH_IT = NCH // 4
        S = {n: sem(n) for n in names}

        class Steps:
            def __init__(self, eng, name, start, it, per):
                self.eng, self.sem, self.start, self.it, self.per, self.n = eng, S[name], start, it, per, 0

            def __call__(self, ins):
                self.n += 1
                ins.then_inc(self.sem, 1)
                base = self.start + self.n
                self.eng.wait_ge(self.sem, base if self.it is None else self.it * self.per + base)

        def apart(eng):
            eng.sem_inc(S["apart"], 1)

        def one(i):
            return bass.ds(i, 1)

        block = ctx.enter_context(nc.Block())
        HIST_IT = NT // 32
        consts_in = 13
        DVE_CH, DVE_MIX = 4 * 9, 2 * 4
        DVE_SEQ = 75

        @block.sync
        def _(sp):
            sp.dma_start(xi[:, :], x).then_inc(S["ids_loaded"], 16)
            sp.dma_start(big_i[:, 0:NT], edges[1:2, :].rearrange("a (p t) -> (a p) t", p=P)).then_inc(S["edges_loaded"], 16)
            sp.dma_start(pay_i[:, 0:NT], edges[0:1, :].rearrange("a (p t) -> (a p) t", p=P)).then_inc(S["edges_loaded"], 16)
            for dst, src in ((cst[:, :], consts[0:P, :]), (pe_sb[:, :, :], pos_enc.rearrange("(w p) d -> p w d", p=P)),
                             (qkvw_sb[:, :], qkv_w), (projw_sb[:, :], proj_w), (w1_sb[:, :, :], w1.rearrange("e k n -> k e n")),
                             (w2_sb[:, :, :], w2.rearrange("e k n -> k e n")), (wg_sb[:, :], w_gat),
                             (b2_sb[:, :, :].rearrange("p e d -> p (e d)"), b2_rows.to_broadcast([P, NX * D])),
                             (att_sb[:, :, :].rearrange("p a b -> p (a b)"), att.to_broadcast([P, 32])),
                             (gr_sb[:, :, :].rearrange("p a b -> p (a b)"), gat_rows.to_broadcast([P, 48])),
                             (hmask[:, :], consts[P:P + D, 0:NH])):
                sp.dma_start(dst, src).then_inc(S["const_loaded"], 16)
            for v in range(2):
                src = bass.AP(tensor=bias_rev.tensor, offset=bias_rev.offset, ap=[[1, P], [2 * P - 1, NH], [1, P]])
                sp.dma_start(rb_sb[:, v, :, :], src).then_inc(S["const_loaded"], 16)
            sp.sem_inc(S["eo_free"], 1)
            with sp.Fori(0, SEQS) as s:
                sp.wait_ge(S["rows_ready"], s + 1)
                sp.dma_start(node_rows.rearrange("(b p) f -> p b f", p=P)[:, bass.ds(s * WIN, WIN), :], rows_sb[:, bass.ds(s * WIN, WIN), :]).then_inc(S["rows_out"], 16)
                sp.wait_ge(S["eo_ready"], s + 1)
                sp.dma_start(expert_out.rearrange("(b p) f -> p b f", p=P)[:, bass.ds(s * WIN, WIN), :], eo[:, :, :, :].rearrange("p w e d -> p w (e d)")).then_inc(S["eo_out"], 16)
                sp.wait_ge(S["eo_out"], s * 16 + 16)
                sp.sem_inc(S["eo_free"], 1)
            sp.wait_ge(S["scat_a"], 16 * NS * (NB + 1))
            sp.wait_ge(S["scat_b"], 16 * NS * (NB + 1))
            sp.wait_ge(S["sorted_read"], 1)
            sp.dma_start(big_i[:, :], edge_list.rearrange("(p t) a -> p (t a)", p=P)).then_inc(S["list_loaded"], 16)
            sp.wait_ge(S["eo_out"], 16 * SEQS)
            with sp.Fori(0, NB // GB // 2) as i:
                for k, loaded in ((0, "eb_a"), (1, "eb_b")):
                    sp.wait_ge(S["eb_used"], i * 2 + k + 1)
                    sp.dma_start(eb[:, k, :, :, :].rearrange("p b e d -> p b (e d)"),
                                 expert_out.rearrange("(b p) f -> p b f", p=P)[:, bass.ds((i * 2 + k) * GB, GB), :]).then_inc(S[loaded], 16)
            sp.wait_ge(S["out_ready"], 1)
            for w in range(WIN - 1):
                sp.dma_start(out[:, w * P + SHIFT:(w + 1) * P + SHIFT, :].rearrange("s p d -> p s d"), h_sb[:, w:NB:WIN, :]).then_inc(S["out_done"], 16)
            sp.dma_start(out[:, SEQ - SHIFT:SEQ, :].rearrange("s p d -> p s d"), h_sb[0:SHIFT, WIN - 1:NB:WIN, :]).then_inc(S["out_done"], 16)
            sp.dma_start(out[:, 0:SHIFT, :].rearrange("s p d -> p s d"), h_sb[SHIFT:P, WIN - 1:NB:WIN, :]).then_inc(S["out_done"], 16)
            sp.wait_ge(S["out_done"], 16 * (WIN + 1))

        @block.gpsimd
        def _(gp):
            def gather_tokens(w):
                gp.indirect_dma_start(emb_now[:, w, :], None, emb, bass.IndirectOffsetOnAxis(ap=tok_now[:, w:w + 1], axis=0)).then_inc(S["emb_gathered"], 16)
            gp.wait_ge(S["const_ready"], 1)
            for k, scattered in ((0, "scat_a"), (1, "scat_b")):
                gp.dma_start(edge_list.rearrange("(p t) a -> p (t a)", p=P)[:, k * LC // 2:(k + 1) * LC // 2],
                             rows_sb[:, :, :].rearrange("p a b -> p (a b)")[:, 0:LC // 2].bitcast(i32)).then_inc(S[scattered], 16 * NS)
            gp.wait_ge(S["scat_a"], 16 * NS)
            gp.wait_ge(S["scat_b"], 16 * NS)
            with gp.Fori(0, SEQS) as s:
                gp.wait_ge(S["tok_now_ready"], s + 1)
                apart(gp)
                for w in range(WIN):
                    gather_tokens(w)
                for w in range(WIN):
                    for b, ready, scattered in ((0, "addr_a", "scat_a"), (1, "addr_b", "scat_b")):
                        gp.wait_ge(S[ready], s * WIN + w + 1)
                        apart(gp)
                        for j in range(NS):
                            gp.indirect_dma_start(edge_list, bass.IndirectOffsetOnAxis(ap=addr_i[:, b, j:j + 1], axis=0), pay_now[:, b, j:j + 1], None).then_inc(S[scattered], 16)

            def gather_nodes(k):
                for j in range(CH):
                    gp.indirect_dma_start(nodes[:, k, j, :], None, node_rows, bass.IndirectOffsetOnAxis(ap=src_now[:, k, j:j + 1], axis=0)).then_inc(S[f"gath_{k}"], 16)

            gp.wait_ge(S["rows_out"], 16 * SEQS)
            with gp.Fori(0, NCH_IT) as i:
                for k in range(4):
                    gp.wait_ge(S["src_ready"], i * 4 + k + 1)
                    gp.wait_ge(S["sums_mm"], i * 4 + k + 1)
                    apart(gp)
                    gather_nodes(k)
            gp.wait_ge(S["src_ready"], NCH + 1)
            gp.wait_ge(S["sums_mm"], NCH + 1)
            gather_nodes(0)

        @block.vector
        def _(dve):
            v = nc.vector
            do = Steps(dve, "dve_step", 0, None, 0)
            dve.wait_ge(S["ids_loaded"], 16)
            do(v.tensor_copy(xf[:, 0:SEQ - SHIFT], xi[:, SHIFT:SEQ]))
            v.tensor_copy(xf[:, SEQ - SHIFT:SEQ], xi[:, 0:SHIFT]).then_inc(S["tok_T"], 1)
            dve.wait_ge(S["const_loaded"], 16 * consts_in)
            v.tensor_copy(iota_b[:, :], iota_f)
            v.tensor_copy(before_b[:, :], upper)
            v.tensor_copy(ones_b[:, :], ones)
            v.tensor_tensor(notbefore_b[:, :], ones, upper, ALU.subtract)
            v.tensor_scalar(bigi_b[:, :], ident, BIG, None, ALU.mult)
            v.memset(zeros_b[:, :], 0.0)
            v.tensor_scalar(rb_sb[0:SHIFT, 1, :, 0:SHIFT], rb_sb[0:SHIFT, 1, :, 0:SHIFT], -100.0, None, ALU.add)
            v.tensor_scalar(rb_sb[SHIFT:P, 1, :, SHIFT:P], rb_sb[SHIFT:P, 1, :, SHIFT:P], -100.0, None, ALU.add)
            v.memset(xT[D:D + 1, :], 1.0)
            v.memset(oT[D:D + 1, :], 1.0)
            v.memset(xT2[D:D + 1, :, :], 1.0)
            v.memset(v1[:, :, HD:HD + 1], 1.0)
            for h in range(NX):
                v.tensor_tensor(sel_b[:, h, :], ident[0:8, h:h + 1].to_broadcast([8, P]), ident[0:8, h + NX:h + NX + 1].to_broadcast([8, P]), ALU.add)
            v.memset(rows_sb[:, :, :].rearrange("p a b -> p (a b)")[:, 0:LC].bitcast(i32), EMPTY).then_inc(S["const_ready"], 1)
            dve.wait_ge(S["const_ready"], 1)
            dve.wait_ge(S["edges_loaded"], 32)
            tmp_i = h_sb[:, 0:NT // D, :].rearrange("p a b -> p (a b)").bitcast(i32)
            for ids in (big_i[:, 0:NT], pay_i[:, 0:NT]):
                do(v.tensor_scalar(tmp_i, ids, float(SEQ - SHIFT), None, ALU.add))
                do(v.tensor_single_scalar(tmp_i, tmp_i, SEQ - 1, ALU.bitwise_and))
                do(v.tensor_scalar(ids, ids, -SEQ, None, ALU.bitwise_and))
                do(v.tensor_tensor(ids, ids, tmp_i, ALU.bitwise_or))
            do(v.tensor_scalar(tmp_i, big_i[:, 0:NT], P - 1, 14, ALU.bitwise_and, ALU.logical_shift_left))
            do(v.tensor_tensor(pay_i[:, 0:NT], pay_i[:, 0:NT], tmp_i, ALU.bitwise_or))
            do(v.tensor_scalar(big_i[:, 0:NT], big_i[:, 0:NT], 7, None, ALU.logical_shift_right))
            do(v.tensor_copy(big_f[:, 0:NT], big_i[:, 0:NT]))
            dve.wait_ge(S["tok_ready"], 1)
            do(v.tensor_copy(tok_i[:, :, :].rearrange("p w s -> p (w s)"), bank_x[:, 0:WIN * SEQS]))
            with dve.Fori(0, HIST_IT) as i:
                for g in range(8):
                    dve.wait_ge(S["hist_added"], i * 8 + g + 1)
                    for j in range(CH):
                        last = v.tensor_scalar(oh[:, g % 2, j, :], iota_b[:, :], big_f[:, one(i * 32 + g * 4 + j)], None, ALU.is_equal)
                    last.then_inc(S["hist_oh"], 1)
            dve.wait_ge(S["hist_done"], 1)
            do(v.tensor_copy(hist[:, 0:4, :].rearrange("p s b -> p (s b)"), count_ps[0][:, :]))
            do(v.tensor_copy(hist[:, 4:8, :].rearrange("p s b -> p (s b)"), count_ps[1][:, :]))
            do(v.tensor_reduce(rowa[:, :], hist[:, :, :].rearrange("p s b -> p b s"), AX.X, ALU.add))
            do(v.tensor_scalar(rowi[:, :], rowa[:, :], float(CE - 1), None, ALU.add))
            do(v.tensor_scalar(rowi[:, :], rowi[:, :], 9, None, ALU.logical_shift_right))
            do(v.tensor_copy(rowa[:, :], rowi[:, :]))
            do(v.tensor_tensor(rowb[:, :], rowa[:, :], ident, ALU.mult))
            do(v.tensor_reduce(colv[:, 0:1], rowb[:, :], AX.X, ALU.add))
            v.tensor_scalar(rowb[:, :], ones, colv[:, 0:1], None, ALU.mult).then_inc(S["base_mm"], 1)
            dve.wait_ge(S["base_row"], 1)
            do(v.tensor_copy(rowa[:, :], bank_x[:, 0:P]))
            do(v.tensor_tensor(rowb[:, :], rowa[:, :], ident, ALU.mult))
            do(v.tensor_reduce(colv[:, 1:2], rowb[:, :], AX.X, ALU.add))
            do(v.tensor_tensor(colv[:, 2:3], colv[:, 0:1], colv[:, 1:2], ALU.add))
            v.tensor_scalar(cmp_b[:, :], chunk_iota, colv[:, 2:3], None, ALU.is_ge).then_inc(S["chunk_cmp"], 1)
            do(v.tensor_scalar(rowa[:, :], rowa[:, :], float(CE), None, ALU.mult))
            for k in range(NS):
                do(v.tensor_tensor(rowb[:, :], hist[:, k, :], rowa[:, :], ALU.add))
                do(v.tensor_copy(hist[:, k, :], rowa[:, :]))
                do(v.tensor_copy(rowa[:, :], rowb[:, :]))
            dve.sem_inc(S["base_set"], 1)
            dve.wait_ge(S["chunk_sum"], 1)
            do(v.tensor_copy(block_of[:, 0:512], bank_x[:, :]))
            do(v.tensor_copy(block_of[:, 512:LC // CH], bank_y[:, 0:LC // CH - 512]))
            pre = do.n

            with dve.Fori(0, SEQS) as s:
                do = Steps(dve, "dve_step", pre, s, DVE_SEQ)
                v.tensor_copy(tok_now[:, :].rearrange("p (w a) -> p w a", a=1), tok_i[:, :, one(s)]).then_inc(S["tok_now_ready"], 1)

                def norm(src, dst, k):
                    apart(dve)
                    do(v.bn_stats(stat[:, :], src))
                    apart(dve)
                    do(v.bn_aggr(mv[:, :], stat[:, :]))
                    v.tensor_scalar(rstd[:, :], mv[:, 1:2], EPS, None, ALU.add).then_inc(S["var_ready"], 1)
                    dve.wait_ge(S["rstd_ready"], s * (2 * WIN) + k)
                    return v.tensor_scalar(dst, src, mv[:, 0:1], rstd[:, 0:1], ALU.subtract, ALU.mult)

                def onehots(w, g):
                    dve.wait_ge(S["counted"], s * 16 + w * 4 + g + 1)
                    for j in range(CH):
                        last = v.tensor_scalar(oh[:, g % 2, j, :], iota_b[:, :], big_f[:, one(s * 64 + w * 16 + g * 4 + j)], None, ALU.is_equal)
                    last.then_inc(S["oh_ready"], 1)

                def ranks(w, g):
                    b = g // 2
                    dve.wait_ge(S["ranked"], s * 16 + w * 4 + g + 1)
                    for j in range(CH):
                        last = v.tensor_tensor_reduce(out=junk[:, j, :], in0=oh[:, g % 2, j, :], in1=count_ps[g % 2][:, j * P:(j + 1) * P], scale=1.0, scalar=0.0,
                                                      op0=ALU.mult, op1=ALU.add, accum_out=pos_f[:, b, (g % 2) * CH + j:(g % 2) * CH + j + 1])
                    last.then_inc(S["ranks_read"], 1)
                    dve.wait_ge(S["ranks_read"], s * 16 + w * 4 + g + 1)
                    if g % 2:
                        do(v.tensor_copy(pos_i[:, b, :], pos_f[:, b, :]))
                        do(v.tensor_scalar(lo_i[:, b, :], pos_i[:, b, :], P - 1, None, ALU.bitwise_and))
                        do(v.tensor_scalar(pos_i[:, b, :], pos_i[:, b, :], 7, None, ALU.logical_shift_right))
                        scattered = S["scat_b" if b else "scat_a"]
                        dve.wait_ge(scattered, (s * WIN + w + 1) * (16 * NS))
                        do(v.scalar_tensor_tensor(addr_i[:, b, :], lo_i[:, b, :], float(LC), pos_i[:, b, :], ALU.mult, ALU.add))
                        apart(dve)
                        v.tensor_copy(pay_now[:, b, :], pay_i[:, bass.ds(s * 64 + w * 16 + b * NS, NS)]).then_inc(S["addr_b" if b else "addr_a"], 1)

                for w in range(WIN):
                    tile = h_sb[:, one(s * WIN + w), :].rearrange("p a d -> p (a d)")
                    n = s * WIN + w
                    if w == 0:
                        dve.wait_ge(S["emb_gathered"], s * (16 * WIN) + 16 * WIN)
                    do(v.tensor_tensor(tile, emb_now[:, w, :], pe_sb[:, w, :], ALU.add))
                    norm(tile, xn[:, :], 2 * w + 1).then_inc(S["xn_ready"], 1)
                    onehots(w, 0)
                    onehots(w, 1)
                    dve.wait_ge(S["v_mm"], n + 1)
                    v.tensor_copy(v1[:, :, 0:HD], bank_x[:, P:P + D].rearrange("p (h d) -> p h d", h=NH))
                    dve.wait_ge(S["kT_ready"], n + 1)
                    v.tensor_tensor(qm[:, :, :], bank_y[0:D, 0:P].rearrange("p (a q) -> p a q", a=1).to_broadcast([D, NH, P]),
                                    hmask[:, :].rearrange("p (h a) -> p h a", a=1).to_broadcast([D, NH, P]), ALU.mult).then_inc(S["q_v_ready"], 1)
                    ranks(w, 0)
                    onehots(w, 2)
                    dve.wait_ge(S["s_mm"], n + 1)
                    for k in range(2):
                        do(v.tensor_reduce(nmax[:, 4 * k:4 * k + 4], psum[2 + k][:, :].rearrange("p (h k) -> p h k", h=4), AX.X, ALU.max))
                    for k in range(2):
                        last = v.tensor_tensor(pr[:, 4 * k:4 * k + 4, :], psum[2 + k][:, :].rearrange("p (h k) -> p h k", h=4),
                                               nmax[:, 4 * k:4 * k + 4].rearrange("p (h a) -> p h a", a=1).to_broadcast([P, 4, P]), ALU.subtract)
                    last.then_inc(S["shifted"], 1)
                    ranks(w, 1)
                    onehots(w, 3)
                    dve.wait_ge(S["o_mm"], n + 1)
                    o_ps = bank_y[:, 256:256 + NH * (HD + 1)].rearrange("p (h d) -> p h d", h=NH)
                    do(v.reciprocal(rden[:, :].rearrange("p (h a) -> p h a", a=1), o_ps[:, :, HD:HD + 1]))
                    v.tensor_tensor(on[:, :].rearrange("p (h d) -> p h d", h=NH), o_ps[:, :, 0:HD],
                                    rden[:, :].rearrange("p (h a) -> p h a", a=1).to_broadcast([P, NH, HD]), ALU.mult).then_inc(S["o_ready"], 1)
                    ranks(w, 2)
                    dve.wait_ge(S["proj_mm"], n + 1)
                    do(v.tensor_tensor(tile, tile, bank_y[:, 384:384 + D], ALU.add))
                    norm(tile, xn2[:, :], 2 * w + 2).then_inc(S["xn2_ready"], 1)
                    ranks(w, 3)

                dve.wait_ge(S["gat_mm"], s + 1)
                rows = rows_sb[:, bass.ds(s * WIN, WIN), :]
                apart(dve)
                do(v.tensor_copy(rows[:, :, 0:16], bank_y[:, 0:64].rearrange("p (w f) -> p w f", w=WIN)))
                for k, col in ((0, 16), (1, 28)):
                    do(v.tensor_tensor(gt[:, :, :], rows[:, :, 0:16], att_sb[:, k:k + 1, :].to_broadcast([P, WIN, 16]), ALU.mult))
                    do(v.tensor_reduce(rows[:, :, col:col + NX], gt[:, :, :].rearrange("p w (h k) -> p w h k", h=NX), AX.X, ALU.add))
                apart(dve)
                do(v.tensor_copy(ab16[:, :, :], rows[:, :, 16:20]))
                apart(dve)
                do(v.tensor_copy(rows[:, :, 20:24], ab16[:, :, :]))
                v.tensor_tensor(rows[:, :, 24:28], rows[:, :, 16:20], rows[:, :, 20:24], ALU.subtract).then_inc(S["rows_ready"], 1)
                dve.wait_ge(S["eo_mm"], s + 1)
                dve.wait_ge(S["eo_free"], s + 1)
                for e in range(NX):
                    src = (bank_x, bank_y)[e // 2][:, (e % 2) * 256:(e % 2) * 256 + 256].rearrange("p (w d) -> p w d", w=WIN)
                    last = v.tensor_tensor(eo[:, :, e, :], src, b2_sb[:, e:e + 1, :].to_broadcast([P, WIN, D]), ALU.add)
                last.then_inc(S["eo_ready"], 1)
                assert do.n == DVE_SEQ, do.n

            do = Steps(dve, "dve_late", 0, None, 0)
            v.memset(state[:, NB:NB + 1, :], 0.0)
            v.memset(acc[:, NB:NB + 1, :, :], 0.0)
            v.tensor_copy(state[:, 0:NB, 0:4], rows_sb[:, :, 16:20])
            v.tensor_copy(state[:, 0:NB, 8:12], rows_sb[:, :, 28:32])
            do(v.tensor_tensor(state[:, 0:NB, 4:8], rows_sb[:, :, 16:20], rows_sb[:, :, 28:32], ALU.add))
            do(v.scalar_tensor_tensor(state[:, 0:NB, 4:8], state[:, 0:NB, 4:8], 0.2, state[:, 0:NB, 4:8], ALU.mult, ALU.max))
            v.memset(acc[:, 0:NB, :, 0:1], 1.0)
            v.tensor_copy(acc[:, 0:NB, :, 1:NX + 1], rows_sb[:, :, 0:16].rearrange("p b (h k) -> p b h k", h=NX)).then_inc(S["state_ready"], 1)
            dve.wait_ge(S["state_ready"], 1)
            dve.sem_inc(S["sorted_read"], 1)
            dve.wait_ge(S["list_loaded"], 16)
            do(v.tensor_single_scalar(pay_i[:, :], big_i[:, :], 14, ALU.logical_shift_right))
            do(v.tensor_copy(big_f[:, :], pay_i[:, :]))
            v.tensor_single_scalar(big_i[:, :], big_i[:, :], (1 << 14) - 1, ALU.bitwise_and).then_inc(S["list_ready"], 1)

            def hots(c, k):
                for j in range(CH):
                    last = v.tensor_scalar(hot[:, k % 2, j, :], iota_f, big_f[:, one(c * CH + j)], None, ALU.is_equal)
                last.then_inc(S["hot_ready"], 1)

            hots(0, 0)
            with dve.Fori(0, NCH_IT) as i:
                do = Steps(dve, "dve_chunk", 0, i, DVE_CH)
                for k in range(4):
                    c = i * 4 + k
                    s2 = k % 2
                    b = dve.value_load(block_of[0:1, one(c)], min_val=0, max_val=NB)
                    st = state[:, one(b), :].rearrange("p a f -> p (a f)")
                    hots(c + 1, k + 1)
                    v.tensor_copy(dst_in[:, s2, 0:4], st[:, 8:12])
                    dve.wait_ge(S["top_mm"], c + 1)
                    for q in range(4):
                        last = v.tensor_reduce(top[:, q:q + 1], psum[2 + q][:, :], AX.X, ALU.max)
                    last.then_inc(S["top_read"], 1)
                    dve.wait_ge(S["top_read"], c + 1)
                    do(v.scalar_tensor_tensor(st[:, 0:4], top[:, :], -BIG, st[:, 0:4], ALU.add, ALU.max))
                    do(v.tensor_tensor(lg[:, s2, 0, :], st[:, 0:4], st[:, 8:12], ALU.add))
                    do(v.scalar_tensor_tensor(dst_in[:, s2, 4:8], lg[:, s2, 0, :], 0.2, lg[:, s2, 0, :], ALU.mult, ALU.max))
                    dve.sem_inc(S["dst_ready"], 1)
                    v.tensor_tensor(fade[:, s2, :], st[:, 4:8], dst_in[:, s2, 4:8], ALU.subtract).then_inc(S["fade_in"], 1)
                    dve.wait_ge(S["fade_in"], c + 1)
                    do(v.tensor_scalar(st[:, 4:8], dst_in[:, s2, 4:8], 1.0, None, ALU.mult))
                    dve.wait_ge(S["edge_mm"], c + 1)
                    dst_ps = psum[6][:, 0:32].rearrange("p (j f) -> p j f", j=CH)
                    do(v.tensor_tensor(lg[:, s2, :, :], nodes[:, k, :, 16:20], dst_ps[:, :, 0:4], ALU.add))
                    do(v.scalar_tensor_tensor(lg[:, s2, :, :], lg[:, s2, :, :], 0.2, lg[:, s2, :, :], ALU.mult, ALU.max))
                    do(v.tensor_tensor(lg[:, s2, :, :], lg[:, s2, :, :], dst_ps[:, :, 4:8], ALU.subtract))
                    v.tensor_scalar(lg[:, s2, :, :], lg[:, s2, :, :], 20.0, None, ALU.min).then_inc(S["lg_ready"], 1)
                    dve.wait_ge(S["weights"], c + 1)
                    for h in range(NX):
                        last = v.tensor_tensor(msg[:, s2, :, h, 1:NX + 1], nodes[:, k, :, 4 * h:4 * h + 4], msg[:, s2, :, h, 0:1].to_broadcast([P, CH, NX]), ALU.mult)
                    last.then_inc(S["msg_ready"], 1)
                    ac = acc[:, one(b), :, :].rearrange("p a h f -> p (a h) f")
                    dve.wait_ge(S["fade_ready"], c + 1)
                    do(v.tensor_tensor(ac, ac, fade[:, s2, :].rearrange("p (h a) -> p h a", a=1).to_broadcast([P, NX, NX + 1]), ALU.mult))
                    dve.wait_ge(S["sums_mm"], c + 5)
                    do(v.tensor_tensor(ac, ac, psum[7][:, 0:20].rearrange("p (h f) -> p h f", h=NX), ALU.add))
                assert do.n == DVE_CH, do.n

            do = Steps(dve, "dve_end", 0, None, 0)
            def wide(ap):
                return ap.rearrange("p (b a) -> p b a", a=1)
            dve.sem_inc(S["eb_used"], 2)
            w4 = acc[:, 0:NB, :, 0:1].rearrange("p b h a -> p b (h a)")
            do(v.tensor_scalar(sc[:, :, :], w4, 1e-16, None, ALU.add))
            do(v.reciprocal(sc[:, :, :], sc[:, :, :]))
            ag4 = ag[:, :, :].rearrange("p b (h k) -> p b h k", h=NX)
            for h in range(NX):
                last = do(v.tensor_tensor(ag4[:, :, h, :], acc[:, 0:NB, h, 1:NX + 1], sc[:, :, h:h + 1].to_broadcast([P, NB, NX]), ALU.mult))
            do(v.tensor_tensor(ag[:, :, :], ag[:, :, :], gr_sb[:, 0:1, :].to_broadcast([P, NB, 16]), ALU.add))
            do(v.tensor_reduce(g1[:, :], ag[:, :, :], AX.X, ALU.add))
            do(v.tensor_scalar(g1[:, :], g1[:, :], 1.0 / 16, None, ALU.mult))
            do(v.tensor_tensor(ag[:, :, :], ag[:, :, :], wide(g1[:, :]).to_broadcast([P, NB, 16]), ALU.subtract))
            do(v.tensor_tensor(ag2[:, :, :], ag[:, :, :], ag[:, :, :], ALU.mult))
            do(v.tensor_reduce(g1[:, :], ag2[:, :, :], AX.X, ALU.add))
            v.tensor_scalar(g1[:, :], g1[:, :], 1.0 / 16, EPS, ALU.mult, ALU.add).then_inc(S["gvar_ready"], 1)
            dve.wait_ge(S["grstd"], 1)
            do(v.tensor_tensor(ag[:, :, :], ag[:, :, :], wide(g1[:, :]).to_broadcast([P, NB, 16]), ALU.mult))
            do(v.tensor_tensor(ag[:, :, :], ag[:, :, :], gr_sb[:, 1:2, :].to_broadcast([P, NB, 16]), ALU.mult))
            do(v.tensor_tensor(ag[:, :, :], ag[:, :, :], gr_sb[:, 2:3, :].to_broadcast([P, NB, 16]), ALU.add))
            do(v.tensor_reduce(sc[:, :, :], ag[:, :, :].rearrange("p b (h k) -> p b k h", h=NX), AX.X, ALU.add))
            do(v.tensor_scalar(sc[:, :, :], sc[:, :, :], 0.25, None, ALU.mult))
            do(v.memset(wins[:, :, :], 0.0))
            for e in range(NX):
                for f in range(e + 1, NX):
                    do(v.tensor_tensor(wide(g1[:, :]), sc[:, :, e:e + 1], sc[:, :, f:f + 1], ALU.is_ge))
                    do(v.tensor_tensor(wins[:, :, e:e + 1], wins[:, :, e:e + 1], wide(g1[:, :]), ALU.add))
                    do(v.tensor_scalar(g1[:, :], g1[:, :], -1.0, 1.0, ALU.mult, ALU.add))
                    do(v.tensor_tensor(wins[:, :, f:f + 1], wins[:, :, f:f + 1], wide(g1[:, :]), ALU.add))
            do(v.tensor_reduce(g1[:, :], sc[:, :, :], AX.X, ALU.max))
            do(v.tensor_scalar(gate[:, :, :], wins[:, :, :], 2.0, None, ALU.is_equal))
            do(v.tensor_tensor(sc[:, :, :], sc[:, :, :], gate[:, :, :], ALU.mult))
            do(v.tensor_reduce(g2[:, :], sc[:, :, :], AX.X, ALU.add))
            v.tensor_tensor(g2[:, :], g2[:, :], g1[:, :], ALU.subtract).then_inc(S["gate_in"], 1)
            dve.wait_ge(S["gate_exp"], 1)
            do(v.tensor_scalar(g1[:, :], g2[:, :], 1.0, None, ALU.add))
            do(v.reciprocal(g1[:, :], g1[:, :]))
            do(v.tensor_tensor(g2[:, :], g2[:, :], g1[:, :], ALU.mult))
            do(v.tensor_tensor(gate[:, :, :], gate[:, :, :], wide(g2[:, :]).to_broadcast([P, NB, NX]), ALU.mult))
            do(v.tensor_scalar(wins[:, :, :], wins[:, :, :], 3.0, None, ALU.is_equal))
            do(v.tensor_tensor(wins[:, :, :], wins[:, :, :], wide(g1[:, :]).to_broadcast([P, NB, NX]), ALU.mult))
            do(v.tensor_tensor(gate[:, :, :], gate[:, :, :], wins[:, :, :], ALU.add))
            with dve.Fori(0, NB // GB // 2) as i:
                do = Steps(dve, "dve_mix", 0, i, DVE_MIX)
                for k, loaded in ((0, "eb_a"), (1, "eb_b")):
                    dve.wait_ge(S[loaded], i * 16 + 16)
                    blocks = bass.ds((i * 2 + k) * GB, GB)
                    for e in range(NX):
                        last = v.tensor_tensor(eb[:, k, :, e, :], eb[:, k, :, e, :], gate[:, blocks, e:e + 1].to_broadcast([P, GB, D]), ALU.mult)
                    do(last)
                    do(v.tensor_tensor(eb[:, k, :, 0:2, :], eb[:, k, :, 0:2, :], eb[:, k, :, 2:4, :], ALU.add))
                    do(v.tensor_tensor(h_sb[:, blocks, :], h_sb[:, blocks, :], eb[:, k, :, 0, :], ALU.add))
                    do(v.tensor_tensor(h_sb[:, blocks, :], h_sb[:, blocks, :], eb[:, k, :, 1, :], ALU.add))
                    dve.sem_inc(S["eb_used"], 1)
                assert do.n == DVE_MIX, do.n
            dve.sem_inc(S["out_ready"], 1)

        @block.scalar
        def _(act):
            a = nc.scalar
            with act.Fori(0, SEQS) as s:
                def root(k):
                    act.wait_ge(S["var_ready"], s * (2 * WIN) + k)
                    a.activation(rstd[:, :], rstd[:, :], ACT.Ln).then_inc(S["log_ready"], 1)
                    act.wait_ge(S["log_ready"], s * (2 * WIN) + k)
                    a.activation(rstd[:, :], rstd[:, :], ACT.Exp, scale=-0.5).then_inc(S["rstd_ready"], 1)

                for w in range(WIN):
                    n = s * WIN + w
                    root(2 * w + 1)
                    act.wait_ge(S["xT_mm"], n + 1)
                    a.activation(xT[0:D, :], bank_x[0:D, 0:P], ACT.Copy).then_inc(S["xT_ready"], 1)
                    act.wait_ge(S["qk_mm"], n + 1)
                    a.activation(kT[:, :], bank_y[0:D, P:2 * P], ACT.Copy).then_inc(S["kT_ready"], 1)
                    act.wait_ge(S["shifted"], n + 1)
                    a.activation(pr[:, :, :], pr[:, :, :], ACT.Exp).then_inc(S["probs"], 1)
                    act.wait_ge(S["pT_mm"], n + 1)
                    for k in range(2):
                        last = a.activation(prT[:, 4 * k:4 * k + 4, :], psum[4 + k][:, :].rearrange("p (h k) -> p h k", h=4), ACT.Copy)
                    last.then_inc(S["pT_ready"], 1)
                    act.wait_ge(S["oT_mm"], n + 1)
                    a.activation(oT[0:D, :], bank_x[0:D, 192:192 + P], ACT.Copy).then_inc(S["oT_ready"], 1)
                    root(2 * w + 2)
                    act.wait_ge(S["xT2_mm"], n + 1)
                    a.activation(xT2[0:D, w, :], bank_x[0:D, 320:320 + P], ACT.Copy).then_inc(S["xT2_ready"], 1)
                act.wait_ge(S["hid_mm"], s + 1)
                for e in range(NX):
                    last = a.activation(hh[:, e, :], psum[2 + e][:, :], ACT.Gelu)
                last.then_inc(S["hid_ready"], 1)

            def sources(c, k):
                a.activation(src_now[:, k % 4, :], big_i[:, bass.ds(c * CH, CH)], ACT.Copy).then_inc(S["src_ready"], 1)

            def turned(c, k):
                act.wait_ge(S["hotT_mm"], c + 1)
                a.activation(hotT[:, k % 2, :, :], psum[0][:, :], ACT.Copy)
                a.activation(hotT_b[:, k % 2, :, :], psum[0][:, :], ACT.Copy).then_inc(S["hotT_ready"], 1)
                act.wait_ge(S["halves_mm"], c + 1)
                a.activation(halves_b[:, k % 2, :], psum[1][0:8, :], ACT.Copy).then_inc(S["halves_ready"], 1)

            act.wait_ge(S["list_ready"], 1)
            for k in range(3):
                sources(k, k)
            turned(0, 0)
            with act.Fori(0, NCH_IT) as i:
                for k in range(4):
                    c = i * 4 + k
                    sources(c + 3, k + 3)
                    turned(c + 1, k + 1)
                    act.wait_ge(S["fade_in"], c + 1)
                    a.activation(fade[:, k % 2, :], fade[:, k % 2, :], ACT.Exp).then_inc(S["fade_ready"], 1)
                    act.wait_ge(S["lg_ready"], c + 1)
                    a.activation(msg[:, k % 2, :, :, 0:1].rearrange("p j h a -> p (j h) a"), lg[:, k % 2, :, :].rearrange("p j (h a) -> p (j h) a", a=1), ACT.Exp).then_inc(S["weights"], 1)
            act.wait_ge(S["gvar_ready"], 1)
            a.activation(g1[:, :], g1[:, :], ACT.Ln).then_inc(S["glog"], 1)
            act.wait_ge(S["glog"], 1)
            a.activation(g1[:, :], g1[:, :], ACT.Exp, scale=-0.5).then_inc(S["grstd"], 1)
            act.wait_ge(S["gate_in"], 1)
            a.activation(g2[:, :], g2[:, :], ACT.Exp).then_inc(S["gate_exp"], 1)

        @block.tensor
        def _(pe):
            t = nc.tensor
            pe.wait_ge(S["tok_T"], 1)
            pe.wait_ge(S["const_loaded"], 16 * consts_in)
            pe.wait_ge(S["const_ready"], 1)
            for w in range(WIN):
                last = t.transpose(bank_x[:, w * SEQS:(w + 1) * SEQS], xf[:, w * P:(w + 1) * P], ident[0:SEQS, 0:SEQS])
            last.then_inc(S["tok_ready"], 1)
            for k in range(2):
                t.matmul(count_ps[k][:, :], ones_b[:, :], zeros_b[:, :], start=True, stop=True, skip_group_check=True)
            pe.sem_inc(S["hist_added"], 2)
            with pe.Fori(0, HIST_IT) as i:
                for g in range(8):
                    pe.wait_ge(S["hist_oh"], i * 8 + g + 1)
                    t.matmul(count_ps[g % 2][:, :], ones_b[:, :], oh[:, g % 2, :, :], start=False, stop=True, skip_group_check=True).then_inc(S["hist_added"], 1)
            t.transpose(bank_y[0:SEQS, 0:SEQS], xf[:, 0:SEQS], ident[0:SEQS, 0:SEQS]).then_inc(S["hist_done"], 1)
            pe.wait_ge(S["base_mm"], 1)
            t.matmul(bank_x[:, 0:P], rowb[:, :], upper, start=True, stop=True).then_inc(S["base_row"], 1)
            pe.wait_ge(S["chunk_cmp"], 1)
            t.matmul(bank_x[:, :], ones_b[:, :], cmp_b[:, 0:512], start=True, stop=True)
            t.matmul(bank_y[:, 0:LC // CH - 512], ones_b[:, :], cmp_b[:, 512:], start=True, stop=True).then_inc(S["chunk_sum"], 1)
            pe.wait_ge(S["base_set"], 1)
            for k in range(2):
                t.matmul(count_ps[k][:, :], ident, hist[:, 4 * k:4 * k + 4, :], start=True, stop=True, skip_group_check=True)

            pe.sem_inc(S["counted"], 2)
            with pe.Fori(0, SEQS) as s:
                def rank(w, g):
                    pe.wait_ge(S["oh_ready"], s * 16 + w * 4 + g + 1)
                    t.matmul(count_ps[g % 2][:, :], before_b[:, :], oh[:, g % 2, :, :], start=False, stop=True, skip_group_check=True).then_inc(S["ranked"], 1)

                def count(w, g):
                    pe.wait_ge(S["ranks_read"], s * 16 + w * 4 + g + 1)
                    t.matmul(count_ps[g % 2][:, :], notbefore_b[:, :], oh[:, g % 2, :, :], start=False, stop=True, skip_group_check=True).then_inc(S["counted"], 1)

                for w in range(WIN):
                    n = s * WIN + w
                    pe.wait_ge(S["xn_ready"], n + 1)
                    apart(pe)
                    t.transpose(bank_x[0:D, 0:P], xn[:, :], ident).then_inc(S["xT_mm"], 1)
                    rank(w, 0)
                    rank(w, 1)
                    pe.wait_ge(S["xT_ready"], n + 1)
                    t.matmul(bank_y[0:D, 0:P], qkvw_sb[:, 0:D], xT[:, :], start=True, stop=True)
                    t.matmul(bank_y[0:D, P:2 * P], qkvw_sb[:, D:2 * D], xT[:, :], start=True, stop=True).then_inc(S["qk_mm"], 1)
                    t.matmul(bank_x[:, P:P + D], xT[:, :], qkvw_sb[:, 2 * D:3 * D], start=True, stop=True).then_inc(S["v_mm"], 1)
                    count(w, 0)
                    rank(w, 2)
                    pe.wait_ge(S["kT_ready"], n + 1)
                    pe.wait_ge(S["q_v_ready"], n + 1)
                    for h in range(NH):
                        bank = psum[2 + h // 4]
                        if h % 4 == 0:
                            t.matmul(bank[:, :], flip, rb_sb[:, w // (WIN - 1), h:h + 4, :], start=True, stop=False)
                        last = t.matmul(bank[:, (h % 4) * P:(h % 4 + 1) * P], qm[:, h, :], kT[:, :], start=False, stop=h % 4 == 3)
                    last.then_inc(S["s_mm"], 1)
                    count(w, 1)
                    rank(w, 3)
                    pe.wait_ge(S["probs"], n + 1)
                    for h in range(NH):
                        last = t.transpose(psum[4 + h // 4][:, (h % 4) * P:(h % 4 + 1) * P], pr[:, h, :], ident)
                    last.then_inc(S["pT_mm"], 1)
                    pe.wait_ge(S["pT_ready"], n + 1)
                    for h in range(NH):
                        last = t.matmul(bank_y[:, 256 + h * (HD + 1):256 + (h + 1) * (HD + 1)], prT[:, h, :], v1[:, h, :], start=True, stop=True)
                    last.then_inc(S["o_mm"], 1)
                    pe.wait_ge(S["o_ready"], n + 1)
                    apart(pe)
                    t.transpose(bank_x[0:D, 192:192 + P], on[:, :], ident).then_inc(S["oT_mm"], 1)
                    pe.wait_ge(S["oT_ready"], n + 1)
                    t.matmul(bank_y[:, 384:384 + D], oT[:, :], projw_sb[:, :], start=True, stop=True).then_inc(S["proj_mm"], 1)
                    count(w, 2)
                    pe.wait_ge(S["xn2_ready"], n + 1)
                    apart(pe)
                    t.transpose(bank_x[0:D, 320:320 + P], xn2[:, :], ident).then_inc(S["xT2_mm"], 1)
                    count(w, 3)
                pe.wait_ge(S["xT2_ready"], s * WIN + WIN)
                for w in range(WIN):
                    last = t.matmul(bank_y[:, w * 16:(w + 1) * 16], xT2[0:D, w, :], wg_sb[:, :], start=True, stop=True)
                last.then_inc(S["gat_mm"], 1)
                for e in range(NX):
                    last = t.matmul(psum[2 + e][:, :], w1_sb[:, e, :], xT2[:, :, :], start=True, stop=True)
                last.then_inc(S["hid_mm"], 1)
                pe.wait_ge(S["hid_ready"], s + 1)
                pe.wait_ge(S["rows_ready"], s + 1)
                for e in range(NX):
                    for w in range(WIN):
                        c = (e % 2) * 256 + w * D
                        last = t.matmul((bank_x, bank_y)[e // 2][:, c:c + D], hh[:, e, w * P:(w + 1) * P], w2_sb[:, e, :], start=True, stop=True)
                last.then_inc(S["eo_mm"], 1)

            def turn(c, k, gathers):
                pe.wait_ge(S["hot_ready"], c + 1)
                for j in range(CH):
                    last = t.transpose(psum[0][:, j * P:(j + 1) * P], hot[:, k % 2, j, :], ident)
                last.then_inc(S["hotT_mm"], 1)
                pe.wait_ge(S[f"gath_{k % 4}"], gathers * (16 * CH))
                for j in range(CH):
                    last = t.transpose(psum[1][0:8, j * P:(j + 1) * P], nodes[:, k % 4, j, 20:28], ident)
                last.then_inc(S["halves_mm"], 1)

            def tops(c, k):
                pe.wait_ge(S["hotT_ready"], c + 1)
                pe.wait_ge(S["halves_ready"], c + 1)
                for h in range(NX):
                    t.matmul(psum[2 + h][:, :], bigi_b[:, :], hotT_b[:, k % 2, :, :], start=True, stop=False)
                    last = t.matmul(psum[2 + h][:, :], sel_b[:, h, :], halves_b[:, k % 2, :], start=False, stop=True)
                last.then_inc(S["top_mm"], 1)

            pe.sem_inc(S["sums_mm"], 4)
            pe.wait_ge(S["state_ready"], 1)
            turn(0, 0, 1)
            tops(0, 0)
            with pe.Fori(0, NCH_IT) as i:
                for k in range(4):
                    c = i * 4 + k
                    turn(c + 1, k + 1, i + 1 + (k + 1) // 4)
                    pe.wait_ge(S["dst_ready"], c + 1)
                    for j in range(CH):
                        last = t.matmul(psum[6][:, j * 8:(j + 1) * 8], hotT[:, k % 2, j, :], dst_in[:, k % 2, :], start=True, stop=True)
                    last.then_inc(S["edge_mm"], 1)
                    tops(c + 1, k + 1)
                    pe.wait_ge(S["msg_ready"], c + 1)
                    for j in range(CH):
                        last = t.matmul(psum[7][:, 0:20], hot[:, k % 2, j, :], msg[:, k % 2, j, :, :], start=j == 0, stop=j == CH - 1)
                    last.then_inc(S["sums_mm"], 1)


def kernel(**inputs):
    import concourse.bacc as bacc
    from concourse.bass_utils import run_bass_kernel_spmd as run

    f = {k: np.ascontiguousarray(a) for k, a in inputs.items()}
    seq, d, p = 512, 64, 128
    lc = 4 * (262144 // 512 + 128 + 4)
    pos = np.arange(seq, dtype=np.float32)[:, None]
    k = np.arange(d)
    inv = np.power(np.float32(10000.0), -((k - k % 2).astype(np.float32) / np.float32(d))).astype(np.float32)
    angle = pos * inv
    pos_enc = np.roll(np.where(k % 2 == 0, np.sin(angle), np.cos(angle)).astype(np.float32), -p // 2, axis=0)
    top = np.concatenate([np.eye(p), np.tile(np.arange(p), (p, 1)), np.triu(np.ones((p, p)), 1), np.ones((p, p)), np.eye(p)[::-1],
                          np.tile(np.arange(lc // 4), (p, 1))], axis=1)
    mask = np.zeros((d, top.shape[1]))
    mask[np.arange(d), np.arange(d) // 8] = 8 ** -0.5
    consts = np.concatenate([top, mask]).astype(np.float32)
    arrays = {
        "x": f["x"], "emb": f["L0_tok_W"],
        "qkv_w": np.concatenate([f["L0_attn_qkv_weight"].T, f["L0_attn_qkv_bias"][None]]),
        "proj_w": np.concatenate([f["L0_attn_proj_weight"].T, f["L0_attn_proj_bias"][None]]),
        "bias_rev": np.ascontiguousarray(f["L0_attn_bias_table"][::-1].T),
        "att": np.concatenate([f["L0_ffn_att_src"].reshape(1, 16), f["L0_ffn_att_dst"].reshape(1, 16)], axis=1),
        "w_gat": f["L0_ffn_W_gat"],
        "gat_rows": np.concatenate([f["L0_ffn_b_gat"], f["L0_ffn_ln_gamma"], f["L0_ffn_ln_beta"]])[None],
        "w1": np.concatenate([f["L0_ffn_W1"], f["L0_ffn_b1"][:, None]], axis=1),
        "w2": f["L0_ffn_W2"], "b2_rows": f["L0_ffn_b2"].reshape(1, 256), "edges": f["L0_ffn_edge_index"],
        "pos_enc": pos_enc, "consts": consts,
    }
    nc = bacc.Bacc("TRN2", target_bir_lowering=False, num_devices=1)
    args = [nc.dram_tensor("in_" + n, a.shape, mybir.dt.from_np(a.dtype), kind="ExternalInput").ap() for n, a in arrays.items()]
    out = nc.dram_tensor("out_0", (32, 512, 64), mybir.dt.float32, kind="ExternalOutput").ap()
    lm_tower_kernel(nc, *args, out)
    r = run(nc, [{"in_" + n: np.ascontiguousarray(a) for n, a in arrays.items()}], core_ids=[0])
    return r.results[0]["out_0"]
```

```python
import concourse.bass as bass
from concourse import mybir
from contextlib import ExitStack
import numpy as np


def lm_tower_kernel(nc, x, emb, qkv_w, proj_w, bias_rev, att, w_gat, gat_rows, w1, w2, b2_rows, edges, pos_enc, consts, out):
    f32, bf16, i32 = mybir.dt.float32, mybir.dt.bfloat16, mybir.dt.int32
    ALU, ACT, AX = mybir.AluOpType, mybir.ActivationFunctionType, mybir.AxisListType
    P = 128
    SEQS, SEQ = x.shape
    D = emb.shape[1]
    WIN = SEQ // P
    SHIFT = P // 2
    NH, HD = 8, 8
    NB = SEQS * WIN
    NE = edges.shape[1]
    NT = NE // P
    NX = 4
    HID = 2 * D
    CH = 4
    CE = CH * P
    NCH = NE // CE + NB
    LC = (NCH + 8) * CH
    NS = 8
    TW = NT // NB
    FW = 32
    BIG = float(2 ** 20)
    EMPTY = P << 14
    EPS = 1e-5

    ctx = ExitStack()
    with ctx:
        def sb(name, shape, dt=f32):
            return ctx.enter_context(nc.sbuf_tensor(name, shape, dt))

        def sem(name):
            return ctx.enter_context(nc.semaphore(name))

        edge_list = nc.dram_tensor("edge_list", [P * LC, 1], i32, kind="Internal").ap()
        node_rows = nc.dram_tensor("node_rows", [NB * P, FW], f32, kind="Internal").ap()
        expert_out = nc.dram_tensor("expert_out", [NB * P, NX * D], f32, kind="Internal").ap()

        h_sb = sb("h_sb", [P, NB + WIN, D])
        rows_sb = sb("rows_sb", [P, NB, FW])
        big_i = sb("big_i", [P, LC], i32)
        pay_i = sb("pay_i", [P, LC], i32)
        big_f = sb("big_f", [P, LC])
        iota_b = sb("iota_b", [P, P], bf16)
        cst = sb("cst", [P, 5 * P + LC // CH])
        ident, iota_f, upper, ones, flip = (cst[:, k * P:(k + 1) * P] for k in range(5))
        chunk_iota = cst[:, 5 * P:]
        before_b = sb("before_b", [P, P], bf16)
        notbefore_b = sb("notbefore_b", [P, P], bf16)
        ones_b = sb("ones_b", [P, P], bf16)
        zeros_b = sb("zeros_b", [P, CE], bf16)
        bigi_b = sb("bigi_b", [P, P], bf16)
        sel_b = sb("sel_b", [8, NX, P], bf16)
        pe_sb = sb("pe_sb", [P, WIN, D])
        rb_sb = sb("rb_sb", [P, 2, NH, P])
        hmask = sb("hmask", [D, NH])
        qkvw_sb = sb("qkvw_sb", [D + 1, 3 * D])
        projw_sb = sb("projw_sb", [D + 1, D])
        w1_sb = sb("w1_sb", [D + 1, NX, HID])
        w2_sb = sb("w2_sb", [HID, NX, D])
        b2_sb = sb("b2_sb", [P, NX, D])
        wg_sb = sb("wg_sb", [D, 16])
        att_sb = sb("att_sb", [P, 2, 16])
        gr_sb = sb("gr_sb", [P, 3, 16])
        xi = sb("xi", [SEQS, SEQ], i32)
        xf = sb("xf", [SEQS, SEQ])
        tok_i = sb("tok_i", [P, WIN, SEQS + 2], i32)
        tok_now = sb("tok_now", [P, WIN], i32)
        emb_now = sb("emb_now", [P, WIN, D])
        oh = sb("oh", [P, 4, CH, P], bf16)
        junk = sb("junk", [P, CH, P])
        pos_f = sb("pos_f", [P, 2, NS])
        pos_i = sb("pos_i", [P, 2, NS], i32)
        lo_i = sb("lo_i", [P, 2, NS], i32)
        addr_i = sb("addr_i", [P, 2, NS], i32)
        pay_now = sb("pay_now", [P, 2, NS], i32)
        hist = sb("hist", [P, NS, P])
        rowa = sb("rowa", [P, P])
        rowi = sb("rowi", [P, P], i32)
        rowb = sb("rowb", [P, P])
        colv = sb("colv", [P, 4])
        cmp_b = sb("cmp_b", [P, LC // CH], bf16)
        block_of = sb("block_of", [P, LC // CH], i32)
        stat = sb("stat", [P, WIN, 6])
        mv = sb("mv", [P, 2, WIN, 2])
        rstd = sb("rstd", [P, 2, WIN])
        root_t = sb("root_t", [P, WIN])
        xn = sb("xn", [P, D])
        xT = sb("xT", [D + 1, P])
        kT = sb("kT", [D, P])
        qm = sb("qm", [D, NH, P])
        v1 = sb("v1", [P, 2, NH, HD + 1])
        nmax = sb("nmax", [P, NH])
        pr = sb("pr", [P, NH, P])
        prT = sb("prT", [P, NH, P])
        rden = sb("rden", [P, NH])
        on = sb("on", [P, D])
        oT = sb("oT", [D + 1, P])
        xn2 = sb("xn2", [P, WIN, D])
        xT2 = sb("xT2", [D + 1, WIN, P])
        hh = sb("hh", [HID, NX, SEQ])
        eo = sb("eo", [P, WIN, NX, D])
        gt = sb("gt", [P, WIN, 16])
        ab16 = sb("ab16", [P, WIN, NX], bf16)

        state = sb("state", [P, NB + 1, 12])
        acc = sb("acc", [P, NB + 1, NX, NX + 1])
        SL = 8
        src_now = sb("src_now", [P, SL, CH], i32)
        nodes = sb("nodes", [P, SL, CH, FW])
        hot = sb("hot", [P, SL, CH, P])
        hotT = sb("hotT", [P, 2, CH, P])
        hotT_b = sb("hotT_b", [P, 2, CH, P], bf16)
        halves_b = sb("halves_b", [8, 2, CE], bf16)
        top = sb("top", [P, NX])
        dst_in = sb("dst_in", [P, 2, 8])
        score = sb("score", [P, 2, NX])
        dst_e = sb("dst_e", [P, 2, CH, 8])
        fade = sb("fade", [P, 4, NX])
        lg = sb("lg", [P, 2, CH, NX])
        msg = sb("msg", [P, 4, CH, NX, NX + 1])
        ss = hot[:, 0:2, :, :].rearrange("p s j k -> p (s j) k")
        ag, ag2 = (hot[:, k * SL // 2:(k + 1) * SL // 2, :, :].rearrange("p s j e -> p (s j e)").rearrange("p (b f) -> p b f", f=16) for k in range(2))
        g1 = sb("g1", [P, NB])
        g2 = sb("g2", [P, NB])
        g3 = sb("g3", [P, NB])
        sc = sb("sc", [P, NB, NX])
        wins = sb("wins", [P, NB, NX])
        gate = sb("gate", [P, NB, NX])
        GB = 8
        eb = rows_sb[:, :, :].rearrange("p b f -> p (b f)").rearrange("p (k b e d) -> p k b e d", k=2, b=GB, e=NX)

        def pb(name, banks):
            return ctx.enter_context(nc.psum_tensor(name, [P, banks * 512], f32))

        four = pb("four", 4)
        psum = [pb("bank0", 1), pb("bank1", 1)] + [four[:, k * 512:(k + 1) * 512] for k in range(4)] + [pb("bank6", 1), pb("bank7", 1)]
        count_ps = psum[0:2]
        bank_x, bank_y = psum[6], psum[7]

        names = """apart dve_late dve_end dve_mix const_loaded const_ready ids_loaded edges_loaded eo_free dve_step
            tok_T tok_ready tok_now_ready emb_gathered emb_used hist_oh hist_added hist_done base_mm base_row base_set
            chunk_cmp chunk_sum oh_ready ranked ranks_read counted addr_a addr_b scat_a scat_b edges_sorted
            bias_mm xn_ready xT_mm xT_ready qkv_mm kT_ready q_v_ready s_mm nmax_ready probs resid_done pT_mm pT_ready o_mm o_ready oT_mm oT_ready
            proj_mm xn2_ready xT2_mm xT2_ready gat_mm rows_ready rows_out hid_mm hid_ready eo_mm eo_ready eo_out
            sorted_read list_loaded list_ready state_ready src_ready hot_ready hotT_mm halves_mm hotT_ready halves_ready
            top_kept score_ready shift_kept lg_1 lg_2 lg_3 faded sums_kept top_mm top_read dst_ready edge_mm edge_out fade_in fade_ready lg_ready weights msg_ready sums_mm
            gvar_ready glog grstd gate_in gate_exp eb_a eb_b eb_used out_ready
            out_done""".split()
        gathered = [sem(f"gathered_{k}") for k in range(SL)]

        def chunks(eng, step):
            for c in range(SL):
                step(c, c, True, 0)
            with eng.Fori(1, NCH // SL) as i:
                for k in range(SL):
                    step(i * SL + k, k, False, i)
            for c in range(NCH, NCH + 3):
                step(c, c % SL, True, c // SL)

        def windows(eng, step):
            for w in range(WIN):
                step(w, w, 0, True, w > 0, False)
            with eng.Fori(1, SEQS) as s:
                for w in range(WIN):
                    step(s * WIN + w, w, s, True, True, True)
            for w in range(WIN):
                step(NB + w, w, SEQS, False, w == 0, True)

        S = {n: sem(n) for n in names}

        class Steps:
            def __init__(self, eng, name, start, it, per):
                self.eng, self.sem, self.start, self.it, self.per, self.n = eng, S[name], start, it, per, 0

            def __call__(self, ins):
                self.n += 1
                ins.then_inc(self.sem, 1)
                base = self.start + self.n
                self.eng.wait_ge(self.sem, base if self.it is None else self.it * self.per + base)

        def apart(eng):
            eng.sem_inc(S["apart"], 1)

        def one(i):
            return bass.ds(i, 1)

        block = ctx.enter_context(nc.Block())
        HIST_IT = NT // 32
        consts_in = 13
        DVE_MIX = 2 * 4
        DVE_SEQ = 88

        @block.sync
        def _(sp):
            sp.dma_start(xi[:, :], x).then_inc(S["ids_loaded"], 16)
            sp.dma_start(big_i[:, 0:NT], edges[1:2, :].rearrange("a (p t) -> (a p) t", p=P)).then_inc(S["edges_loaded"], 16)
            sp.dma_start(pay_i[:, 0:NT], edges[0:1, :].rearrange("a (p t) -> (a p) t", p=P)).then_inc(S["edges_loaded"], 16)
            for dst, src in ((cst[:, :], consts[0:P, :]), (pe_sb[:, :, :], pos_enc.rearrange("(w p) d -> p w d", p=P)),
                             (qkvw_sb[:, :], qkv_w), (projw_sb[:, :], proj_w), (w1_sb[:, :, :], w1.rearrange("e k n -> k e n")),
                             (w2_sb[:, :, :], w2.rearrange("e k n -> k e n")), (wg_sb[:, :], w_gat),
                             (b2_sb[:, :, :].rearrange("p e d -> p (e d)"), b2_rows.to_broadcast([P, NX * D])),
                             (att_sb[:, :, :].rearrange("p a b -> p (a b)"), att.to_broadcast([P, 32])),
                             (gr_sb[:, :, :].rearrange("p a b -> p (a b)"), gat_rows.to_broadcast([P, 48])),
                             (hmask[:, :], consts[P:P + D, 0:NH])):
                sp.dma_start(dst, src).then_inc(S["const_loaded"], 16)
            for v in range(2):
                src = bass.AP(tensor=bias_rev.tensor, offset=bias_rev.offset, ap=[[1, P], [2 * P - 1, NH], [1, P]])
                sp.dma_start(rb_sb[:, v, :, :], src).then_inc(S["const_loaded"], 16)
            sp.sem_inc(S["eo_free"], 1)
            with sp.Fori(0, SEQS) as s:
                sp.wait_ge(S["rows_ready"], s + 1)
                sp.dma_start(node_rows.rearrange("(b p) f -> p b f", p=P)[:, bass.ds(s * WIN, WIN), :], rows_sb[:, bass.ds(s * WIN, WIN), :]).then_inc(S["rows_out"], 16)
                sp.wait_ge(S["eo_ready"], s + 2)
                sp.dma_start(expert_out.rearrange("(b p) f -> p b f", p=P)[:, bass.ds(s * WIN, WIN), :], eo[:, :, :, :].rearrange("p w e d -> p w (e d)")).then_inc(S["eo_out"], 16)
                sp.wait_ge(S["eo_out"], s * 16 + 16)
                sp.sem_inc(S["eo_free"], 1)
            sp.wait_ge(S["scat_a"], 16 * NS * (NB + 1))
            sp.wait_ge(S["scat_b"], 16 * NS * (NB + 1))
            sp.wait_ge(S["sorted_read"], 1)
            sp.dma_start(big_i[:, :], edge_list.rearrange("(p t) a -> p (t a)", p=P)).then_inc(S["list_loaded"], 16)
            sp.wait_ge(S["eo_out"], 16 * SEQS)
            with sp.Fori(0, NB // GB // 2) as i:
                for k, loaded in ((0, "eb_a"), (1, "eb_b")):
                    sp.wait_ge(S["eb_used"], i * 2 + k + 1)
                    sp.dma_start(eb[:, k, :, :, :].rearrange("p b e d -> p b (e d)"),
                                 expert_out.rearrange("(b p) f -> p b f", p=P)[:, bass.ds((i * 2 + k) * GB, GB), :]).then_inc(S[loaded], 16)
            sp.wait_ge(S["out_ready"], 1)
            for w in range(WIN - 1):
                sp.dma_start(out[:, w * P + SHIFT:(w + 1) * P + SHIFT, :].rearrange("s p d -> p s d"), h_sb[:, w:NB:WIN, :]).then_inc(S["out_done"], 16)
            sp.dma_start(out[:, SEQ - SHIFT:SEQ, :].rearrange("s p d -> p s d"), h_sb[0:SHIFT, WIN - 1:NB:WIN, :]).then_inc(S["out_done"], 16)
            sp.dma_start(out[:, 0:SHIFT, :].rearrange("s p d -> p s d"), h_sb[SHIFT:P, WIN - 1:NB:WIN, :]).then_inc(S["out_done"], 16)
            sp.wait_ge(S["out_done"], 16 * (WIN + 1))

        @block.gpsimd
        def _(gp):
            def gather_tokens(w):
                gp.indirect_dma_start(emb_now[:, w, :], None, emb, bass.IndirectOffsetOnAxis(ap=tok_now[:, w:w + 1], axis=0)).then_inc(S["emb_gathered"], 16)
            gp.wait_ge(S["const_ready"], 1)
            for k, scattered in ((0, "scat_a"), (1, "scat_b")):
                gp.dma_start(edge_list.rearrange("(p t) a -> p (t a)", p=P)[:, k * LC // 2:(k + 1) * LC // 2],
                             rows_sb[:, :, :].rearrange("p a b -> p (a b)")[:, 0:LC // 2].bitcast(i32)).then_inc(S[scattered], 16 * NS)
            gp.wait_ge(S["scat_a"], 16 * NS)
            gp.wait_ge(S["scat_b"], 16 * NS)
            gp.wait_ge(S["tok_now_ready"], 1)
            for w in range(WIN):
                gather_tokens(w)
            with gp.Fori(0, SEQS) as s:
                gp.wait_ge(S["tok_now_ready"], s + 2)
                apart(gp)
                for w in range(WIN):
                    gather_tokens(w)
                for w in range(WIN):
                    for b, ready, scattered in ((0, "addr_a", "scat_a"), (1, "addr_b", "scat_b")):
                        gp.wait_ge(S[ready], s * WIN + w + 1)
                        apart(gp)
                        for j in range(NS):
                            gp.indirect_dma_start(edge_list, bass.IndirectOffsetOnAxis(ap=addr_i[:, b, j:j + 1], axis=0), pay_now[:, b, j:j + 1], None).then_inc(S[scattered], 16)

            def gather_nodes(c, k, first, lap):
                if first and not 0 <= c < NCH + 2:
                    return
                gp.wait_ge(S["src_ready"], c + 1)
                if not (first and c < SL):
                    gp.wait_ge(S["sums_mm"], c + 1 - SL)
                apart(gp)
                for j in range(CH):
                    gp.indirect_dma_start(nodes[:, k, j, :], None, node_rows, bass.IndirectOffsetOnAxis(ap=src_now[:, k, j:j + 1], axis=0)).then_inc(gathered[k], 16)

            gp.wait_ge(S["rows_out"], 16 * SEQS)
            chunks(gp, gather_nodes)

        @block.vector
        def _(dve):
            v = nc.vector
            do = Steps(dve, "dve_step", 0, None, 0)
            dve.wait_ge(S["ids_loaded"], 16)
            do(v.tensor_copy(xf[:, 0:SEQ - SHIFT], xi[:, SHIFT:SEQ]))
            v.tensor_copy(xf[:, SEQ - SHIFT:SEQ], xi[:, 0:SHIFT]).then_inc(S["tok_T"], 1)
            dve.wait_ge(S["const_loaded"], 16 * consts_in)
            v.tensor_copy(iota_b[:, :], iota_f)
            v.tensor_copy(before_b[:, :], upper)
            v.tensor_copy(ones_b[:, :], ones)
            v.tensor_tensor(notbefore_b[:, :], ones, upper, ALU.subtract)
            v.tensor_scalar(bigi_b[:, :], ident, BIG, None, ALU.mult)
            v.memset(zeros_b[:, :], 0.0)
            v.tensor_scalar(rb_sb[0:SHIFT, 1, :, 0:SHIFT], rb_sb[0:SHIFT, 1, :, 0:SHIFT], -100.0, None, ALU.add)
            v.tensor_scalar(rb_sb[SHIFT:P, 1, :, SHIFT:P], rb_sb[SHIFT:P, 1, :, SHIFT:P], -100.0, None, ALU.add)
            v.memset(tok_i[:, :, SEQS:], 0)
            v.memset(xT[D:D + 1, :], 1.0)
            v.memset(oT[D:D + 1, :], 1.0)
            v.memset(xT2[D:D + 1, :, :], 1.0)
            v.memset(v1[:, :, :, HD:HD + 1], 1.0)
            for h in range(NX):
                v.tensor_tensor(sel_b[:, h, :], ident[0:8, h:h + 1].to_broadcast([8, P]), ident[0:8, h + NX:h + NX + 1].to_broadcast([8, P]), ALU.add)
            v.memset(rows_sb[:, :, :].rearrange("p a b -> p (a b)")[:, 0:LC].bitcast(i32), EMPTY).then_inc(S["const_ready"], 1)
            dve.wait_ge(S["const_ready"], 1)
            dve.wait_ge(S["edges_loaded"], 32)
            tmp_i = h_sb[:, 0:NT // D, :].rearrange("p a b -> p (a b)").bitcast(i32)
            for ids in (big_i[:, 0:NT], pay_i[:, 0:NT]):
                do(v.tensor_scalar(tmp_i, ids, float(SEQ - SHIFT), None, ALU.add))
                do(v.tensor_single_scalar(tmp_i, tmp_i, SEQ - 1, ALU.bitwise_and))
                do(v.tensor_scalar(ids, ids, -SEQ, None, ALU.bitwise_and))
                do(v.tensor_tensor(ids, ids, tmp_i, ALU.bitwise_or))
            do(v.tensor_scalar(tmp_i, big_i[:, 0:NT], P - 1, 14, ALU.bitwise_and, ALU.logical_shift_left))
            do(v.tensor_tensor(pay_i[:, 0:NT], pay_i[:, 0:NT], tmp_i, ALU.bitwise_or))
            do(v.tensor_scalar(big_i[:, 0:NT], big_i[:, 0:NT], 7, None, ALU.logical_shift_right))
            do(v.tensor_copy(big_f[:, 0:NT], big_i[:, 0:NT]))
            dve.wait_ge(S["tok_ready"], 1)
            do(v.tensor_copy(tok_i[:, :, 0:SEQS], bank_x[:, 0:WIN * SEQS].rearrange("p (w s) -> p w s", w=WIN)))
            dve.wait_ge(S["bias_mm"], 1)
            for v2 in range(4):
                do(v.tensor_copy(rb_sb[:, v2 // 2, 4 * (v2 % 2):4 * (v2 % 2) + 4, :], psum[2 + v2][:, :].rearrange("p (h k) -> p h k", h=4)))
            with dve.Fori(0, HIST_IT) as i:
                for g in range(8):
                    dve.wait_ge(S["hist_added"], i * 8 + g + 1)
                    for j in range(CH):
                        last = v.tensor_scalar(oh[:, g % 4, j, :], iota_b[:, :], big_f[:, one(i * 32 + g * 4 + j)], None, ALU.is_equal)
                    last.then_inc(S["hist_oh"], 1)
            dve.wait_ge(S["hist_done"], 1)
            do(v.tensor_copy(hist[:, 0:4, :].rearrange("p s b -> p (s b)"), count_ps[0][:, :]))
            do(v.tensor_copy(hist[:, 4:8, :].rearrange("p s b -> p (s b)"), count_ps[1][:, :]))
            do(v.tensor_reduce(rowa[:, :], hist[:, :, :].rearrange("p s b -> p b s"), AX.X, ALU.add))
            do(v.tensor_scalar(rowi[:, :], rowa[:, :], float(CE - 1), None, ALU.add))
            do(v.tensor_scalar(rowi[:, :], rowi[:, :], 9, None, ALU.logical_shift_right))
            do(v.tensor_copy(rowa[:, :], rowi[:, :]))
            do(v.tensor_tensor(rowb[:, :], rowa[:, :], ident, ALU.mult))
            do(v.tensor_reduce(colv[:, 0:1], rowb[:, :], AX.X, ALU.add))
            v.tensor_scalar(rowb[:, :], ones, colv[:, 0:1], None, ALU.mult).then_inc(S["base_mm"], 1)
            dve.wait_ge(S["base_row"], 1)
            do(v.tensor_copy(rowa[:, :], bank_x[:, 0:P]))
            do(v.tensor_tensor(rowb[:, :], rowa[:, :], ident, ALU.mult))
            do(v.tensor_reduce(colv[:, 1:2], rowb[:, :], AX.X, ALU.add))
            do(v.tensor_tensor(colv[:, 2:3], colv[:, 0:1], colv[:, 1:2], ALU.add))
            v.tensor_scalar(cmp_b[:, :], chunk_iota, colv[:, 2:3], None, ALU.is_ge).then_inc(S["chunk_cmp"], 1)
            do(v.tensor_scalar(rowa[:, :], rowa[:, :], float(CE), None, ALU.mult))
            for k in range(NS):
                do(v.tensor_tensor(rowb[:, :], hist[:, k, :], rowa[:, :], ALU.add))
                do(v.tensor_copy(hist[:, k, :], rowa[:, :]))
                do(v.tensor_copy(rowa[:, :], rowb[:, :]))
            dve.sem_inc(S["base_set"], 1)
            dve.wait_ge(S["chunk_sum"], 1)
            do(v.tensor_copy(block_of[:, 0:512], bank_x[:, :]))
            do(v.tensor_copy(block_of[:, 512:LC // CH], bank_y[:, 0:LC // CH - 512]))
            pre = do.n

            dve.sem_inc(S["eo_ready"], 1)

            def stats(src, which, w):
                do(v.bn_stats(stat[:, w, :], src))
                apart(dve)
                do(v.bn_aggr(mv[:, which, w, :], stat[:, w, :]))

            def root(which):
                y = rstd[:, which, :]
                var = mv[:, which, :, 1:2].rearrange("p w a -> p (w a)")
                do(v.tensor_scalar(var, var, EPS, None, ALU.add))
                do(v.tensor_single_scalar(y.bitcast(i32), var.bitcast(i32), 1, ALU.logical_shift_right))
                do(v.tensor_scalar(y.bitcast(i32), y.bitcast(i32), -1.0, float(0x5F3759DF), ALU.mult, ALU.add))
                for _ in range(3):
                    do(v.tensor_tensor(root_t[:, :], y, y, ALU.mult))
                    do(v.scalar_tensor_tensor(root_t[:, :], root_t[:, :], -0.5, var, ALU.mult, ALU.mult))
                    do(v.scalar_tensor_tensor(y, root_t[:, :], 1.5, y, ALU.add, ALU.mult))

            def embed(s):
                dve.wait_ge(S["emb_gathered"], s * (16 * WIN) + 16 * WIN)
                apart(dve)
                do(v.tensor_tensor(h_sb[:, bass.ds(s * WIN, WIN), :], emb_now[:, :, :], pe_sb[:, :, :], ALU.add))
                v.tensor_copy(tok_now[:, :].rearrange("p (w a) -> p w a", a=1), tok_i[:, :, one(s + 1)]).then_inc(S["tok_now_ready"], 1)
                for w in range(WIN):
                    stats(h_sb[:, one(s * WIN + w), :].rearrange("p a d -> p (a d)"), 0, w)
                root(0)

            def normed(n, w):
                v.tensor_scalar(xn[:, :], h_sb[:, one(n), :].rearrange("p a d -> p (a d)"), mv[:, 0, w, 0:1], rstd[:, 0, w:w + 1], ALU.subtract, ALU.mult).then_inc(S["xn_ready"], 1)

            def queries(n, w):
                dve.wait_ge(S["qkv_mm"], n + 1)
                dve.wait_ge(S["kT_ready"], n + 1)
                v.tensor_copy(v1[:, w % 2, :, 0:HD], bank_x[:, 2 * P:2 * P + D].rearrange("p (h d) -> p h d", h=NH))
                v.tensor_tensor(qm[:, :, :], bank_x[0:D, 0:P].rearrange("p (a q) -> p a q", a=1).to_broadcast([D, NH, P]),
                                hmask[:, :].rearrange("p (h a) -> p h a", a=1).to_broadcast([D, NH, P]), ALU.mult).then_inc(S["q_v_ready"], 1)

            def onehots(n, g):
                dve.wait_ge(S["counted"], n * 4 + g + 1)
                for j in range(CH):
                    last = v.tensor_scalar(oh[:, g % 2, j, :], iota_b[:, :], big_f[:, one(n * 16 + g * 4 + j)], None, ALU.is_equal)
                last.then_inc(S["oh_ready"], 1)

            def ranks(n, g):
                b = g // 2
                dve.wait_ge(S["ranked"], n * 4 + g + 1)
                for j in range(CH):
                    last = v.tensor_tensor_reduce(out=junk[:, j, :], in0=oh[:, g % 2, j, :], in1=count_ps[g % 2][:, j * P:(j + 1) * P], scale=1.0, scalar=0.0,
                                                  op0=ALU.mult, op1=ALU.add, accum_out=pos_f[:, b, (g % 2) * CH + j:(g % 2) * CH + j + 1])
                last.then_inc(S["ranks_read"], 1)
                dve.wait_ge(S["ranks_read"], n * 4 + g + 1)
                if g % 2:
                    do(v.tensor_copy(pos_i[:, b, :], pos_f[:, b, :]))
                    do(v.tensor_scalar(lo_i[:, b, :], pos_i[:, b, :], P - 1, None, ALU.bitwise_and))
                    do(v.tensor_scalar(pos_i[:, b, :], pos_i[:, b, :], 7, None, ALU.logical_shift_right))
                    scattered = S["scat_b" if b else "scat_a"]
                    dve.wait_ge(scattered, (n + 1) * (16 * NS))
                    do(v.scalar_tensor_tensor(addr_i[:, b, :], lo_i[:, b, :], float(LC), pos_i[:, b, :], ALU.mult, ALU.add))
                    apart(dve)
                    v.tensor_copy(pay_now[:, b, :], pay_i[:, bass.ds(n * 16 + b * NS, NS)]).then_inc(S["addr_b" if b else "addr_a"], 1)

            def window(n, w, s, front, back, tail):
                if front:
                    if w == WIN - 1:
                        embed(s + 1)
                    normed(n + 1, (w + 1) % WIN)
                    onehots(n, 0)
                    onehots(n, 1)
                    dve.wait_ge(S["s_mm"], n + 1)
                    if back:
                        dve.wait_ge(S["probs"], n)
                    apart(dve)
                    for h in range(NH):
                        last = v.tensor_tensor_reduce(out=ss[:, h, :], in0=rb_sb[:, w // (WIN - 1), h, :], in1=psum[2 + h // 4][:, (h % 4) * P:(h % 4 + 1) * P], scale=1.0,
                                                      scalar=-3.0e38, op0=ALU.add, op1=ALU.max, accum_out=nmax[:, h:h + 1])
                    do(last)
                    v.tensor_scalar(nmax[:, :], nmax[:, :], -1.0, None, ALU.mult).then_inc(S["nmax_ready"], 1)
                    ranks(n, 0)
                    onehots(n, 2)
                if back:
                    dve.wait_ge(S["o_mm"], n)
                    o_ps = bank_y[:, 0:NH * (HD + 1)].rearrange("p (h d) -> p h d", h=NH)
                    do(v.reciprocal(rden[:, :].rearrange("p (h a) -> p h a", a=1), o_ps[:, :, HD:HD + 1]))
                    v.tensor_tensor(on[:, :].rearrange("p (h d) -> p h d", h=NH), o_ps[:, :, 0:HD],
                                    rden[:, :].rearrange("p (h a) -> p h a", a=1).to_broadcast([P, NH, HD]), ALU.mult).then_inc(S["o_ready"], 1)
                if front:
                    ranks(n, 1)
                    onehots(n, 3)
                    queries(n + 1, w + 1)
                    ranks(n, 2)
                if back:
                    tile = h_sb[:, one(n - 1), :].rearrange("p a d -> p (a d)")
                    dve.wait_ge(S["proj_mm"], n)
                    v.tensor_tensor(tile, tile, bank_y[:, 384:384 + D], ALU.add).then_inc(S["resid_done"], 1)
                    dve.wait_ge(S["resid_done"], n)
                    apart(dve)
                    stats(tile, 1, (w - 1) % WIN)
                if tail and w == 0:
                    root(1)
                    for k in range(WIN):
                        last = v.tensor_scalar(xn2[:, k, :], h_sb[:, one(s * WIN - WIN + k), :].rearrange("p a d -> p (a d)"), mv[:, 1, k, 0:1], rstd[:, 1, k:k + 1], ALU.subtract, ALU.mult)
                    last.then_inc(S["xn2_ready"], 1)
                if front:
                    ranks(n, 3)
                if tail and w == 0:
                    dve.wait_ge(S["gat_mm"], s)
                    rows = rows_sb[:, bass.ds(s * WIN - WIN, WIN), :]
                    apart(dve)
                    do(v.tensor_copy(rows[:, :, 0:16], psum[5][:, 0:64].rearrange("p (w f) -> p w f", w=WIN)))
                    for k, col in ((0, 16), (1, 28)):
                        do(v.tensor_tensor(gt[:, :, :], rows[:, :, 0:16], att_sb[:, k:k + 1, :].to_broadcast([P, WIN, 16]), ALU.mult))
                        do(v.tensor_reduce(rows[:, :, col:col + NX], gt[:, :, :].rearrange("p w (h k) -> p w h k", h=NX), AX.X, ALU.add))
                    apart(dve)
                    do(v.tensor_copy(ab16[:, :, :], rows[:, :, 16:20]))
                    apart(dve)
                    do(v.tensor_copy(rows[:, :, 20:24], ab16[:, :, :]))
                    v.tensor_tensor(rows[:, :, 24:28], rows[:, :, 16:20], rows[:, :, 20:24], ALU.subtract).then_inc(S["rows_ready"], 1)
                if tail and w == WIN - 1:
                    dve.wait_ge(S["eo_mm"], s)
                    dve.wait_ge(S["eo_free"], s)
                    for e in range(NX):
                        src = psum[4 + e // 2][:, (e % 2) * 256:(e % 2) * 256 + 256].rearrange("p (w d) -> p w d", w=WIN)
                        last = v.tensor_tensor(eo[:, :, e, :], src, b2_sb[:, e:e + 1, :].to_broadcast([P, WIN, D]), ALU.add)
                    last.then_inc(S["eo_ready"], 1)

            v.tensor_copy(tok_now[:, :].rearrange("p (w a) -> p w a", a=1), tok_i[:, :, 0:1]).then_inc(S["tok_now_ready"], 1)
            embed(0)
            normed(0, 0)
            queries(0, 0)
            for w in range(WIN):
                window(w, w, 0, True, w > 0, False)
            pre = do.n - DVE_SEQ
            with dve.Fori(1, SEQS) as s:
                do = Steps(dve, "dve_step", pre, s, DVE_SEQ)
                for w in range(WIN):
                    window(s * WIN + w, w, s, True, True, True)
                assert do.n == DVE_SEQ, do.n
            do = Steps(dve, "dve_step", pre + SEQS * DVE_SEQ, None, 0)
            for w in range(WIN):
                window(NB + w, w, SEQS, False, w == 0, True)

            do = Steps(dve, "dve_late", 0, None, 0)
            v.memset(state[:, NB:NB + 1, :], 0.0)
            v.memset(acc[:, NB:NB + 1, :, :], 0.0)
            v.tensor_copy(state[:, 0:NB, 0:4], rows_sb[:, :, 16:20])
            v.tensor_copy(state[:, 0:NB, 8:12], rows_sb[:, :, 28:32])
            do(v.tensor_tensor(state[:, 0:NB, 4:8], rows_sb[:, :, 16:20], rows_sb[:, :, 28:32], ALU.add))
            do(v.scalar_tensor_tensor(state[:, 0:NB, 4:8], state[:, 0:NB, 4:8], 0.2, state[:, 0:NB, 4:8], ALU.mult, ALU.max))
            v.memset(acc[:, 0:NB, :, 0:1], 1.0)
            v.tensor_copy(acc[:, 0:NB, :, 1:NX + 1], rows_sb[:, :, 0:16].rearrange("p b (h k) -> p b h k", h=NX)).then_inc(S["state_ready"], 1)
            dve.wait_ge(S["state_ready"], 1)
            dve.sem_inc(S["sorted_read"], 1)
            dve.wait_ge(S["list_loaded"], 16)
            do(v.tensor_single_scalar(pay_i[:, :], big_i[:, :], 14, ALU.logical_shift_right))
            do(v.tensor_copy(big_f[:, :], pay_i[:, :]))
            v.tensor_single_scalar(big_i[:, :], big_i[:, :], (1 << 14) - 1, ALU.bitwise_and).then_inc(S["list_ready"], 1)

            def hots(c, k):
                for j in range(CH):
                    last = v.tensor_scalar(hot[:, k % SL, j, :], iota_f, big_f[:, one(c * CH + j)], None, ALU.is_equal)
                last.then_inc(S["hot_ready"], 1)

            def block_number(c):
                return dve.value_load(block_of[0:1, one(c)], min_val=0, max_val=NB)

            numbers = {}

            def chunk(c, k, first, lap):
                lead, logits, weigh, close = (not first or c - back in range(NCH) for back in range(4))
                e2, w2 = (k - 1) % 2, k % 2
                if k == 0:
                    numbers.clear()
                if lead:
                    b = numbers[k] = block_number(c)
                    st = state[:, one(b), :].rearrange("p a f -> p (a f)")
                    hots(c + 2, k + 2)
                    v.tensor_copy(dst_in[:, w2, 0:4], st[:, 8:12])
                    dve.wait_ge(S["top_mm"], c + 1)
                    v.tensor_reduce(top[:, :], four[:, :].rearrange("p (h e) -> p h e", h=NX), AX.X, ALU.max).then_inc(S["top_read"], 1)
                    dve.wait_ge(S["top_read"], c + 1)
                    v.scalar_tensor_tensor(st[:, 0:4], top[:, :], -BIG, st[:, 0:4], ALU.add, ALU.max).then_inc(S["top_kept"], 1)
                le = lg[:, e2, :, :]
                if logits:
                    dve.wait_ge(S["edge_out"], c)
                    v.tensor_tensor(le, nodes[:, (k - 1) % SL, :, 16:20], dst_e[:, e2, :, 0:4], ALU.add).then_inc(S["lg_1"], 1)
                if lead:
                    dve.wait_ge(S["top_kept"], c + 1)
                    v.tensor_tensor(score[:, w2, :], st[:, 0:4], st[:, 8:12], ALU.add).then_inc(S["score_ready"], 1)
                if logits:
                    dve.wait_ge(S["lg_1"], c)
                    v.scalar_tensor_tensor(le, le, 0.2, le, ALU.mult, ALU.max).then_inc(S["lg_2"], 1)
                if lead:
                    dve.wait_ge(S["score_ready"], c + 1)
                    v.scalar_tensor_tensor(dst_in[:, w2, 4:8], score[:, w2, :], 0.2, score[:, w2, :], ALU.mult, ALU.max).then_inc(S["dst_ready"], 1)
                if logits:
                    dve.wait_ge(S["lg_2"], c)
                    v.tensor_tensor(le, le, dst_e[:, e2, :, 4:8], ALU.subtract).then_inc(S["lg_3"], 1)
                if lead:
                    dve.wait_ge(S["dst_ready"], c + 1)
                    v.tensor_tensor(fade[:, k % 4, :], st[:, 4:8], dst_in[:, w2, 4:8], ALU.subtract).then_inc(S["fade_in"], 1)
                if logits:
                    dve.wait_ge(S["lg_3"], c)
                    v.tensor_scalar(le, le, 20.0, None, ALU.min).then_inc(S["lg_ready"], 1)
                if lead:
                    dve.wait_ge(S["fade_in"], c + 1)
                    v.tensor_scalar(st[:, 4:8], dst_in[:, w2, 4:8], 1.0, None, ALU.mult).then_inc(S["shift_kept"], 1)
                if close:
                    bc = numbers[k - 3] if k >= 3 and k - 3 in numbers else block_number(c - 3)
                    ac = acc[:, one(bc), :, :].rearrange("p a h f -> p (a h) f")
                    if not first or c > 3:
                        dve.wait_ge(S["sums_kept"], c - 3)
                    dve.wait_ge(S["fade_ready"], c - 2)
                    v.tensor_tensor(ac, ac, fade[:, (k - 3) % 4, :].rearrange("p (h a) -> p h a", a=1).to_broadcast([P, NX, NX + 1]), ALU.mult).then_inc(S["faded"], 1)
                    dve.wait_ge(S["sums_mm"], c - 2)
                if weigh:
                    m = msg[:, (k - 2) % 4, :, :, :]
                    dve.wait_ge(S["weights"], c - 1)
                    v.tensor_tensor(m[:, :, :, 1:NX + 1], nodes[:, (k - 2) % SL, :, 0:16].rearrange("p j (h f) -> p j h f", h=NX), m[:, :, :, 0:1].to_broadcast([P, CH, NX, NX]),
                                    ALU.mult).then_inc(S["msg_ready"], 1)
                if close:
                    dve.wait_ge(S["faded"], c - 2)
                    v.tensor_tensor(ac, ac, psum[7][:, 0:20].rearrange("p (h f) -> p h f", h=NX), ALU.add).then_inc(S["sums_kept"], 1)
                if lead:
                    dve.wait_ge(S["shift_kept"], c + 1)

            for k in range(2):
                hots(k, k)
            chunks(dve, chunk)
            dve.wait_ge(S["sums_kept"], NCH)

            do = Steps(dve, "dve_end", 0, None, 0)
            def wide(ap):
                return ap.rearrange("p (b a) -> p b a", a=1)
            dve.sem_inc(S["eb_used"], 2)
            w4 = acc[:, 0:NB, :, 0:1].rearrange("p b h a -> p b (h a)")
            do(v.tensor_scalar(sc[:, :, :], w4, 1e-16, None, ALU.add))
            do(v.reciprocal(sc[:, :, :], sc[:, :, :]))
            ag4 = ag[:, :, :].rearrange("p b (h k) -> p b h k", h=NX)
            for h in range(NX):
                last = do(v.tensor_tensor(ag4[:, :, h, :], acc[:, 0:NB, h, 1:NX + 1], sc[:, :, h:h + 1].to_broadcast([P, NB, NX]), ALU.mult))
            do(v.tensor_tensor(ag[:, :, :], ag[:, :, :], gr_sb[:, 0:1, :].to_broadcast([P, NB, 16]), ALU.add))
            do(v.tensor_reduce(g1[:, :], ag[:, :, :], AX.X, ALU.add))
            do(v.tensor_scalar(g1[:, :], g1[:, :], 1.0 / 16, None, ALU.mult))
            do(v.tensor_tensor(ag[:, :, :], ag[:, :, :], wide(g1[:, :]).to_broadcast([P, NB, 16]), ALU.subtract))
            do(v.tensor_tensor(ag2[:, :, :], ag[:, :, :], ag[:, :, :], ALU.mult))
            do(v.tensor_reduce(g1[:, :], ag2[:, :, :], AX.X, ALU.add))
            v.tensor_scalar(g1[:, :], g1[:, :], 1.0 / 16, EPS, ALU.mult, ALU.add).then_inc(S["gvar_ready"], 1)
            dve.wait_ge(S["grstd"], 1)
            do(v.tensor_tensor(ag[:, :, :], ag[:, :, :], wide(g1[:, :]).to_broadcast([P, NB, 16]), ALU.mult))
            do(v.tensor_tensor(ag[:, :, :], ag[:, :, :], gr_sb[:, 1:2, :].to_broadcast([P, NB, 16]), ALU.mult))
            do(v.tensor_tensor(ag[:, :, :], ag[:, :, :], gr_sb[:, 2:3, :].to_broadcast([P, NB, 16]), ALU.add))
            do(v.tensor_reduce(sc[:, :, :], ag[:, :, :].rearrange("p b (h k) -> p b k h", h=NX), AX.X, ALU.add))
            do(v.tensor_scalar(sc[:, :, :], sc[:, :, :], 0.25, None, ALU.mult))
            do(v.memset(wins[:, :, :], 0.0))
            for e in range(NX):
                for f in range(e + 1, NX):
                    do(v.tensor_tensor(wide(g1[:, :]), sc[:, :, e:e + 1], sc[:, :, f:f + 1], ALU.is_ge))
                    do(v.tensor_tensor(wins[:, :, e:e + 1], wins[:, :, e:e + 1], wide(g1[:, :]), ALU.add))
                    do(v.tensor_scalar(g1[:, :], g1[:, :], -1.0, 1.0, ALU.mult, ALU.add))
                    do(v.tensor_tensor(wins[:, :, f:f + 1], wins[:, :, f:f + 1], wide(g1[:, :]), ALU.add))
            do(v.tensor_reduce(g1[:, :], sc[:, :, :], AX.X, ALU.max))
            do(v.tensor_scalar(gate[:, :, :], wins[:, :, :], 2.0, None, ALU.is_equal))
            do(v.tensor_tensor(sc[:, :, :], sc[:, :, :], gate[:, :, :], ALU.mult))
            do(v.tensor_reduce(g2[:, :], sc[:, :, :], AX.X, ALU.add))
            v.tensor_tensor(g2[:, :], g2[:, :], g1[:, :], ALU.subtract).then_inc(S["gate_in"], 1)
            dve.wait_ge(S["gate_exp"], 1)
            do(v.tensor_scalar(g1[:, :], g2[:, :], 1.0, None, ALU.add))
            do(v.reciprocal(g1[:, :], g1[:, :]))
            do(v.tensor_tensor(g2[:, :], g2[:, :], g1[:, :], ALU.mult))
            do(v.tensor_tensor(gate[:, :, :], gate[:, :, :], wide(g2[:, :]).to_broadcast([P, NB, NX]), ALU.mult))
            do(v.tensor_scalar(wins[:, :, :], wins[:, :, :], 3.0, None, ALU.is_equal))
            do(v.tensor_tensor(wins[:, :, :], wins[:, :, :], wide(g1[:, :]).to_broadcast([P, NB, NX]), ALU.mult))
            do(v.tensor_tensor(gate[:, :, :], gate[:, :, :], wins[:, :, :], ALU.add))
            with dve.Fori(0, NB // GB // 2) as i:
                do = Steps(dve, "dve_mix", 0, i, DVE_MIX)
                for k, loaded in ((0, "eb_a"), (1, "eb_b")):
                    dve.wait_ge(S[loaded], i * 16 + 16)
                    blocks = bass.ds((i * 2 + k) * GB, GB)
                    for e in range(NX):
                        last = v.tensor_tensor(eb[:, k, :, e, :], eb[:, k, :, e, :], gate[:, blocks, e:e + 1].to_broadcast([P, GB, D]), ALU.mult)
                    do(last)
                    do(v.tensor_tensor(eb[:, k, :, 0:2, :], eb[:, k, :, 0:2, :], eb[:, k, :, 2:4, :], ALU.add))
                    do(v.tensor_tensor(h_sb[:, blocks, :], h_sb[:, blocks, :], eb[:, k, :, 0, :], ALU.add))
                    do(v.tensor_tensor(h_sb[:, blocks, :], h_sb[:, blocks, :], eb[:, k, :, 1, :], ALU.add))
                    dve.sem_inc(S["eb_used"], 1)
                assert do.n == DVE_MIX, do.n
            dve.sem_inc(S["out_ready"], 1)

        @block.scalar
        def _(act):
            a = nc.scalar

            def turned_x(n):
                act.wait_ge(S["xT_mm"], n + 1)
                a.activation(xT[0:D, :], bank_x[0:D, 384:384 + P], ACT.Copy).then_inc(S["xT_ready"], 1)

            def keys(n):
                act.wait_ge(S["qkv_mm"], n + 1)
                a.activation(kT[:, :], bank_x[0:D, P:2 * P], ACT.Copy).then_inc(S["kT_ready"], 1)

            def window(n, w, s, front, back, tail):
                if front:
                    turned_x(n + 1)
                if back:
                    act.wait_ge(S["pT_mm"], n)
                    for k in range(2):
                        last = a.activation(prT[:, 4 * k:4 * k + 4, :], psum[4 + k][:, :].rearrange("p (h k) -> p h k", h=4), ACT.Copy)
                    last.then_inc(S["pT_ready"], 1)
                if front:
                    act.wait_ge(S["nmax_ready"], n + 1)
                    for h in range(NH):
                        last = a.activation(pr[:, h, :], ss[:, h, :], ACT.Exp, bias=nmax[:, h:h + 1])
                    last.then_inc(S["probs"], 1)
                    keys(n + 1)
                if back:
                    act.wait_ge(S["oT_mm"], n)
                    a.activation(oT[0:D, :], bank_y[0:D, 128:256], ACT.Copy).then_inc(S["oT_ready"], 1)
                if tail and w == 0:
                    act.wait_ge(S["xT2_mm"], s)
                    a.activation(xT2[0:D, :, :].rearrange("p w k -> p (w k)"), psum[4][0:D, :], ACT.Copy).then_inc(S["xT2_ready"], 1)
                if tail and w in (1, 2):
                    act.wait_ge(S["hid_mm"], s * 2 + w - 2)
                    for k in range(2):
                        last = a.activation(hh[:, (w - 1) * 2 + k, :], psum[4 + k][:, :], ACT.Gelu)
                    last.then_inc(S["hid_ready"], 1)

            turned_x(0)
            keys(0)
            windows(act, window)

            AHEAD = 6

            def sources(c, k):
                apart(act)
                a.activation(src_now[:, k % SL, :], big_i[:, bass.ds(c * CH, CH)], ACT.Copy).then_inc(S["src_ready"], 1)

            def turned(c, k):
                act.wait_ge(S["hotT_mm"], c + 1)
                a.activation(hotT[:, k % 2, :, :], psum[0][:, :], ACT.Copy)
                a.activation(hotT_b[:, k % 2, :, :], psum[0][:, :], ACT.Copy).then_inc(S["hotT_ready"], 1)
                act.wait_ge(S["halves_mm"], c + 1)
                a.activation(halves_b[:, k % 2, :], psum[1][0:8, :], ACT.Copy).then_inc(S["halves_ready"], 1)

            def chunk(c, k, first, lap):
                lead, logits = (not first or c - back in range(NCH) for back in range(2))
                if logits:
                    act.wait_ge(S["lg_ready"], c)
                    a.activation(msg[:, (k - 1) % 4, :, :, 0:1].rearrange("p j h a -> p (j h) a"), lg[:, (k - 1) % 2, :, :].rearrange("p j (h a) -> p (j h) a", a=1), ACT.Exp).then_inc(S["weights"], 1)
                if lead:
                    act.wait_ge(S["fade_in"], c + 1)
                    a.activation(fade[:, k % 4, :], fade[:, k % 4, :], ACT.Exp).then_inc(S["fade_ready"], 1)
                    act.wait_ge(S["edge_mm"], c + 1)
                    a.activation(dst_e[:, k % 2, :, :], psum[6][:, 0:8 * CH].rearrange("p (j f) -> p j f", j=CH), ACT.Copy).then_inc(S["edge_out"], 1)
                    turned(c + 2, k + 2)
                    if not first or c + AHEAD < NCH + 2:
                        sources(c + AHEAD, k + AHEAD)

            act.wait_ge(S["list_ready"], 1)
            for k in range(AHEAD):
                sources(k, k)
            for k in range(2):
                turned(k, k)
            chunks(act, chunk)
            act.wait_ge(S["gvar_ready"], 1)
            a.activation(g1[:, :], g1[:, :], ACT.Ln).then_inc(S["glog"], 1)
            act.wait_ge(S["glog"], 1)
            a.activation(g1[:, :], g1[:, :], ACT.Exp, scale=-0.5).then_inc(S["grstd"], 1)
            act.wait_ge(S["gate_in"], 1)
            a.activation(g2[:, :], g2[:, :], ACT.Exp).then_inc(S["gate_exp"], 1)

        @block.tensor
        def _(pe):
            t = nc.tensor
            pe.wait_ge(S["tok_T"], 1)
            pe.wait_ge(S["const_loaded"], 16 * consts_in)
            pe.wait_ge(S["const_ready"], 1)
            for w in range(WIN):
                last = t.transpose(bank_x[:, w * SEQS:(w + 1) * SEQS], xf[:, w * P:(w + 1) * P], ident[0:SEQS, 0:SEQS])
            last.then_inc(S["tok_ready"], 1)
            for v2 in range(4):
                last = t.matmul(psum[2 + v2][:, :], flip, rb_sb[:, v2 // 2, 4 * (v2 % 2):4 * (v2 % 2) + 4, :], start=True, stop=True)
            last.then_inc(S["bias_mm"], 1)
            for k in range(2):
                t.matmul(count_ps[k][:, :], ones_b[:, :], zeros_b[:, :], start=True, stop=True, skip_group_check=True)
            pe.sem_inc(S["hist_added"], 4)
            with pe.Fori(0, HIST_IT) as i:
                for g in range(8):
                    pe.wait_ge(S["hist_oh"], i * 8 + g + 1)
                    t.matmul(count_ps[g % 2][:, :], ones_b[:, :], oh[:, g % 4, :, :], start=False, stop=True, skip_group_check=True).then_inc(S["hist_added"], 1)
            t.transpose(bank_y[0:SEQS, 0:SEQS], xf[:, 0:SEQS], ident[0:SEQS, 0:SEQS]).then_inc(S["hist_done"], 1)
            pe.wait_ge(S["base_mm"], 1)
            t.matmul(bank_x[:, 0:P], rowb[:, :], upper, start=True, stop=True).then_inc(S["base_row"], 1)
            pe.wait_ge(S["chunk_cmp"], 1)
            t.matmul(bank_x[:, :], ones_b[:, :], cmp_b[:, 0:512], start=True, stop=True)
            t.matmul(bank_y[:, 0:LC // CH - 512], ones_b[:, :], cmp_b[:, 512:], start=True, stop=True).then_inc(S["chunk_sum"], 1)
            pe.wait_ge(S["base_set"], 1)
            for k in range(2):
                t.matmul(count_ps[k][:, :], ident, hist[:, 4 * k:4 * k + 4, :], start=True, stop=True, skip_group_check=True)

            pe.sem_inc(S["counted"], 2)

            def rank(n, g):
                pe.wait_ge(S["oh_ready"], n * 4 + g + 1)
                t.matmul(count_ps[g % 2][:, :], before_b[:, :], oh[:, g % 2, :, :], start=False, stop=True, skip_group_check=True).then_inc(S["ranked"], 1)

            def count(n, g):
                pe.wait_ge(S["ranks_read"], n * 4 + g + 1)
                t.matmul(count_ps[g % 2][:, :], notbefore_b[:, :], oh[:, g % 2, :, :], start=False, stop=True, skip_group_check=True).then_inc(S["counted"], 1)

            def turn_x(n):
                pe.wait_ge(S["xn_ready"], n + 1)
                apart(pe)
                t.transpose(bank_x[0:D, 384:384 + P], xn[:, :], ident).then_inc(S["xT_mm"], 1)

            def qkv(n):
                pe.wait_ge(S["xT_ready"], n + 1)
                t.matmul(bank_x[0:D, 0:P], qkvw_sb[:, 0:D], xT[:, :], start=True, stop=True)
                t.matmul(bank_x[0:D, P:2 * P], qkvw_sb[:, D:2 * D], xT[:, :], start=True, stop=True)
                t.matmul(bank_x[:, 2 * P:2 * P + D], xT[:, :], qkvw_sb[:, 2 * D:3 * D], start=True, stop=True).then_inc(S["qkv_mm"], 1)

            def window(n, w, s, front, back, tail):
                if front:
                    pe.wait_ge(S["q_v_ready"], n + 1)
                    turn_x(n + 1)
                    if back:
                        pe.wait_ge(S["nmax_ready"], n)
                    for h in range(NH):
                        last = t.matmul(psum[2 + h // 4][:, (h % 4) * P:(h % 4 + 1) * P], qm[:, h, :], kT[:, :], start=True, stop=True)
                    last.then_inc(S["s_mm"], 1)
                if back:
                    pe.wait_ge(S["probs"], n)
                    if tail:
                        if w == 0:
                            pe.wait_ge(S["eo_ready"], s)
                        if w == 1:
                            pe.wait_ge(S["rows_ready"], s)
                        if w > 1:
                            pe.wait_ge(S["hid_ready"], s * 2 + w - 3)
                    for h in range(NH):
                        last = t.transpose(psum[4 + h // 4][:, (h % 4) * P:(h % 4 + 1) * P], pr[:, h, :], ident)
                    last.then_inc(S["pT_mm"], 1)
                if front:
                    rank(n, 0)
                    rank(n, 1)
                    qkv(n + 1)
                if back:
                    pe.wait_ge(S["pT_ready"], n)
                    if tail or w > 1:
                        pe.wait_ge(S["resid_done"], n - 1)
                    for h in range(NH):
                        last = t.matmul(bank_y[:, h * (HD + 1):(h + 1) * (HD + 1)], prT[:, h, :], v1[:, (w - 1) % 2, h, :], start=True, stop=True)
                    last.then_inc(S["o_mm"], 1)
                if front:
                    count(n, 0)
                    rank(n, 2)
                if back:
                    pe.wait_ge(S["o_ready"], n)
                    apart(pe)
                    t.transpose(bank_y[0:D, 128:256], on[:, :], ident).then_inc(S["oT_mm"], 1)
                if front:
                    count(n, 1)
                    rank(n, 3)
                if back:
                    pe.wait_ge(S["oT_ready"], n)
                    t.matmul(bank_y[:, 384:384 + D], oT[:, :], projw_sb[:, :], start=True, stop=True).then_inc(S["proj_mm"], 1)
                if front:
                    count(n, 2)
                if tail:
                    if w == 0:
                        pe.wait_ge(S["xn2_ready"], s)
                        apart(pe)
                        for k in range(WIN):
                            last = t.transpose(psum[4][0:D, k * P:(k + 1) * P], xn2[:, k, :], ident)
                        last.then_inc(S["xT2_mm"], 1)
                    if w in (1, 2):
                        if not front:
                            pe.wait_ge(S["rows_ready" if w == 1 else "hid_ready"], s if w == 1 else s * 2 - 1)
                        for k in range(2):
                            last = t.matmul(psum[4 + k][:, :], w1_sb[:, (w - 1) * 2 + k, :], xT2[:, :, :], start=True, stop=True)
                        last.then_inc(S["hid_mm"], 1)
                    if w == WIN - 1:
                        pe.wait_ge(S["hid_ready"], s * 2)
                        for e in range(NX):
                            for k in range(WIN):
                                c = (e % 2) * 256 + k * D
                                last = t.matmul(psum[4 + e // 2][:, c:c + D], hh[:, e, k * P:(k + 1) * P], w2_sb[:, e, :], start=True, stop=True)
                        last.then_inc(S["eo_mm"], 1)
                if front:
                    count(n, 3)
                if tail and w == 0:
                    pe.wait_ge(S["xT2_ready"], s)
                    for k in range(WIN):
                        last = t.matmul(psum[5][:, k * 16:(k + 1) * 16], xT2[0:D, k, :], wg_sb[:, :], start=True, stop=True)
                    last.then_inc(S["gat_mm"], 1)

            turn_x(0)
            qkv(0)
            windows(pe, window)

            def turn(c, k, gathers):
                pe.wait_ge(S["hot_ready"], c + 1)
                for j in range(CH):
                    last = t.transpose(psum[0][:, j * P:(j + 1) * P], hot[:, k % SL, j, :], ident)
                last.then_inc(S["hotT_mm"], 1)
                pe.wait_ge(gathered[k % SL], gathers * (16 * CH))
                for j in range(CH):
                    last = t.transpose(psum[1][0:8, j * P:(j + 1) * P], nodes[:, k % SL, j, 20:28], ident)
                last.then_inc(S["halves_mm"], 1)

            def tops(c, k):
                pe.wait_ge(S["hotT_ready"], c + 1)
                pe.wait_ge(S["halves_ready"], c + 1)
                for h in range(NX):
                    t.matmul(psum[2 + h][:, :], bigi_b[:, :], hotT_b[:, k % 2, :, :], start=True, stop=False)
                    last = t.matmul(psum[2 + h][:, :], sel_b[:, h, :], halves_b[:, k % 2, :], start=False, stop=True)
                last.then_inc(S["top_mm"], 1)

            def chunk(c, k, first, lap):
                lead, _, sums = (not first or c - back in range(NCH) for back in range(3))
                if lead:
                    pe.wait_ge(S["top_read"], c + 1)
                    tops(c + 1, k + 1)
                    pe.wait_ge(S["dst_ready"], c + 1)
                    for j in range(CH):
                        last = t.matmul(psum[6][:, j * 8:(j + 1) * 8], hotT[:, k % 2, j, :], dst_in[:, k % 2, :], start=True, stop=True)
                    last.then_inc(S["edge_mm"], 1)
                    turn(c + 2, k + 2, lap + 1 + (k + 2) // SL)
                if sums:
                    pe.wait_ge(S["msg_ready"], c - 1)
                    if not first or c > 2:
                        pe.wait_ge(S["sums_kept"], c - 2)
                    for j in range(CH):
                        last = t.matmul(psum[7][:, 0:20], hot[:, (k - 2) % SL, j, :], msg[:, (k - 2) % 4, j, :, :], start=j == 0, stop=j == CH - 1)
                    last.then_inc(S["sums_mm"], 1)

            pe.wait_ge(S["state_ready"], 1)
            turn(0, 0, 1)
            tops(0, 0)
            turn(1, 1, 1)
            chunks(pe, chunk)


def kernel(**inputs):
    import concourse.bacc as bacc
    from concourse.bass_utils import run_bass_kernel_spmd as run

    f = {k: np.ascontiguousarray(a) for k, a in inputs.items()}
    seq, d, p = 512, 64, 128
    lc = 4 * (262144 // 512 + 128 + 8)
    pos = np.arange(seq, dtype=np.float32)[:, None]
    k = np.arange(d)
    inv = np.power(np.float32(10000.0), -((k - k % 2).astype(np.float32) / np.float32(d))).astype(np.float32)
    angle = pos * inv
    pos_enc = np.roll(np.where(k % 2 == 0, np.sin(angle), np.cos(angle)).astype(np.float32), -p // 2, axis=0)
    top = np.concatenate([np.eye(p), np.tile(np.arange(p), (p, 1)), np.triu(np.ones((p, p)), 1), np.ones((p, p)), np.eye(p)[::-1],
                          np.tile(np.arange(lc // 4), (p, 1))], axis=1)
    mask = np.zeros((d, top.shape[1]))
    mask[np.arange(d), np.arange(d) // 8] = 8 ** -0.5
    consts = np.concatenate([top, mask]).astype(np.float32)
    arrays = {
        "x": f["x"], "emb": f["L0_tok_W"],
        "qkv_w": np.concatenate([f["L0_attn_qkv_weight"].T, f["L0_attn_qkv_bias"][None]]),
        "proj_w": np.concatenate([f["L0_attn_proj_weight"].T, f["L0_attn_proj_bias"][None]]),
        "bias_rev": np.ascontiguousarray(f["L0_attn_bias_table"][::-1].T),
        "att": np.concatenate([f["L0_ffn_att_src"].reshape(1, 16), f["L0_ffn_att_dst"].reshape(1, 16)], axis=1),
        "w_gat": f["L0_ffn_W_gat"],
        "gat_rows": np.concatenate([f["L0_ffn_b_gat"], f["L0_ffn_ln_gamma"], f["L0_ffn_ln_beta"]])[None],
        "w1": np.concatenate([f["L0_ffn_W1"], f["L0_ffn_b1"][:, None]], axis=1),
        "w2": f["L0_ffn_W2"], "b2_rows": f["L0_ffn_b2"].reshape(1, 256), "edges": f["L0_ffn_edge_index"],
        "pos_enc": pos_enc, "consts": consts,
    }
    nc = bacc.Bacc("TRN2", target_bir_lowering=False, num_devices=1)
    args = [nc.dram_tensor("in_" + n, a.shape, mybir.dt.from_np(a.dtype), kind="ExternalInput").ap() for n, a in arrays.items()]
    out = nc.dram_tensor("out_0", (32, 512, 64), mybir.dt.float32, kind="ExternalOutput").ap()
    lm_tower_kernel(nc, *args, out)
    r = run(nc, [{"in_" + n: np.ascontiguousarray(a) for n, a in arrays.items()}], core_ids=[0])
    return r.results[0]["out_0"]
```

```python
import concourse.bass as bass
from concourse import mybir
from contextlib import ExitStack
import numpy as np


def lm_tower_kernel(nc, x, emb, qkv_w, proj_w, bias_rev, att, w_gat, gat_rows, w1, w2, b2_rows, edges, pos_enc, consts, out):
    f32, bf16, i32 = mybir.dt.float32, mybir.dt.bfloat16, mybir.dt.int32
    ALU, ACT, AX = mybir.AluOpType, mybir.ActivationFunctionType, mybir.AxisListType
    P = 128
    SEQS, SEQ = x.shape
    D = emb.shape[1]
    WIN = SEQ // P
    SHIFT = P // 2
    NH, HD = 8, 8
    NB = SEQS * WIN
    NE = edges.shape[1]
    NT = NE // P
    NX = 4
    HID = 2 * D
    CH = 4
    CE = CH * P
    NCH = NE // CE + NB
    LC = (NCH + 8) * CH
    NS = 8
    TW = NT // NB
    FW = 28
    ROW = 24
    GAP = float(2 ** 18)
    EMPTY = P << 14
    EPS = 1e-5

    ctx = ExitStack()
    with ctx:
        def sb(name, shape, dt=f32):
            return ctx.enter_context(nc.sbuf_tensor(name, shape, dt))

        def sem(name):
            return ctx.enter_context(nc.semaphore(name))

        edge_list = nc.dram_tensor("edge_list", [P * LC, 1], i32, kind="Internal").ap()
        node_rows = nc.dram_tensor("node_rows", [NB * P, ROW], f32, kind="Internal").ap()
        expert_out = nc.dram_tensor("expert_out", [NB * P, NX * D], f32, kind="Internal").ap()

        h_sb = sb("h_sb", [P, NB + WIN, D])
        rows_sb = sb("rows_sb", [P, NB, 32])
        big_i = sb("big_i", [P, LC], i32)
        pay_i = sb("pay_i", [P, LC], i32)
        big_f = sb("big_f", [P, LC])
        iota_b = sb("iota_b", [P, P], bf16)
        cst = sb("cst", [P, 5 * P + LC // CH])
        ident, iota_f, upper, ones, flip = (cst[:, k * P:(k + 1) * P] for k in range(5))
        chunk_iota = cst[:, 5 * P:]
        before_b = sb("before_b", [P, P], bf16)
        notbefore_b = sb("notbefore_b", [P, P], bf16)
        ones_b = sb("ones_b", [P, P], bf16)
        zeros_b = sb("zeros_b", [P, CE], bf16)
        ident_b = sb("ident_b", [P, P], bf16)
        sel_b = sb("sel_b", [16, NX, P], bf16)
        match = sb("match", [P, 1])
        bit_of = sb("bit_of", [P, 8], i32)
        node_i = sb("node_i", [P, 2, 8], i32)
        node_f = sb("node_f", [P, 2 * NX, 16])
        pe_sb = sb("pe_sb", [P, WIN, D])
        rb_sb = sb("rb_sb", [P, 2, NH, P])
        hmask = sb("hmask", [D, NH])
        qkvw_sb = sb("qkvw_sb", [D + 1, 3 * D])
        projw_sb = sb("projw_sb", [D + 1, D])
        w1_sb = sb("w1_sb", [D + 1, NX, HID])
        w2_sb = sb("w2_sb", [HID, NX, D])
        b2_sb = sb("b2_sb", [P, NX, D])
        wg_sb = sb("wg_sb", [D, 16])
        att_sb = sb("att_sb", [P, 2, 16])
        gr_sb = sb("gr_sb", [P, 3, 16])
        xi = sb("xi", [SEQS, SEQ], i32)
        xf = sb("xf", [SEQS, SEQ])
        tok_i = sb("tok_i", [P, WIN, SEQS + 2], i32)
        tok_now = sb("tok_now", [P, WIN], i32)
        emb_now = sb("emb_now", [P, WIN, D])
        oh = sb("oh", [P, 4, CH, P], bf16)
        pos_f = sb("pos_f", [P, 2, NS])
        pos_i = sb("pos_i", [P, 2, NS], i32)
        lo_i = sb("lo_i", [P, 2, NS], i32)
        addr_i = sb("addr_i", [P, 2, NS], i32)
        pay_now = sb("pay_now", [P, 2, NS], i32)
        hist = sb("hist", [P, NS, P])
        rowa = sb("rowa", [P, P])
        rowi = sb("rowi", [P, P], i32)
        rowb = sb("rowb", [P, P])
        colv = sb("colv", [P, 4])
        cmp_b = sb("cmp_b", [P, LC // CH], bf16)
        block_of = sb("block_of", [P, 4 + LC // CH], i32)
        stat = sb("stat", [P, WIN, 6])
        mv = sb("mv", [P, 2, WIN, 2])
        rstd = sb("rstd", [P, 2, WIN])
        root_t = sb("root_t", [P, WIN])
        xn = sb("xn", [P, D])
        xT = sb("xT", [D + 1, P])
        kT = sb("kT", [D, P])
        qm = sb("qm", [D, NH, P])
        v1 = sb("v1", [P, 2, NH, HD + 1])
        nmax = sb("nmax", [P, NH])
        pr = sb("pr", [P, NH, P])
        prT = sb("prT", [P, NH, P])
        rden = sb("rden", [P, NH])
        on = sb("on", [P, D])
        oT = sb("oT", [D + 1, P])
        xn2 = sb("xn2", [P, WIN, D])
        xT2 = sb("xT2", [D + 1, WIN, P])
        hh = sb("hh", [HID, NX, SEQ])
        eo = sb("eo", [P, WIN, NX, D])
        gt = sb("gt", [P, 2, WIN, 16])

        state = sb("state", [P, NB + 1, 12])
        a_dst_b = sb("a_dst_b", [P, NB + 1, 3, NX], bf16)
        acc = sb("acc", [P, NB + 1, NX, NX + 1])
        SL = 8
        src_now = sb("src_now", [P, SL, CH], i32)
        nodes = sb("nodes", [P, SL, CH, FW])
        bits_i = sb("bits_i", [P, 4, CH, 8], i32)
        room = sb("room", [P, 4096])
        hot_f = room[:, 0:2048].rearrange("p (s j d) -> p s j d", s=4, j=CH)
        hot = room[:, 2048:3072].bitcast(bf16).rearrange("p (s j d) -> p s j d", s=4, j=CH)
        sq = sb("sq", [P, CH, P], bf16)
        hotT_b = sb("hotT_b", [P, 2, CH, P], bf16)
        halves_b = sb("halves_b", [16, 2, CE], bf16)
        top = sb("top", [P, NX])
        dst_in = sb("dst_in", [P, 2, 20], bf16)
        shift = sb("shift", [P, 2, 2, NX])
        score = sb("score", [P, 2, NX])
        dst_e = sb("dst_e", [P, 2, CH, 12])
        fade = sb("fade", [P, 4, NX])
        lg = sb("lg", [P, 2, CH, NX])
        msg = sb("msg", [P, 4, CH, NX, NX + 1])
        junk = room[:, 0:CH * P].rearrange("p (j k) -> p j k", j=CH)
        big_b = room[:, CH * P:CH * P + (NT + TW) // 2].bitcast(bf16)
        ss = room[:, 3072:4096].rearrange("p (h k) -> p h k", h=NH)
        ag, ag2 = (room[:, k * 2048:(k + 1) * 2048].rearrange("p (b f) -> p b f", f=16) for k in range(2))
        g1 = sb("g1", [P, NB])
        g2 = sb("g2", [P, NB])
        sc = sb("sc", [P, NB, NX])
        wins = sb("wins", [P, NB, NX])
        gate = sb("gate", [P, NB, NX])
        GB = 8
        eb = rows_sb[:, :, :].rearrange("p b f -> p (b f)").rearrange("p (k b e d) -> p k b e d", k=2, b=GB, e=NX)

        def pb(name, banks):
            return ctx.enter_context(nc.psum_tensor(name, [P, banks * 512], f32))

        four = pb("four", 4)
        psum = [pb("bank0", 1), pb("bank1", 1)] + [four[:, k * 512:(k + 1) * 512] for k in range(4)] + [pb("bank6", 1), pb("bank7", 1)]
        count_ps = psum[0:2]
        bank_x, bank_y = psum[6], psum[7]

        names = """apart dve_late dve_end dve_mix const_loaded const_ready ids_loaded edges_loaded eo_free dve_step
            tok_T tok_ready tok_now_ready emb_gathered hist_oh hist_added hist_done base_mm base_row base_set
            chunk_cmp chunk_sum oh_ready ranked ranks_read counted addr_a addr_b scat_a scat_b
            bias_mm xn_ready xT_mm xT_ready qkv_mm kT_ready q_v_ready s_mm scored nmax_ready probs resid_done pT_mm pT_ready o_mm o_ready oT_mm oT_ready
            proj_mm xn2_ready xT2_mm xT2_ready gat_mm gat_read rows_ready rows_out hid_mm hid_ready eo_mm eo_ready eo_out
            sorted_read list_loaded list_ready state_ready src_ready sel_in sel_mm bits_ready codes_ready hot_f_ready squared hot_ready hotT_mm halves_mm hotT_ready halves_ready
            top_kept score_ready z_ready hi_ready z_sum shift_kept lg_1 lg_2 lg_3 faded sums_kept top_mm_a top_mm_b top_read_a top_read_b dst_ready edge_mm edge_out fade_in fade_ready lg_ready weights msg_ready sums_mm
            gvar_ready glog grstd gate_in gate_exp eb_a eb_b eb_used out_ready
            out_done""".split()
        gathered = [sem(f"gathered_{k}") for k in range(SL)]

        def chunks(eng, step):
            for c in range(SL):
                step(c, c, True, 0)
            with eng.Fori(1, NCH // SL) as i:
                for k in range(SL):
                    step(i * SL + k, k, False, i)
            for c in range(NCH, NCH + 3):
                step(c, c % SL, True, c // SL)

        def windows(eng, step):
            for w in range(WIN):
                step(w, w, 0, True, w > 0, False)
            with eng.Fori(1, SEQS) as s:
                for w in range(WIN):
                    step(s * WIN + w, w, s, True, True, True)
            for w in range(WIN):
                step(NB + w, w, SEQS, False, w == 0, True)

        S = {n: sem(n) for n in names}

        class Steps:
            def __init__(self, eng, name, start, it, per):
                self.eng, self.sem, self.start, self.it, self.per, self.n = eng, S[name], start, it, per, 0

            def __call__(self, ins, beside=None):
                self.n += 1
                ins.then_inc(self.sem, 1)
                base = self.start + self.n
                if beside:
                    beside()
                self.eng.wait_ge(self.sem, base if self.it is None else self.it * self.per + base)

        def apart(eng):
            eng.sem_inc(S["apart"], 1)

        def one(i):
            return bass.ds(i, 1)

        block = ctx.enter_context(nc.Block())
        HIST_IT = NT // 32
        consts_in = 13
        DVE_MIX = 2 * 4
        DVE_SEQ = 60

        @block.sync
        def _(sp):
            sp.dma_start(xi[:, :], x).then_inc(S["ids_loaded"], 16)
            sp.dma_start(big_i[:, 0:NT], edges[1:2, :].rearrange("a (p t) -> (a p) t", p=P)).then_inc(S["edges_loaded"], 16)
            sp.dma_start(pay_i[:, 0:NT], edges[0:1, :].rearrange("a (p t) -> (a p) t", p=P)).then_inc(S["edges_loaded"], 16)
            for dst, src in ((cst[:, :], consts[0:P, :]), (pe_sb[:, :, :], pos_enc.rearrange("(w p) d -> p w d", p=P)),
                             (qkvw_sb[:, :], qkv_w), (projw_sb[:, :], proj_w), (w1_sb[:, :, :], w1.rearrange("e k n -> k e n")),
                             (w2_sb[:, :, :], w2.rearrange("e k n -> k e n")), (wg_sb[:, :], w_gat),
                             (b2_sb[:, :, :].rearrange("p e d -> p (e d)"), b2_rows.to_broadcast([P, NX * D])),
                             (att_sb[:, :, :].rearrange("p a b -> p (a b)"), att.to_broadcast([P, 32])),
                             (gr_sb[:, :, :].rearrange("p a b -> p (a b)"), gat_rows.to_broadcast([P, 48])),
                             (hmask[:, :], consts[P:P + D, 0:NH])):
                sp.dma_start(dst, src).then_inc(S["const_loaded"], 16)
            for v in range(2):
                src = bass.AP(tensor=bias_rev.tensor, offset=bias_rev.offset, ap=[[1, P], [2 * P - 1, NH], [1, P]])
                sp.dma_start(rb_sb[:, v, :, :], src).then_inc(S["const_loaded"], 16)
            sp.sem_inc(S["eo_free"], 1)
            with sp.Fori(0, SEQS) as s:
                sp.wait_ge(S["rows_ready"], s + 1)
                sp.dma_start(node_rows.rearrange("(b p) f -> p b f", p=P)[:, bass.ds(s * WIN, WIN), :], rows_sb[:, bass.ds(s * WIN, WIN), 0:ROW]).then_inc(S["rows_out"], 16)
                sp.wait_ge(S["eo_ready"], s + 2)
                sp.dma_start(expert_out.rearrange("(b p) f -> p b f", p=P)[:, bass.ds(s * WIN, WIN), :], eo[:, :, :, :].rearrange("p w e d -> p w (e d)")).then_inc(S["eo_out"], 16)
                sp.wait_ge(S["eo_out"], s * 16 + 16)
                sp.sem_inc(S["eo_free"], 1)
            sp.wait_ge(S["scat_a"], 16 * NS * (NB + 1))
            sp.wait_ge(S["scat_b"], 16 * NS * (NB + 1))
            sp.wait_ge(S["sorted_read"], 1)
            sp.dma_start(big_i[:, :], edge_list.rearrange("(p t) a -> p (t a)", p=P)).then_inc(S["list_loaded"], 16)
            sp.wait_ge(S["eo_out"], 16 * SEQS)
            with sp.Fori(0, NB // GB // 2) as i:
                for k, loaded in ((0, "eb_a"), (1, "eb_b")):
                    sp.wait_ge(S["eb_used"], i * 2 + k + 1)
                    sp.dma_start(eb[:, k, :, :, :].rearrange("p b e d -> p b (e d)"),
                                 expert_out.rearrange("(b p) f -> p b f", p=P)[:, bass.ds((i * 2 + k) * GB, GB), :]).then_inc(S[loaded], 16)
            sp.wait_ge(S["out_ready"], 1)
            for w in range(WIN - 1):
                sp.dma_start(out[:, w * P + SHIFT:(w + 1) * P + SHIFT, :].rearrange("s p d -> p s d"), h_sb[:, w:NB:WIN, :]).then_inc(S["out_done"], 16)
            sp.dma_start(out[:, SEQ - SHIFT:SEQ, :].rearrange("s p d -> p s d"), h_sb[0:SHIFT, WIN - 1:NB:WIN, :]).then_inc(S["out_done"], 16)
            sp.dma_start(out[:, 0:SHIFT, :].rearrange("s p d -> p s d"), h_sb[SHIFT:P, WIN - 1:NB:WIN, :]).then_inc(S["out_done"], 16)
            sp.wait_ge(S["out_done"], 16 * (WIN + 1))

        @block.gpsimd
        def _(gp):
            def gather_tokens(w):
                gp.indirect_dma_start(emb_now[:, w, :], None, emb, bass.IndirectOffsetOnAxis(ap=tok_now[:, w:w + 1], axis=0)).then_inc(S["emb_gathered"], 16)
            gp.wait_ge(S["const_ready"], 1)
            for k, scattered in ((0, "scat_a"), (1, "scat_b")):
                gp.dma_start(edge_list.rearrange("(p t) a -> p (t a)", p=P)[:, k * LC // 2:(k + 1) * LC // 2],
                             rows_sb[:, :, :].rearrange("p a b -> p (a b)")[:, 0:LC // 2].bitcast(i32)).then_inc(S[scattered], 16 * NS)
            gp.wait_ge(S["scat_a"], 16 * NS)
            gp.wait_ge(S["scat_b"], 16 * NS)
            gp.wait_ge(S["tok_now_ready"], 1)
            for w in range(WIN):
                gather_tokens(w)
            with gp.Fori(0, SEQS) as s:
                gp.wait_ge(S["tok_now_ready"], s + 2)
                apart(gp)
                for w in range(WIN):
                    gather_tokens(w)
                for w in range(WIN):
                    for b, ready, scattered in ((0, "addr_a", "scat_a"), (1, "addr_b", "scat_b")):
                        gp.wait_ge(S[ready], s * WIN + w + 1)
                        apart(gp)
                        for j in range(NS):
                            gp.indirect_dma_start(edge_list, bass.IndirectOffsetOnAxis(ap=addr_i[:, b, j:j + 1], axis=0), pay_now[:, b, j:j + 1], None).then_inc(S[scattered], 16)

            def gather_nodes(c, k, first, lap):
                if first and not 0 <= c < NCH + 2:
                    return
                gp.wait_ge(S["src_ready"], c + 1)
                if not (first and c < SL):
                    gp.wait_ge(S["sums_mm"], c + 1 - SL)
                apart(gp)
                for j in range(CH):
                    gp.indirect_dma_start(nodes[:, k, j, 0:ROW], None, node_rows, bass.IndirectOffsetOnAxis(ap=src_now[:, k, j:j + 1], axis=0)).then_inc(gathered[k], 16)

            gp.wait_ge(S["rows_out"], 16 * SEQS)
            chunks(gp, gather_nodes)

        @block.vector
        def _(dve):
            v = nc.vector
            do = Steps(dve, "dve_step", 0, None, 0)
            dve.wait_ge(S["ids_loaded"], 16)
            do(v.tensor_copy(xf[:, 0:SEQ - SHIFT], xi[:, SHIFT:SEQ]))
            v.tensor_copy(xf[:, SEQ - SHIFT:SEQ], xi[:, 0:SHIFT]).then_inc(S["tok_T"], 1)
            dve.wait_ge(S["const_loaded"], 16 * consts_in)
            v.tensor_copy(iota_b[:, :], iota_f)
            v.tensor_copy(before_b[:, :], upper)
            v.tensor_copy(ones_b[:, :], ones)
            v.tensor_tensor(notbefore_b[:, :], ones, upper, ALU.subtract)
            v.tensor_copy(ident_b[:, :], ident)
            v.memset(zeros_b[:, :], 0.0)
            v.tensor_scalar(rb_sb[0:SHIFT, 1, :, 0:SHIFT], rb_sb[0:SHIFT, 1, :, 0:SHIFT], -100.0, None, ALU.add)
            v.tensor_scalar(rb_sb[SHIFT:P, 1, :, SHIFT:P], rb_sb[SHIFT:P, 1, :, SHIFT:P], -100.0, None, ALU.add)
            v.memset(tok_i[:, :, SEQS:], 0)
            v.memset(xT[D:D + 1, :], 1.0)
            v.memset(oT[D:D + 1, :], 1.0)
            v.memset(xT2[D:D + 1, :, :], 1.0)
            v.memset(v1[:, :, :, HD:HD + 1], 1.0)
            for k in range(8):
                v.memset(bit_of[:, k:k + 1], 1 << k)
            v.memset(rows_sb[:, :, :].rearrange("p a b -> p (a b)")[:, 0:LC].bitcast(i32), EMPTY).then_inc(S["const_ready"], 1)
            dve.wait_ge(S["const_ready"], 1)
            dve.wait_ge(S["edges_loaded"], 32)
            tmp_i = h_sb[:, 0:NT // D, :].rearrange("p a b -> p (a b)").bitcast(i32)
            for ids in (big_i[:, 0:NT], pay_i[:, 0:NT]):
                do(v.tensor_scalar(tmp_i, ids, float(SEQ - SHIFT), None, ALU.add))
                do(v.tensor_single_scalar(tmp_i, tmp_i, SEQ - 1, ALU.bitwise_and))
                do(v.tensor_scalar(ids, ids, -SEQ, None, ALU.bitwise_and))
                do(v.tensor_tensor(ids, ids, tmp_i, ALU.bitwise_or))
            do(v.tensor_scalar(tmp_i, big_i[:, 0:NT], P - 1, 14, ALU.bitwise_and, ALU.logical_shift_left))
            do(v.tensor_tensor(pay_i[:, 0:NT], pay_i[:, 0:NT], tmp_i, ALU.bitwise_or))
            do(v.tensor_scalar(big_i[:, 0:NT], big_i[:, 0:NT], 7, None, ALU.logical_shift_right))
            do(v.tensor_copy(big_f[:, 0:NT], big_i[:, 0:NT]))
            do(v.tensor_copy(big_b[:, 0:NT], big_f[:, 0:NT]))
            do(v.memset(big_b[:, NT:], 0.0))
            do(v.tensor_tensor(rowa[:, :], iota_f, ident, ALU.mult))
            do(v.tensor_reduce(colv[:, 3:4], rowa[:, :], AX.X, ALU.add))
            do(v.tensor_copy(node_i[:, 0, 0:1], colv[:, 3:4]))
            do(v.tensor_tensor(node_i[:, 1, :], node_i[:, 0, 0:1].to_broadcast([P, 8]), bit_of[:, :], ALU.bitwise_and))
            do(v.tensor_copy(node_f[:, 1, 0:8], node_i[:, 1, :]))
            do(v.tensor_copy(node_f[:, 2, 0:8], bit_of[:, :]))
            do(v.reciprocal(node_f[:, 2, 0:8], node_f[:, 2, 0:8]))
            do(v.tensor_tensor(node_f[:, 1, 0:8], node_f[:, 1, 0:8], node_f[:, 2, 0:8], ALU.mult))
            do(v.tensor_reduce(match[:, :], node_f[:, 1, 0:8], AX.X, ALU.add))
            do(v.tensor_scalar(match[:, :], match[:, :], -GAP, None, ALU.mult))
            do(v.tensor_scalar(node_f[:, 1, 0:8], node_f[:, 1, 0:8], 2 * GAP, -GAP, ALU.mult, ALU.add))
            do(v.tensor_tensor(node_f[:, 3, 8:16], node_f[:, 1, 0:8], node_f[:, 2, 0:8], ALU.mult))
            for h in range(NX):
                do(v.memset(node_f[:, 4 + h, 0:8], 0.0))
                do(v.memset(node_f[:, 4 + h, h:h + 1], 1.0))
                do(v.memset(node_f[:, 4 + h, h + NX:h + NX + 1], 1.0))
                do(v.tensor_copy(node_f[:, 4 + h, 8:16], node_f[:, 3, 8:16]))
            dve.sem_inc(S["sel_in"], 1)
            dve.wait_ge(S["sel_mm"], 1)
            do(v.tensor_copy(sel_b[:, :, :].rearrange("k h d -> k (h d)"), bank_y[0:16, :]))
            dve.wait_ge(S["tok_ready"], 1)
            do(v.tensor_copy(tok_i[:, :, 0:SEQS], bank_x[:, 0:WIN * SEQS].rearrange("p (w s) -> p w s", w=WIN)))
            dve.wait_ge(S["bias_mm"], 1)
            for v2 in range(4):
                do(v.tensor_copy(rb_sb[:, v2 // 2, 4 * (v2 % 2):4 * (v2 % 2) + 4, :], psum[2 + v2][:, :].rearrange("p (h k) -> p h k", h=4)))
            with dve.Fori(0, HIST_IT) as i:
                for g in range(8):
                    dve.wait_ge(S["hist_added"], i * 8 + g + 1)
                    v.tensor_tensor(oh[:, g % 4, :, :], iota_b[:, :].rearrange("p (a b) -> p a b", a=1).to_broadcast([P, CH, P]),
                                    big_b[:, bass.ds(i * 32 + g * 4, CH)].rearrange("p (j a) -> p j a", a=1).to_broadcast([P, CH, P]), ALU.is_equal).then_inc(S["hist_oh"], 1)
            dve.wait_ge(S["hist_done"], 1)
            do(v.tensor_copy(hist[:, 0:4, :].rearrange("p s b -> p (s b)"), count_ps[0][:, :]))
            do(v.tensor_copy(hist[:, 4:8, :].rearrange("p s b -> p (s b)"), count_ps[1][:, :]))
            do(v.tensor_reduce(rowa[:, :], hist[:, :, :].rearrange("p s b -> p b s"), AX.X, ALU.add))
            do(v.tensor_scalar(rowi[:, :], rowa[:, :], float(CE - 1), None, ALU.add))
            do(v.tensor_scalar(rowi[:, :], rowi[:, :], 9, None, ALU.logical_shift_right))
            do(v.tensor_copy(rowa[:, :], rowi[:, :]))
            do(v.tensor_tensor(rowb[:, :], rowa[:, :], ident, ALU.mult))
            do(v.tensor_reduce(colv[:, 0:1], rowb[:, :], AX.X, ALU.add))
            v.tensor_scalar(rowb[:, :], ones, colv[:, 0:1], None, ALU.mult).then_inc(S["base_mm"], 1)
            dve.wait_ge(S["base_row"], 1)
            do(v.tensor_copy(rowa[:, :], bank_x[:, 0:P]))
            do(v.tensor_tensor(rowb[:, :], rowa[:, :], ident, ALU.mult))
            do(v.tensor_reduce(colv[:, 1:2], rowb[:, :], AX.X, ALU.add))
            do(v.tensor_tensor(colv[:, 2:3], colv[:, 0:1], colv[:, 1:2], ALU.add))
            v.tensor_scalar(cmp_b[:, :], chunk_iota, colv[:, 2:3], None, ALU.is_ge).then_inc(S["chunk_cmp"], 1)
            do(v.tensor_scalar(rowa[:, :], rowa[:, :], float(CE), None, ALU.mult))
            for k in range(NS):
                do(v.tensor_tensor(rowb[:, :], hist[:, k, :], rowa[:, :], ALU.add))
                do(v.tensor_copy(hist[:, k, :], rowa[:, :]))
                do(v.tensor_copy(rowa[:, :], rowb[:, :]))
            dve.sem_inc(S["base_set"], 1)
            dve.wait_ge(S["chunk_sum"], 1)
            do(v.memset(block_of[:, 0:4], 0))
            do(v.tensor_copy(block_of[:, 4:516], bank_x[:, :]))
            do(v.tensor_copy(block_of[:, 516:], bank_y[:, 0:LC // CH - 512]))
            pre = do.n

            dve.sem_inc(S["eo_ready"], 1)

            def root(which, beside):
                y = rstd[:, which, :]
                var = mv[:, which, :, 1:2].rearrange("p w a -> p (w a)")
                do(v.tensor_scalar(var, var, EPS, None, ALU.add), beside)
                do(v.tensor_single_scalar(y.bitcast(i32), var.bitcast(i32), 1, ALU.logical_shift_right), beside)
                do(v.tensor_scalar(y.bitcast(i32), y.bitcast(i32), -1.0, float(0x5F3759DF), ALU.mult, ALU.add), beside)
                for _ in range(3):
                    do(v.tensor_tensor(root_t[:, :], y, y, ALU.mult), beside)
                    do(v.scalar_tensor_tensor(root_t[:, :], root_t[:, :], -0.5, var, ALU.mult, ALU.mult), beside)
                    do(v.scalar_tensor_tensor(y, root_t[:, :], 1.5, y, ALU.add, ALU.mult), beside)

            def embed(s, beside):
                dve.wait_ge(S["emb_gathered"], s * (16 * WIN) + 16 * WIN)
                apart(dve)
                do(v.tensor_tensor(h_sb[:, bass.ds(s * WIN, WIN), :], emb_now[:, :, :], pe_sb[:, :, :], ALU.add), beside)
                v.tensor_copy(tok_now[:, :].rearrange("p (w a) -> p w a", a=1), tok_i[:, :, one(s + 1)]).then_inc(S["tok_now_ready"], 1)
                for w in range(WIN):
                    last = v.bn_stats(stat[:, w, :], h_sb[:, one(s * WIN + w), :].rearrange("p a d -> p (a d)"))
                do(last, beside)
                apart(dve)
                for w in range(WIN):
                    last = v.bn_aggr(mv[:, 0, w, :], stat[:, w, :])
                do(last, beside)
                root(0, beside)

            def normed(n, w):
                v.tensor_scalar(xn[:, :], h_sb[:, one(n), :].rearrange("p a d -> p (a d)"), mv[:, 0, w, 0:1], rstd[:, 0, w:w + 1], ALU.subtract, ALU.mult).then_inc(S["xn_ready"], 1)

            def queries(n, w):
                dve.wait_ge(S["qkv_mm"], n + 1)
                dve.wait_ge(S["kT_ready"], n + 1)
                v.tensor_copy(v1[:, w % 2, :, 0:HD], bank_x[:, 2 * P:2 * P + D].rearrange("p (h d) -> p h d", h=NH))
                v.tensor_tensor(qm[:, :, :], bank_x[0:D, 0:P].rearrange("p (a q) -> p a q", a=1).to_broadcast([D, NH, P]),
                                hmask[:, :].rearrange("p (h a) -> p h a", a=1).to_broadcast([D, NH, P]), ALU.mult).then_inc(S["q_v_ready"], 1)

            def onehots(n, g):
                if not isinstance(n, int) or n > 0:
                    dve.wait_ge(S["counted"], n * 4 + g - 3)
                v.tensor_tensor(oh[:, g, :, :], iota_b[:, :].rearrange("p (a b) -> p a b", a=1).to_broadcast([P, CH, P]),
                                big_b[:, bass.ds(n * TW + g * CH, CH)].rearrange("p (j a) -> p j a", a=1).to_broadcast([P, CH, P]), ALU.is_equal).then_inc(S["oh_ready"], 1)

            def ranks(n, g, tiles=range(4)):
                if 0 in tiles:
                    dve.wait_ge(S["ranked"], n * 4 + g + 1)
                for j in tiles:
                    last = v.tensor_tensor_reduce(out=junk[:, j, :], in0=oh[:, g, j, :], in1=count_ps[g % 2][:, j * P:(j + 1) * P], scale=1.0, scalar=0.0,
                                                  op0=ALU.mult, op1=ALU.add, accum_out=pos_f[:, g // 2, (g % 2) * CH + j:(g % 2) * CH + j + 1])
                if CH - 1 in tiles:
                    last.then_inc(S["ranks_read"], 1)
                    if len(tiles) == CH:
                        dve.wait_ge(S["ranks_read"], n * 4 + g + 1)

            def places(n, b, beside):
                do(v.tensor_copy(pos_i[:, b, :], pos_f[:, b, :]), beside)
                v.tensor_scalar(lo_i[:, b, :], pos_i[:, b, :], P - 1, None, ALU.bitwise_and)
                do(v.tensor_scalar(pos_i[:, b, :], pos_i[:, b, :], 7, None, ALU.logical_shift_right), beside)
                dve.wait_ge(S["scat_b" if b else "scat_a"], (n + 1) * (16 * NS))
                v.scalar_tensor_tensor(addr_i[:, b, :], lo_i[:, b, :], float(LC), pos_i[:, b, :], ALU.mult, ALU.add)
                apart(dve)
                v.tensor_copy(pay_now[:, b, :], pay_i[:, bass.ds(n * TW + b * NS, NS)]).then_inc(S["addr_b" if b else "addr_a"], 1)

            def node_rows_of(s):
                rows = rows_sb[:, bass.ds(s * WIN, WIN), :]
                for k, col in ((0, 16), (1, 28)):
                    do(v.tensor_tensor(gt[:, k, :, :], rows[:, :, 0:16], att_sb[:, k:k + 1, :].to_broadcast([P, WIN, 16]), ALU.mult))
                    do(v.tensor_reduce(rows[:, :, col:col + NX], gt[:, k, :, :].rearrange("p w (h k) -> p w h k", h=NX), AX.X, ALU.add))
                parts = rows.bitcast(bf16)
                apart(dve)
                do(v.tensor_copy(parts[:, :, 40:44], rows[:, :, 16:20]))
                v.tensor_tensor(parts[:, :, 44:48], rows[:, :, 16:20], parts[:, :, 40:44], ALU.subtract).then_inc(S["rows_ready"], 1)

            def window(n, w, s, front, back, tail):
                if tail and w == 1:
                    dve.wait_ge(S["gat_mm"], s)
                    apart(dve)
                    v.tensor_copy(rows_sb[:, bass.ds(s * WIN - WIN, WIN), 0:16], psum[5][:, 0:64].rearrange("p (w f) -> p w f", w=WIN)).then_inc(S["gat_read"], 1)
                if front:
                    def score():
                        for _ in range(4):
                            if not heads:
                                return
                            h = heads.pop(0)
                            last = v.tensor_tensor_reduce(out=ss[:, h, :], in0=rb_sb[:, w // (WIN - 1), h, :], in1=psum[2 + h // 4][:, (h % 4) * P:(h % 4 + 1) * P], scale=1.0,
                                                          scalar=-3.0e38, op0=ALU.add, op1=ALU.max, accum_out=nmax[:, h:h + 1])
                            if not heads:
                                last.then_inc(S["scored"], 1)

                    heads = list(range(NH))
                    tiles = list(range(WIN))
                    if w == WIN - 1:
                        rest = [(g, j) for g in range(2) for j in range(CH)]

                        def some_ranks():
                            if rest:
                                g, j = rest.pop(0)
                                ranks(n, g, [j])

                        embed(s + 1, some_ranks)
                        dve.wait_ge(S["ranks_read"], n * 4 + 2)
                        normed(n + 1, 0)
                    else:
                        normed(n + 1, w + 1)
                        ranks(n, 0)
                        ranks(n, 1)
                    dve.wait_ge(S["s_mm"], n + 1)
                    if back:
                        dve.wait_ge(S["probs"], n)
                    apart(dve)
                    places(n, 0, score)
                    score()
                    dve.wait_ge(S["scored"], n + 1)
                    v.tensor_scalar(nmax[:, :], nmax[:, :], -1.0, None, ALU.mult).then_inc(S["nmax_ready"], 1)
                    ranks(n, 2)
                    ranks(n, 3)
                    places(n, 1, lambda: onehots(n + 1, tiles.pop(0)))
                if tail and w == 1:
                    dve.wait_ge(S["gat_read"], s)
                    node_rows_of(s - 1)
                if back:
                    dve.wait_ge(S["o_mm"], n)
                    o_ps = bank_y[:, 0:NH * (HD + 1)].rearrange("p (h d) -> p h d", h=NH)
                    do(v.reciprocal(rden[:, :].rearrange("p (h a) -> p h a", a=1), o_ps[:, :, HD:HD + 1]))
                    v.tensor_tensor(on[:, :].rearrange("p (h d) -> p h d", h=NH), o_ps[:, :, 0:HD],
                                    rden[:, :].rearrange("p (h a) -> p h a", a=1).to_broadcast([P, NH, HD]), ALU.mult).then_inc(S["o_ready"], 1)
                if front:
                    queries(n + 1, w + 1)
                if back:
                    tile = h_sb[:, one(n - 1), :].rearrange("p a d -> p (a d)")
                    dve.wait_ge(S["proj_mm"], n)
                    v.tensor_tensor(tile, tile, bank_y[:, 384:384 + D], ALU.add).then_inc(S["resid_done"], 1)
                more = (lambda: onehots(n + 1, tiles.pop(0)) if tiles else None) if front else None
                if front and w > 0:
                    more()
                if back:
                    dve.wait_ge(S["resid_done"], n)
                    apart(dve)
                    do(v.bn_stats(stat[:, (w - 1) % WIN, :], tile), more)
                    apart(dve)
                    do(v.bn_aggr(mv[:, 1, (w - 1) % WIN, :], stat[:, (w - 1) % WIN, :]))
                elif front:
                    more()
                    more()
                if tail and w == 0:
                    root(1, more)
                    for k in range(WIN):
                        last = v.tensor_scalar(xn2[:, k, :], h_sb[:, one(s * WIN - WIN + k), :].rearrange("p a d -> p (a d)"), mv[:, 1, k, 0:1], rstd[:, 1, k:k + 1], ALU.subtract, ALU.mult)
                    last.then_inc(S["xn2_ready"], 1)
                if tail and w == WIN - 1:
                    dve.wait_ge(S["eo_mm"], s)
                    dve.wait_ge(S["eo_free"], s)
                    for e in range(NX):
                        src = psum[4 + e // 2][:, (e % 2) * 256:(e % 2) * 256 + 256].rearrange("p (w d) -> p w d", w=WIN)
                        last = v.tensor_tensor(eo[:, :, e, :], src, b2_sb[:, e:e + 1, :].to_broadcast([P, WIN, D]), ALU.add)
                    last.then_inc(S["eo_ready"], 1)

            v.tensor_copy(tok_now[:, :].rearrange("p (w a) -> p w a", a=1), tok_i[:, :, 0:1]).then_inc(S["tok_now_ready"], 1)
            embed(0, None)
            normed(0, 0)
            queries(0, 0)
            for g in range(4):
                onehots(0, g)
            for w in range(WIN):
                window(w, w, 0, True, w > 0, False)
            pre = do.n - DVE_SEQ
            with dve.Fori(1, SEQS) as s:
                do = Steps(dve, "dve_step", pre, s, DVE_SEQ)
                for w in range(WIN):
                    window(s * WIN + w, w, s, True, True, True)
                assert do.n == DVE_SEQ, do.n
            do = Steps(dve, "dve_step", pre + SEQS * DVE_SEQ, None, 0)
            for w in range(WIN):
                window(NB + w, w, SEQS, False, w == 0, True)

            do = Steps(dve, "dve_late", 0, None, 0)
            v.memset(state[:, NB:NB + 1, :], 0.0)
            v.memset(acc[:, NB:NB + 1, :, :], 0.0)
            v.tensor_copy(state[:, 0:NB, 0:4], rows_sb[:, :, 16:20])
            v.tensor_copy(state[:, 0:NB, 8:12], rows_sb[:, :, 28:32])
            do(v.tensor_tensor(state[:, 0:NB, 4:8], rows_sb[:, :, 16:20], rows_sb[:, :, 28:32], ALU.add))
            do(v.scalar_tensor_tensor(state[:, 0:NB, 4:8], state[:, 0:NB, 4:8], 0.2, state[:, 0:NB, 4:8], ALU.mult, ALU.max))
            v.memset(a_dst_b[:, NB:NB + 1, :, :], 0.0)
            rest = rows_sb[:, :, 28:32]
            for k in range(3):
                do(v.tensor_copy(a_dst_b[:, 0:NB, k, :], rest))
                if k < 2:
                    do(v.tensor_tensor(rest, rest, a_dst_b[:, 0:NB, k, :], ALU.subtract))
            v.memset(acc[:, 0:NB, :, 0:1], 1.0)
            v.tensor_copy(acc[:, 0:NB, :, 1:NX + 1], rows_sb[:, :, 0:16].rearrange("p b (h k) -> p b h k", h=NX)).then_inc(S["state_ready"], 1)
            dve.wait_ge(S["state_ready"], 1)
            dve.sem_inc(S["sorted_read"], 1)
            dve.wait_ge(S["list_loaded"], 16)
            do(v.tensor_single_scalar(pay_i[:, :], big_i[:, :], 14, ALU.logical_shift_right))
            do(v.tensor_copy(big_f[:, :], pay_i[:, :]))
            v.tensor_single_scalar(big_i[:, :], big_i[:, :], (1 << 14) - 1, ALU.bitwise_and).then_inc(S["list_ready"], 1)

            def bits(c, k):
                v.tensor_tensor(bits_i[:, k % 4, :, :], pay_i[:, bass.ds(c * CH, CH)].rearrange("p (j a) -> p j a", a=1).to_broadcast([P, CH, 8]),
                                bit_of[:, :].rearrange("p (a k) -> p a k", a=1).to_broadcast([P, CH, 8]), ALU.bitwise_and).then_inc(S["bits_ready"], 1)

            block_regs = [dve.alloc_register(f"block_{k}") for k in range(SL + 4)]
            blocks = []

            def chunk(c, k, first, lap):
                lead, logits, weigh, close = (not first or c - back in range(NCH) for back in range(4))
                e2, w2 = (k - 1) % 2, k % 2
                if k == 0:
                    dve.load(block_regs, block_of[0:1, bass.ds(lap * SL, SL + 4)])
                    blocks[:] = [dve.snap(reg, min_val=0, max_val=NB) for reg in block_regs]
                if lead:
                    b = blocks[k + 4]
                    st = state[:, one(b), :].rearrange("p a f -> p (a f)")
                    dve.wait_ge(S["top_mm_a"], c + 1)
                    v.tensor_reduce(top[:, 0:2], four[:, 0:1024].rearrange("p (h e) -> p h e", h=2), AX.X, ALU.max).then_inc(S["top_read_a"], 1)
                le = lg[:, e2, :, :]
                if logits:
                    dve.wait_ge(S["edge_out"], c)
                    v.tensor_tensor(le, nodes[:, (k - 1) % SL, :, 16:20], dst_e[:, e2, :, 8:12], ALU.add).then_inc(S["lg_1"], 1)
                if lead:
                    dve.wait_ge(S["top_mm_b"], c + 1)
                    v.tensor_reduce(top[:, 2:4], four[:, 1024:2048].rearrange("p (h e) -> p h e", h=2), AX.X, ALU.max).then_inc(S["top_read_b"], 1)
                if logits:
                    dve.wait_ge(S["lg_1"], c)
                    v.scalar_tensor_tensor(le, le, 0.2, le, ALU.mult, ALU.max).then_inc(S["lg_2"], 1)
                if logits:
                    before = state[:, one(blocks[k + 3]), :].rearrange("p a f -> p (a f)")
                    dve.wait_ge(S["dst_ready"], c)
                    v.tensor_tensor(shift[:, e2, 1, :], dst_in[:, e2, 0:4], dst_in[:, e2, 4:8], ALU.add).then_inc(S["z_sum"], 1)
                if lead:
                    dve.wait_ge(S["top_read_a"], c + 1)
                    dve.wait_ge(S["top_read_b"], c + 1)
                    v.scalar_tensor_tensor(st[:, 0:4], top[:, :], match[:, 0:1], st[:, 0:4], ALU.add, ALU.max).then_inc(S["top_kept"], 1)
                if logits:
                    dve.wait_ge(S["lg_2"], c)
                    v.tensor_tensor(le, le, dst_e[:, e2, :, 0:4], ALU.subtract).then_inc(S["lg_3"], 1)
                if lead:
                    v.tensor_copy(dst_in[:, w2, 8:20], a_dst_b[:, one(b), :, :].rearrange("p a k h -> p (a k h)"))
                    dve.wait_ge(S["top_kept"], c + 1)
                    v.tensor_tensor(score[:, w2, :], st[:, 0:4], st[:, 8:12], ALU.add).then_inc(S["score_ready"], 1)
                if logits:
                    dve.wait_ge(S["lg_3"], c)
                    v.scalar_tensor_tensor(le, le, 20.0, dst_e[:, e2, :, 4:8], ALU.min, ALU.subtract).then_inc(S["lg_ready"], 1)
                    if not first or c > 1:
                        dve.wait_ge(S["shift_kept"], c - 1)
                    dve.wait_ge(S["z_sum"], c)
                    v.tensor_tensor(fade[:, (k - 1) % 4, :], before[:, 4:8], shift[:, e2, 1, :], ALU.subtract).then_inc(S["fade_in"], 1)
                if lead:
                    dve.wait_ge(S["score_ready"], c + 1)
                    v.scalar_tensor_tensor(shift[:, w2, 0, :], score[:, w2, :], 0.2, score[:, w2, :], ALU.mult, ALU.max).then_inc(S["z_ready"], 1)
                    bits(c + 3, k + 3)
                if close:
                    bc = blocks[k + 1]
                    ac = acc[:, one(bc), :, :].rearrange("p a h f -> p (a h) f")
                    if not first or c > 3:
                        dve.wait_ge(S["sums_kept"], c - 3)
                    dve.wait_ge(S["fade_ready"], c - 2)
                    v.tensor_tensor(ac, ac, fade[:, (k - 3) % 4, :].rearrange("p (h a) -> p h a", a=1).to_broadcast([P, NX, NX + 1]), ALU.mult).then_inc(S["faded"], 1)
                if lead:
                    dve.wait_ge(S["z_ready"], c + 1)
                    v.tensor_copy(dst_in[:, w2, 0:4], shift[:, w2, 0, :]).then_inc(S["hi_ready"], 1)
                if logits:
                    dve.wait_ge(S["fade_in"], c)
                    v.tensor_scalar(before[:, 4:8], shift[:, e2, 1, :], 1.0, None, ALU.mult).then_inc(S["shift_kept"], 1)
                if weigh:
                    m = msg[:, (k - 2) % 4, :, :, :]
                    dve.wait_ge(S["weights"], c - 1)
                    v.tensor_tensor(m[:, :, :, 1:NX + 1], nodes[:, (k - 2) % SL, :, 0:16].rearrange("p j (h f) -> p j h f", h=NX), m[:, :, :, 0:1].to_broadcast([P, CH, NX, NX]),
                                    ALU.mult).then_inc(S["msg_ready"], 1)
                if lead:
                    dve.wait_ge(S["hi_ready"], c + 1)
                    v.tensor_tensor(dst_in[:, w2, 4:8], shift[:, w2, 0, :], dst_in[:, w2, 0:4], ALU.subtract).then_inc(S["dst_ready"], 1)
                if close:
                    dve.wait_ge(S["sums_mm"], c - 2)
                    dve.wait_ge(S["faded"], c - 2)
                    v.tensor_tensor(ac, ac, psum[7][:, 0:20].rearrange("p (h f) -> p h f", h=NX), ALU.add).then_inc(S["sums_kept"], 1)

            for k in range(3):
                bits(k, k)
            chunks(dve, chunk)
            dve.wait_ge(S["sums_kept"], NCH)

            do = Steps(dve, "dve_end", 0, None, 0)
            def wide(ap):
                return ap.rearrange("p (b a) -> p b a", a=1)
            dve.sem_inc(S["eb_used"], 2)
            w4 = acc[:, 0:NB, :, 0:1].rearrange("p b h a -> p b (h a)")
            do(v.tensor_scalar(sc[:, :, :], w4, 1e-16, None, ALU.add))
            do(v.reciprocal(sc[:, :, :], sc[:, :, :]))
            ag4 = ag[:, :, :].rearrange("p b (h k) -> p b h k", h=NX)
            for h in range(NX):
                last = do(v.tensor_tensor(ag4[:, :, h, :], acc[:, 0:NB, h, 1:NX + 1], sc[:, :, h:h + 1].to_broadcast([P, NB, NX]), ALU.mult))
            do(v.tensor_tensor(ag[:, :, :], ag[:, :, :], gr_sb[:, 0:1, :].to_broadcast([P, NB, 16]), ALU.add))
            do(v.tensor_reduce(g1[:, :], ag[:, :, :], AX.X, ALU.add))
            do(v.tensor_scalar(g1[:, :], g1[:, :], 1.0 / 16, None, ALU.mult))
            do(v.tensor_tensor(ag[:, :, :], ag[:, :, :], wide(g1[:, :]).to_broadcast([P, NB, 16]), ALU.subtract))
            do(v.tensor_tensor(ag2[:, :, :], ag[:, :, :], ag[:, :, :], ALU.mult))
            do(v.tensor_reduce(g1[:, :], ag2[:, :, :], AX.X, ALU.add))
            v.tensor_scalar(g1[:, :], g1[:, :], 1.0 / 16, EPS, ALU.mult, ALU.add).then_inc(S["gvar_ready"], 1)
            dve.wait_ge(S["grstd"], 1)
            do(v.tensor_tensor(ag[:, :, :], ag[:, :, :], wide(g1[:, :]).to_broadcast([P, NB, 16]), ALU.mult))
            do(v.tensor_tensor(ag[:, :, :], ag[:, :, :], gr_sb[:, 1:2, :].to_broadcast([P, NB, 16]), ALU.mult))
            do(v.tensor_tensor(ag[:, :, :], ag[:, :, :], gr_sb[:, 2:3, :].to_broadcast([P, NB, 16]), ALU.add))
            do(v.tensor_reduce(sc[:, :, :], ag[:, :, :].rearrange("p b (h k) -> p b k h", h=NX), AX.X, ALU.add))
            do(v.tensor_scalar(sc[:, :, :], sc[:, :, :], 0.25, None, ALU.mult))
            do(v.memset(wins[:, :, :], 0.0))
            for e in range(NX):
                for f in range(e + 1, NX):
                    do(v.tensor_tensor(wide(g1[:, :]), sc[:, :, e:e + 1], sc[:, :, f:f + 1], ALU.is_ge))
                    do(v.tensor_tensor(wins[:, :, e:e + 1], wins[:, :, e:e + 1], wide(g1[:, :]), ALU.add))
                    do(v.tensor_scalar(g1[:, :], g1[:, :], -1.0, 1.0, ALU.mult, ALU.add))
                    do(v.tensor_tensor(wins[:, :, f:f + 1], wins[:, :, f:f + 1], wide(g1[:, :]), ALU.add))
            do(v.tensor_reduce(g1[:, :], sc[:, :, :], AX.X, ALU.max))
            do(v.tensor_scalar(gate[:, :, :], wins[:, :, :], 2.0, None, ALU.is_equal))
            do(v.tensor_tensor(sc[:, :, :], sc[:, :, :], gate[:, :, :], ALU.mult))
            do(v.tensor_reduce(g2[:, :], sc[:, :, :], AX.X, ALU.add))
            v.tensor_tensor(g2[:, :], g2[:, :], g1[:, :], ALU.subtract).then_inc(S["gate_in"], 1)
            dve.wait_ge(S["gate_exp"], 1)
            do(v.tensor_scalar(g1[:, :], g2[:, :], 1.0, None, ALU.add))
            do(v.reciprocal(g1[:, :], g1[:, :]))
            do(v.tensor_tensor(g2[:, :], g2[:, :], g1[:, :], ALU.mult))
            do(v.tensor_tensor(gate[:, :, :], gate[:, :, :], wide(g2[:, :]).to_broadcast([P, NB, NX]), ALU.mult))
            do(v.tensor_scalar(wins[:, :, :], wins[:, :, :], 3.0, None, ALU.is_equal))
            do(v.tensor_tensor(wins[:, :, :], wins[:, :, :], wide(g1[:, :]).to_broadcast([P, NB, NX]), ALU.mult))
            do(v.tensor_tensor(gate[:, :, :], gate[:, :, :], wins[:, :, :], ALU.add))
            with dve.Fori(0, NB // GB // 2) as i:
                do = Steps(dve, "dve_mix", 0, i, DVE_MIX)
                for k, loaded in ((0, "eb_a"), (1, "eb_b")):
                    dve.wait_ge(S[loaded], i * 16 + 16)
                    blocks = bass.ds((i * 2 + k) * GB, GB)
                    for e in range(NX):
                        last = v.tensor_tensor(eb[:, k, :, e, :], eb[:, k, :, e, :], gate[:, blocks, e:e + 1].to_broadcast([P, GB, D]), ALU.mult)
                    do(last)
                    do(v.tensor_tensor(eb[:, k, :, 0:2, :], eb[:, k, :, 0:2, :], eb[:, k, :, 2:4, :], ALU.add))
                    do(v.tensor_tensor(h_sb[:, blocks, :], h_sb[:, blocks, :], eb[:, k, :, 0, :], ALU.add))
                    do(v.tensor_tensor(h_sb[:, blocks, :], h_sb[:, blocks, :], eb[:, k, :, 1, :], ALU.add))
                    dve.sem_inc(S["eb_used"], 1)
                assert do.n == DVE_MIX, do.n
            dve.sem_inc(S["out_ready"], 1)

        @block.scalar
        def _(act):
            a = nc.scalar

            def turned_x(n):
                act.wait_ge(S["xT_mm"], n + 1)
                a.activation(xT[0:D, :], bank_x[0:D, 384:384 + P], ACT.Copy).then_inc(S["xT_ready"], 1)

            def keys(n):
                act.wait_ge(S["qkv_mm"], n + 1)
                a.activation(kT[:, :], bank_x[0:D, P:2 * P], ACT.Copy).then_inc(S["kT_ready"], 1)

            def window(n, w, s, front, back, tail):
                if front:
                    turned_x(n + 1)
                if back:
                    act.wait_ge(S["pT_mm"], n)
                    for k in range(2):
                        last = a.activation(prT[:, 4 * k:4 * k + 4, :], psum[4 + k][:, :].rearrange("p (h k) -> p h k", h=4), ACT.Copy)
                    last.then_inc(S["pT_ready"], 1)
                if front:
                    keys(n + 1)
                    act.wait_ge(S["nmax_ready"], n + 1)
                    for h in range(NH):
                        last = a.activation(pr[:, h, :], ss[:, h, :], ACT.Exp, bias=nmax[:, h:h + 1])
                    last.then_inc(S["probs"], 1)
                if back:
                    act.wait_ge(S["oT_mm"], n)
                    a.activation(oT[0:D, :], bank_y[0:D, 128:256], ACT.Copy).then_inc(S["oT_ready"], 1)
                if tail and w == 0:
                    act.wait_ge(S["xT2_mm"], s)
                    a.activation(xT2[0:D, :, :].rearrange("p w k -> p (w k)"), psum[4][0:D, :], ACT.Copy).then_inc(S["xT2_ready"], 1)
                if tail and w in (1, 2):
                    act.wait_ge(S["hid_mm"], s * 2 + w - 2)
                    for k in range(2):
                        last = a.activation(hh[:, (w - 1) * 2 + k, :], psum[4 + k][:, :], ACT.Gelu)
                    last.then_inc(S["hid_ready"], 1)

            turned_x(0)
            keys(0)
            windows(act, window)

            AHEAD = 6

            def sources(c, k):
                apart(act)
                a.activation(src_now[:, k % SL, :], big_i[:, bass.ds(c * CH, CH)], ACT.Copy).then_inc(S["src_ready"], 1)

            def squares(c, k):
                for j in range(CH):
                    last = a.activation(sq[:, j, :], iota_b[:, :], ACT.Square, bias=big_f[:, one(c * CH + j)], scale=-1.0)
                last.then_inc(S["squared"], 1)

            def hots(c, k):
                act.wait_ge(S["squared"], c + 1)
                a.activation(hot[:, k % 4, :, :], sq[:, :, :], ACT.Relu, bias=ones[:, 0:1], scale=-1.0).then_inc(S["hot_ready"], 1)

            def codes(c, k):
                act.wait_ge(S["bits_ready"], c + 1)
                a.activation(nodes[:, k % SL, :, ROW:FW].bitcast(bf16), bits_i[:, k % 4, :, :], ACT.Copy).then_inc(S["codes_ready"], 1)

            def turned(c, k):
                act.wait_ge(S["hotT_mm"], c + 1)
                a.activation(hotT_b[:, k % 2, :, :].rearrange("p j e -> p (j e)"), psum[0][:, 0:256].bitcast(bf16), ACT.Copy).then_inc(S["hotT_ready"], 1)
                act.wait_ge(S["halves_mm"], c + 1)
                a.activation(halves_b[:, k % 2, :], psum[1][0:16, 0:256].bitcast(bf16), ACT.Copy).then_inc(S["halves_ready"], 1)

            def chunk(c, k, first, lap):
                lead, logits = (not first or c - back in range(NCH) for back in range(2))
                if logits:
                    act.wait_ge(S["lg_ready"], c)
                    a.activation(msg[:, (k - 1) % 4, :, :, 0:1].rearrange("p j h a -> p (j h) a"), lg[:, (k - 1) % 2, :, :].rearrange("p j (h a) -> p (j h) a", a=1), ACT.Exp).then_inc(S["weights"], 1)
                    act.wait_ge(S["fade_in"], c)
                    a.activation(fade[:, (k - 1) % 4, :], fade[:, (k - 1) % 4, :], ACT.Exp).then_inc(S["fade_ready"], 1)
                if lead:
                    act.wait_ge(S["hot_ready"], c + 3)
                    squares(c + 3, k + 3)
                    act.wait_ge(S["edge_mm"], c + 1)
                    a.activation(dst_e[:, k % 2, :, :], psum[6][:, 0:12 * CH].rearrange("p (j f) -> p j f", j=CH), ACT.Copy).then_inc(S["edge_out"], 1)
                    a.activation(hot_f[:, k % 4, :, :], hot[:, k % 4, :, :], ACT.Copy).then_inc(S["hot_f_ready"], 1)
                    turned(c + 2, k + 2)
                    hots(c + 3, k + 3)
                    codes(c + 3, k + 3)
                    if not first or c + AHEAD < NCH + 2:
                        sources(c + AHEAD, k + AHEAD)

            act.wait_ge(S["list_ready"], 1)
            for k in range(AHEAD):
                sources(k, k)
            for k in range(3):
                codes(k, k)
                if k:
                    act.wait_ge(S["hot_ready"], k)
                squares(k, k)
                hots(k, k)
            for k in range(2):
                turned(k, k)
            chunks(act, chunk)
            act.wait_ge(S["gvar_ready"], 1)
            a.activation(g1[:, :], g1[:, :], ACT.Ln).then_inc(S["glog"], 1)
            act.wait_ge(S["glog"], 1)
            a.activation(g1[:, :], g1[:, :], ACT.Exp, scale=-0.5).then_inc(S["grstd"], 1)
            act.wait_ge(S["gate_in"], 1)
            a.activation(g2[:, :], g2[:, :], ACT.Exp).then_inc(S["gate_exp"], 1)

        @block.tensor
        def _(pe):
            t = nc.tensor
            pe.wait_ge(S["tok_T"], 1)
            pe.wait_ge(S["const_loaded"], 16 * consts_in)
            pe.wait_ge(S["const_ready"], 1)
            for w in range(WIN):
                last = t.transpose(bank_x[:, w * SEQS:(w + 1) * SEQS], xf[:, w * P:(w + 1) * P], ident[0:SEQS, 0:SEQS])
            last.then_inc(S["tok_ready"], 1)
            for v2 in range(4):
                last = t.matmul(psum[2 + v2][:, :], flip, rb_sb[:, v2 // 2, 4 * (v2 % 2):4 * (v2 % 2) + 4, :], start=True, stop=True)
            last.then_inc(S["bias_mm"], 1)
            pe.wait_ge(S["sel_in"], 1)
            for h in range(NX):
                last = t.transpose(bank_y[0:16, h * P:(h + 1) * P], node_f[:, 4 + h, :], ident)
            last.then_inc(S["sel_mm"], 1)
            for k in range(2):
                t.matmul(count_ps[k][:, :], ones_b[:, :], zeros_b[:, :], start=True, stop=True, skip_group_check=True)
            pe.sem_inc(S["hist_added"], 4)
            with pe.Fori(0, HIST_IT) as i:
                for g in range(8):
                    pe.wait_ge(S["hist_oh"], i * 8 + g + 1)
                    t.matmul(count_ps[g % 2][:, :], ones_b[:, :], oh[:, g % 4, :, :], start=False, stop=True, skip_group_check=True).then_inc(S["hist_added"], 1)
            t.transpose(bank_y[0:SEQS, 0:SEQS], xf[:, 0:SEQS], ident[0:SEQS, 0:SEQS]).then_inc(S["hist_done"], 1)
            pe.wait_ge(S["base_mm"], 1)
            t.matmul(bank_x[:, 0:P], rowb[:, :], upper, start=True, stop=True).then_inc(S["base_row"], 1)
            pe.wait_ge(S["chunk_cmp"], 1)
            t.matmul(bank_x[:, :], ones_b[:, :], cmp_b[:, 0:512], start=True, stop=True)
            t.matmul(bank_y[:, 0:LC // CH - 512], ones_b[:, :], cmp_b[:, 512:], start=True, stop=True).then_inc(S["chunk_sum"], 1)
            pe.wait_ge(S["base_set"], 1)
            for k in range(2):
                t.matmul(count_ps[k][:, :], ident, hist[:, 4 * k:4 * k + 4, :], start=True, stop=True, skip_group_check=True)


            def rank(n, g):
                pe.wait_ge(S["oh_ready"], n * 4 + g + 1)
                t.matmul(count_ps[g % 2][:, :], before_b[:, :], oh[:, g, :, :], start=False, stop=True, skip_group_check=True).then_inc(S["ranked"], 1)

            def count(n, g):
                pe.wait_ge(S["ranks_read"], n * 4 + g + 1)
                t.matmul(count_ps[g % 2][:, :], notbefore_b[:, :], oh[:, g, :, :], start=False, stop=True, skip_group_check=True).then_inc(S["counted"], 1)

            def turn_x(n):
                pe.wait_ge(S["xn_ready"], n + 1)
                apart(pe)
                t.transpose(bank_x[0:D, 384:384 + P], xn[:, :], ident).then_inc(S["xT_mm"], 1)

            def qkv(n):
                pe.wait_ge(S["xT_ready"], n + 1)
                t.matmul(bank_x[0:D, 0:P], qkvw_sb[:, 0:D], xT[:, :], start=True, stop=True)
                t.matmul(bank_x[0:D, P:2 * P], qkvw_sb[:, D:2 * D], xT[:, :], start=True, stop=True)
                t.matmul(bank_x[:, 2 * P:2 * P + D], xT[:, :], qkvw_sb[:, 2 * D:3 * D], start=True, stop=True).then_inc(S["qkv_mm"], 1)

            def window(n, w, s, front, back, tail):
                if front:
                    pe.wait_ge(S["q_v_ready"], n + 1)
                    if back:
                        pe.wait_ge(S["nmax_ready"], n)
                    for h in range(NH):
                        last = t.matmul(psum[2 + h // 4][:, (h % 4) * P:(h % 4 + 1) * P], qm[:, h, :], kT[:, :], start=True, stop=True)
                    last.then_inc(S["s_mm"], 1)
                    turn_x(n + 1)
                    count(n, 0)
                    rank(n, 2)
                    count(n, 1)
                    rank(n, 3)
                if back:
                    pe.wait_ge(S["probs"], n)
                    if tail:
                        if w == 0:
                            pe.wait_ge(S["eo_ready"], s)
                        if w == 1:
                            pe.wait_ge(S["gat_read"], s)
                        if w > 1:
                            pe.wait_ge(S["hid_ready"], s * 2 + w - 3)
                    for h in range(NH):
                        last = t.transpose(psum[4 + h // 4][:, (h % 4) * P:(h % 4 + 1) * P], pr[:, h, :], ident)
                    last.then_inc(S["pT_mm"], 1)
                if front:
                    qkv(n + 1)
                if back:
                    pe.wait_ge(S["pT_ready"], n)
                    if tail or w > 1:
                        pe.wait_ge(S["resid_done"], n - 1)
                    for h in range(NH):
                        last = t.matmul(bank_y[:, h * (HD + 1):(h + 1) * (HD + 1)], prT[:, h, :], v1[:, (w - 1) % 2, h, :], start=True, stop=True)
                    last.then_inc(S["o_mm"], 1)
                if tail:
                    if w in (1, 2):
                        if not front:
                            pe.wait_ge(S["gat_read" if w == 1 else "hid_ready"], s if w == 1 else s * 2 - 1)
                        for k in range(2):
                            last = t.matmul(psum[4 + k][:, :], w1_sb[:, (w - 1) * 2 + k, :], xT2[:, :, :], start=True, stop=True)
                        last.then_inc(S["hid_mm"], 1)
                    if w == WIN - 1:
                        pe.wait_ge(S["hid_ready"], s * 2)
                        for e in range(NX):
                            for k in range(WIN):
                                c = (e % 2) * 256 + k * D
                                last = t.matmul(psum[4 + e // 2][:, c:c + D], hh[:, e, k * P:(k + 1) * P], w2_sb[:, e, :], start=True, stop=True)
                        last.then_inc(S["eo_mm"], 1)
                if front:
                    count(n, 2)
                if back:
                    pe.wait_ge(S["o_ready"], n)
                    apart(pe)
                    t.transpose(bank_y[0:D, 128:256], on[:, :], ident).then_inc(S["oT_mm"], 1)
                if front:
                    count(n, 3)
                if back:
                    pe.wait_ge(S["oT_ready"], n)
                    t.matmul(bank_y[:, 384:384 + D], oT[:, :], projw_sb[:, :], start=True, stop=True).then_inc(S["proj_mm"], 1)
                if front:
                    rank(n + 1, 0)
                    rank(n + 1, 1)
                if tail:
                    if w == 0:
                        pe.wait_ge(S["xn2_ready"], s)
                        apart(pe)
                        for k in range(WIN):
                            last = t.transpose(psum[4][0:D, k * P:(k + 1) * P], xn2[:, k, :], ident)
                        last.then_inc(S["xT2_mm"], 1)
                if tail and w == 0:
                    pe.wait_ge(S["xT2_ready"], s)
                    for k in range(WIN):
                        last = t.matmul(psum[5][:, k * 16:(k + 1) * 16], xT2[0:D, k, :], wg_sb[:, :], start=True, stop=True)
                    last.then_inc(S["gat_mm"], 1)

            turn_x(0)
            qkv(0)
            rank(0, 0)
            rank(0, 1)
            windows(pe, window)

            def turn(c, k, gathers):
                pe.wait_ge(S["hot_ready"], c + 1)
                for j in range(CH):
                    last = t.transpose(psum[0][:, j * P // 2:(j + 1) * P // 2].bitcast(bf16), hot[:, k % 4, j, :], ident_b[:, :])
                last.then_inc(S["hotT_mm"], 1)
                pe.wait_ge(S["codes_ready"], c + 1)
                pe.wait_ge(gathered[k % SL], gathers * (16 * CH))
                apart(pe)
                for j in range(CH):
                    last = t.transpose(psum[1][0:16, j * P // 2:(j + 1) * P // 2].bitcast(bf16), nodes[:, k % SL, j, 20:28].bitcast(bf16), ident_b[:, :])
                last.then_inc(S["halves_mm"], 1)

            def tops(c, k, read):
                pe.wait_ge(S["halves_ready"], c + 1)
                for h in range(NX):
                    if read and h % 2 == 0:
                        pe.wait_ge(S["top_read_b" if h else "top_read_a"], c)
                    last = t.matmul(psum[2 + h][:, :], sel_b[:, h, :], halves_b[:, k % 2, :], start=True, stop=True)
                    if h % 2:
                        last.then_inc(S["top_mm_b" if h > 1 else "top_mm_a"], 1)

            def chunk(c, k, first, lap):
                lead, _, sums = (not first or c - back in range(NCH) for back in range(3))
                if lead:
                    tops(c + 1, k + 1, True)
                    pe.wait_ge(S["hotT_ready"], c + 1)
                    pe.wait_ge(S["dst_ready"], c + 1)
                    for j in range(CH):
                        t.matmul(psum[6][:, j * 12:(j + 1) * 12], hotT_b[:, k % 2, j, :], dst_in[:, k % 2, 0:12], start=True, stop=False)
                        t.matmul(psum[6][:, j * 12 + 8:(j + 1) * 12], hotT_b[:, k % 2, j, :], dst_in[:, k % 2, 12:16], start=False, stop=False)
                        last = t.matmul(psum[6][:, j * 12 + 8:(j + 1) * 12], hotT_b[:, k % 2, j, :], dst_in[:, k % 2, 16:20], start=False, stop=True)
                    last.then_inc(S["edge_mm"], 1)
                    turn(c + 2, k + 2, lap + 1 + (k + 2) // SL)
                if sums:
                    pe.wait_ge(S["msg_ready"], c - 1)
                    if not first or c > 2:
                        pe.wait_ge(S["sums_kept"], c - 2)
                    pe.wait_ge(S["hot_f_ready"], c - 1)
                    for j in range(CH):
                        last = t.matmul(psum[7][:, 0:20], hot_f[:, (k - 2) % 4, j, :], msg[:, (k - 2) % 4, j, :, :], start=j == 0, stop=j == CH - 1)
                    last.then_inc(S["sums_mm"], 1)

            pe.wait_ge(S["state_ready"], 1)
            turn(0, 0, 1)
            tops(0, 0, False)
            turn(1, 1, 1)
            chunks(pe, chunk)


def kernel(**inputs):
    import concourse.bacc as bacc
    from concourse.bass_utils import run_bass_kernel_spmd as run

    f = {k: np.ascontiguousarray(a) for k, a in inputs.items()}
    seq, d, p = 512, 64, 128
    lc = 4 * (262144 // 512 + 128 + 8)
    pos = np.arange(seq, dtype=np.float32)[:, None]
    k = np.arange(d)
    inv = np.power(np.float32(10000.0), -((k - k % 2).astype(np.float32) / np.float32(d))).astype(np.float32)
    angle = pos * inv
    pos_enc = np.roll(np.where(k % 2 == 0, np.sin(angle), np.cos(angle)).astype(np.float32), -p // 2, axis=0)
    top = np.concatenate([np.eye(p), np.tile(np.arange(p), (p, 1)), np.triu(np.ones((p, p)), 1), np.ones((p, p)), np.eye(p)[::-1],
                          np.tile(np.arange(lc // 4), (p, 1))], axis=1)
    mask = np.zeros((d, top.shape[1]))
    mask[np.arange(d), np.arange(d) // 8] = 8 ** -0.5
    consts = np.concatenate([top, mask]).astype(np.float32)
    arrays = {
        "x": f["x"], "emb": f["L0_tok_W"],
        "qkv_w": np.concatenate([f["L0_attn_qkv_weight"].T, f["L0_attn_qkv_bias"][None]]),
        "proj_w": np.concatenate([f["L0_attn_proj_weight"].T, f["L0_attn_proj_bias"][None]]),
        "bias_rev": np.ascontiguousarray(f["L0_attn_bias_table"][::-1].T),
        "att": np.concatenate([f["L0_ffn_att_src"].reshape(1, 16), f["L0_ffn_att_dst"].reshape(1, 16)], axis=1),
        "w_gat": f["L0_ffn_W_gat"],
        "gat_rows": np.concatenate([f["L0_ffn_b_gat"], f["L0_ffn_ln_gamma"], f["L0_ffn_ln_beta"]])[None],
        "w1": np.concatenate([f["L0_ffn_W1"], f["L0_ffn_b1"][:, None]], axis=1),
        "w2": f["L0_ffn_W2"], "b2_rows": f["L0_ffn_b2"].reshape(1, 256), "edges": f["L0_ffn_edge_index"],
        "pos_enc": pos_enc, "consts": consts,
    }
    nc = bacc.Bacc("TRN2", target_bir_lowering=False, num_devices=1)
    args = [nc.dram_tensor("in_" + n, a.shape, mybir.dt.from_np(a.dtype), kind="ExternalInput").ap() for n, a in arrays.items()]
    out = nc.dram_tensor("out_0", (32, 512, 64), mybir.dt.float32, kind="ExternalOutput").ap()
    lm_tower_kernel(nc, *args, out)
    r = run(nc, [{"in_" + n: np.ascontiguousarray(a) for n, a in arrays.items()}], core_ids=[0])
    return r.results[0]["out_0"]
```
